# Optimizing a Trainium2 kernel written in Bass

```python
import numpy as np
import jax
import jax.numpy as jnp

def _softmax(x, axis=-1):
    return jax.nn.softmax(x, axis=axis)

def _gelu(x):
    return jax.nn.gelu(x, approximate=True)

def _silu(x):
    return jax.nn.silu(x)

def _sigmoid(x):
    return jax.nn.sigmoid(x)

def _layernorm(x, axis=-1, eps=1e-05):
    m = jnp.mean(x, axis=axis, keepdims=True)
    v = jnp.var(x, axis=axis, keepdims=True)
    return (x - m) / jnp.sqrt(v + eps)

def _scatter_add(tgt, idx, src, axis=0):
    return tgt.at[idx].add(src)

def _segment_sum(src, seg, n):
    return jax.ops.segment_sum(src, seg, n)
kernel_name = 'mk_early_fusion_d2_tok_img1024_r4_e23aa2'

def setup_inputs(seed: int=0):
    np.random.seed(seed)
    _w = jnp.asarray

    def _rec_inputs():
        import jax
        import jax.numpy as jnp
        _rk = jax.random.key(seed)
        x = -0.00016672 + 0.999947 * jax.random.normal(jax.random.fold_in(_rk, 1), (32, 3, 96, 96), jnp.float32)
        txt = 0.00213415 + 1.41303 * jax.random.normal(jax.random.fold_in(_rk, 2), (32, 32, 256), jnp.float32)
        return (x, txt)
    x, txt = _rec_inputs()

    def _L0_tok_setup():
        import jax, jax.numpy as jnp
        import numpy as np
        EMBED_DIM = 256
        IMAGE_SIZE = 96
        CHANNELS = 3
        PATCH = 16
        NUM_PATCHES = (IMAGE_SIZE // PATCH) ** 2
        PATCH_DIM = PATCH * PATCH * CHANNELS

        def _patchify(x, patch):
            B, C, H, W = x.shape
            hp, wp = (H // patch, W // patch)
            x = x.reshape(B, C, hp, patch, wp, patch)
            x = x.transpose(0, 2, 4, 1, 3, 5)
            return x.reshape(B, hp * wp, C * patch * patch)
        key = jax.random.key(seed)
        k_x, k_w, k_b, k_cls, k_pos = jax.random.split(key, 5)
        x = jax.random.normal(k_x, (64, CHANNELS, IMAGE_SIZE, IMAGE_SIZE), dtype=jnp.float32)
        W = jax.random.normal(k_w, (EMBED_DIM, PATCH_DIM), dtype=jnp.float32) / np.sqrt(PATCH_DIM)
        b = jax.random.normal(k_b, (EMBED_DIM,), dtype=jnp.float32) * 0.01
        cls_token = jax.random.normal(k_cls, (1, 1, EMBED_DIM), dtype=jnp.float32)
        pos_embedding = jax.random.normal(k_pos, (1, 1 + NUM_PATCHES, EMBED_DIM), dtype=jnp.float32)
        return {'x': x, 'W': W, 'b': b, 'cls_token': cls_token, 'pos_embedding': pos_embedding}
    _L0_tok_all = _L0_tok_setup()
    _L0_tok_in = {k: v for k, v in _L0_tok_all.items() if k in ('W', 'b', 'cls_token', 'pos_embedding')}
    del _L0_tok_all

    def _L0_attn_setup():
        import jax, jax.numpy as jnp
        import numpy as np
        import math
        DIM = 256
        HEADS = 16
        DIM_K = DIM // HEADS
        SEQ = 512

        def _rope_tables(seq_len, dim):
            pos = jnp.arange(seq_len, dtype=jnp.float32)[:, None]
            freqs = jnp.exp(jnp.arange(0, dim, 2, dtype=jnp.float32) * (-math.log(10000.0) / dim))
            ang = pos * freqs
            return (jnp.cos(ang), jnp.sin(ang))

        def _apply_rope(x, cos, sin):
            even = x[..., ::2]
            odd = x[..., 1::2]
            return jnp.concatenate([even * cos - odd * sin, even * sin + odd * cos], axis=-1)
        key = jax.random.key(seed)
        ks = jax.random.split(key, 6)
        B, S, D = (2, SEQ, DIM)
        scale = 1.0 / math.sqrt(D)
        return {'x': jax.random.normal(ks[0], (B, S, D), dtype=jnp.float32), 'wq': jax.random.normal(ks[1], (D, D), dtype=jnp.float32) * scale, 'wk': jax.random.normal(ks[2], (D, D), dtype=jnp.float32) * scale, 'wv': jax.random.normal(ks[3], (D, D), dtype=jnp.float32) * scale, 'wo_w': jax.random.normal(ks[4], (D, D), dtype=jnp.float32) * scale, 'wo_b': jax.random.normal(ks[5], (D,), dtype=jnp.float32) * 0.01}
    _L0_attn_all = _L0_attn_setup()
    _L0_attn_in = {k: v for k, v in _L0_attn_all.items() if k in ('wq', 'wk', 'wv', 'wo_w', 'wo_b')}
    del _L0_attn_all

    def _L0_ffn_setup():
        import jax, jax.numpy as jnp
        import numpy as np
        B, S, D, E, H, K = (4, 512, 256, 8, 128, 2)
        key = jax.random.key(seed)
        ks = jax.random.split(key, 11)
        sc = 0.02
        return {'x': jax.random.normal(ks[0], (B, S, D), dtype=jnp.float32), 'gate_W': jax.random.normal(ks[1], (D, E), dtype=jnp.float32) * sc, 'W1': jax.random.normal(ks[2], (E, D, H), dtype=jnp.float32) * sc, 'b1': jnp.zeros((E, H), dtype=jnp.float32), 'W2': jax.random.normal(ks[3], (E, H, D), dtype=jnp.float32) * sc, 'b2': jnp.zeros((E, D), dtype=jnp.float32), 'Ws1': jax.random.normal(ks[4], (D, H), dtype=jnp.float32) * sc, 'bs1': jnp.zeros((H,), dtype=jnp.float32), 'Ws2': jax.random.normal(ks[5], (H, D), dtype=jnp.float32) * sc, 'bs2': jnp.zeros((D,), dtype=jnp.float32), 'route_scale': jnp.ones((), dtype=jnp.float32)}
    _L0_ffn_all = _L0_ffn_setup()
    _L0_ffn_in = {k: v for k, v in _L0_ffn_all.items() if k in ('gate_W', 'W1', 'b1', 'W2', 'b2', 'Ws1', 'bs1', 'Ws2', 'bs2', 'route_scale')}
    del _L0_ffn_all

    def _L1_attn_setup():
        import math
        import jax, jax.numpy as jnp
        import numpy as np
        H = 256
        NH = 16
        HD = H // NH
        FF = 1024
        EPS = 1e-12

        def _lin(key, fan_in, fan_out):
            k1, k2 = jax.random.split(key)
            bound = 1.0 / math.sqrt(fan_in)
            W = jax.random.uniform(k1, (fan_in, fan_out), jnp.float32, -bound, bound)
            b = jax.random.uniform(k2, (fan_out,), jnp.float32, -bound, bound)
            return (W, b)

        def _layernorm(x, g, b):
            mu = jnp.mean(x, axis=-1, keepdims=True)
            var = jnp.mean((x - mu) ** 2, axis=-1, keepdims=True)
            return (x - mu) * jax.lax.rsqrt(var + EPS) * g + b

        def _gelu(x):
            return x * 0.5 * (1.0 + jax.lax.erf(x / jnp.sqrt(jnp.float32(2.0))))
        key = jax.random.key(seed)
        ks = jax.random.split(key, 8)
        x = jax.random.normal(ks[0], (4, 1024, H), jnp.float32)
        Wq, bq = _lin(ks[1], H, H)
        Wk, bk = _lin(ks[2], H, H)
        Wv, bv = _lin(ks[3], H, H)
        Wo, bo = _lin(ks[4], H, H)
        W1, b1 = _lin(ks[5], H, FF)
        W2, b2 = _lin(ks[6], FF, H)
        g1 = jnp.ones((H,), jnp.float32)
        be1 = jnp.zeros((H,), jnp.float32)
        g2 = jnp.ones((H,), jnp.float32)
        be2 = jnp.zeros((H,), jnp.float32)
        return dict(x=x, Wq=Wq, bq=bq, Wk=Wk, bk=bk, Wv=Wv, bv=bv, Wo=Wo, bo=bo, g1=g1, be1=be1, W1=W1, b1=b1, W2=W2, b2=b2, g2=g2, be2=be2)
    _L1_attn_all = _L1_attn_setup()
    _L1_attn_in = {k: v for k, v in _L1_attn_all.items() if k in ('Wq', 'bq', 'Wk', 'bk', 'Wv', 'bv', 'Wo', 'bo', 'g1', 'be1', 'W1', 'b1', 'W2', 'b2', 'g2', 'be2')}
    del _L1_attn_all

    def _L1_ffn_setup():
        import jax, jax.numpy as jnp
        import numpy as np
        N_EMBD = 256
        NUM_EXPERTS = 8
        TOP_K = 2

        def new_gelu(x):
            c = jnp.sqrt(2.0 / jnp.pi).astype(x.dtype)
            return 0.5 * x * (1.0 + jnp.tanh(c * (x + 0.044715 * x ** 3)))
        key = jax.random.key(seed)
        ks = jax.random.split(key, 6)
        C, E, H = (N_EMBD, NUM_EXPERTS, 4 * N_EMBD)
        x = jax.random.normal(ks[0], (4, 512, C), dtype=jnp.float32)
        router_w = 0.02 * jax.random.normal(ks[1], (E, C), dtype=jnp.float32)
        w1 = 0.02 * jax.random.normal(ks[2], (E, H, C), dtype=jnp.float32)
        b1 = jnp.zeros((E, H), dtype=jnp.float32)
        w2 = 0.02 * jax.random.normal(ks[3], (E, C, H), dtype=jnp.float32)
        b2 = jnp.zeros((E, C), dtype=jnp.float32)
        return {'x': x, 'router_w': router_w, 'w1': w1, 'b1': b1, 'w2': w2, 'b2': b2}
    _L1_ffn_all = _L1_ffn_setup()
    _L1_ffn_in = {k: v for k, v in _L1_ffn_all.items() if k in ('router_w', 'w1', 'b1', 'w2', 'b2')}
    del _L1_ffn_all
    return {'x': x, 'txt': txt, 'L0_tok_W': _L0_tok_in['W'], 'L0_tok_b': _L0_tok_in['b'], 'L0_tok_cls_token': _L0_tok_in['cls_token'], 'L0_tok_pos_embedding': _L0_tok_in['pos_embedding'], 'L0_attn_wq': _L0_attn_in['wq'], 'L0_attn_wk': _L0_attn_in['wk'], 'L0_attn_wv': _L0_attn_in['wv'], 'L0_attn_wo_w': _L0_attn_in['wo_w'], 'L0_attn_wo_b': _L0_attn_in['wo_b'], 'L0_ffn_gate_W': _L0_ffn_in['gate_W'], 'L0_ffn_W1': _L0_ffn_in['W1'], 'L0_ffn_b1': _L0_ffn_in['b1'], 'L0_ffn_W2': _L0_ffn_in['W2'], 'L0_ffn_b2': _L0_ffn_in['b2'], 'L0_ffn_Ws1': _L0_ffn_in['Ws1'], 'L0_ffn_bs1': _L0_ffn_in['bs1'], 'L0_ffn_Ws2': _L0_ffn_in['Ws2'], 'L0_ffn_bs2': _L0_ffn_in['bs2'], 'L0_ffn_route_scale': _L0_ffn_in['route_scale'], 'L1_attn_Wq': _L1_attn_in['Wq'], 'L1_attn_bq': _L1_attn_in['bq'], 'L1_attn_Wk': _L1_attn_in['Wk'], 'L1_attn_bk': _L1_attn_in['bk'], 'L1_attn_Wv': _L1_attn_in['Wv'], 'L1_attn_bv': _L1_attn_in['bv'], 'L1_attn_Wo': _L1_attn_in['Wo'], 'L1_attn_bo': _L1_attn_in['bo'], 'L1_attn_g1': _L1_attn_in['g1'], 'L1_attn_be1': _L1_attn_in['be1'], 'L1_attn_W1': _L1_attn_in['W1'], 'L1_attn_b1': _L1_attn_in['b1'], 'L1_attn_W2': _L1_attn_in['W2'], 'L1_attn_b2': _L1_attn_in['b2'], 'L1_attn_g2': _L1_attn_in['g2'], 'L1_attn_be2': _L1_attn_in['be2'], 'L1_ffn_router_w': _L1_ffn_in['router_w'], 'L1_ffn_w1': _L1_ffn_in['w1'], 'L1_ffn_b1': _L1_ffn_in['b1'], 'L1_ffn_w2': _L1_ffn_in['w2'], 'L1_ffn_b2': _L1_ffn_in['b2']}

def reference(x, txt, L0_tok_W, L0_tok_b, L0_tok_cls_token, L0_tok_pos_embedding, L0_attn_wq, L0_attn_wk, L0_attn_wv, L0_attn_wo_w, L0_attn_wo_b, L0_ffn_gate_W, L0_ffn_W1, L0_ffn_b1, L0_ffn_W2, L0_ffn_b2, L0_ffn_Ws1, L0_ffn_bs1, L0_ffn_Ws2, L0_ffn_bs2, L0_ffn_route_scale, L1_attn_Wq, L1_attn_bq, L1_attn_Wk, L1_attn_bk, L1_attn_Wv, L1_attn_bv, L1_attn_Wo, L1_attn_bo, L1_attn_g1, L1_attn_be1, L1_attn_W1, L1_attn_b1, L1_attn_W2, L1_attn_b2, L1_attn_g2, L1_attn_be2, L1_ffn_router_w, L1_ffn_w1, L1_ffn_b1, L1_ffn_w2, L1_ffn_b2):
    import jax
    import jax.numpy as jnp

    def _L0_tok_ref(x, W, b, cls_token, pos_embedding):
        import jax, jax.numpy as jnp
        import numpy as np
        EMBED_DIM = 256
        IMAGE_SIZE = 96
        CHANNELS = 3
        PATCH = 16
        NUM_PATCHES = (IMAGE_SIZE // PATCH) ** 2
        PATCH_DIM = PATCH * PATCH * CHANNELS

        def _patchify(x, patch):
            B, C, H, W = x.shape
            hp, wp = (H // patch, W // patch)
            x = x.reshape(B, C, hp, patch, wp, patch)
            x = x.transpose(0, 2, 4, 1, 3, 5)
            return x.reshape(B, hp * wp, C * patch * patch)
        B = x.shape[0]
        patches = _patchify(x, PATCH)
        tokens = jnp.einsum('bnd,ed->bne', patches, W) + b
        cls = jnp.broadcast_to(cls_token, (B, 1, EMBED_DIM))
        out = jnp.concatenate([cls, tokens], axis=1)
        return out + pos_embedding

    def _L0_attn_ref(x, wq, wk, wv, wo_w, wo_b):
        import jax, jax.numpy as jnp
        import numpy as np
        import math
        DIM = 256
        HEADS = 16
        DIM_K = DIM // HEADS
        SEQ = 512

        def _rope_tables(seq_len, dim):
            pos = jnp.arange(seq_len, dtype=jnp.float32)[:, None]
            freqs = jnp.exp(jnp.arange(0, dim, 2, dtype=jnp.float32) * (-math.log(10000.0) / dim))
            ang = pos * freqs
            return (jnp.cos(ang), jnp.sin(ang))

        def _apply_rope(x, cos, sin):
            even = x[..., ::2]
            odd = x[..., 1::2]
            return jnp.concatenate([even * cos - odd * sin, even * sin + odd * cos], axis=-1)
        B, S, D = x.shape
        cos, sin = _rope_tables(S, D)
        Q = _apply_rope(jnp.einsum('bsd,ed->bse', x, wq), cos, sin)
        K = _apply_rope(jnp.einsum('bsd,ed->bse', x, wk), cos, sin)
        V = jnp.einsum('bsd,ed->bse', x, wv)
        Q = Q.reshape(B, S, HEADS, DIM_K).transpose(0, 2, 1, 3)
        K = K.reshape(B, S, HEADS, DIM_K).transpose(0, 2, 1, 3)
        V = V.reshape(B, S, HEADS, DIM_K).transpose(0, 2, 1, 3)
        scores = jnp.einsum('bhqd,bhkd->bhqk', Q, K) / math.sqrt(DIM_K)
        weights = jax.nn.softmax(scores, axis=-1)
        out = jnp.einsum('bhqk,bhkd->bhqd', weights, V)
        out = out.transpose(0, 2, 1, 3).reshape(B, S, D)
        return jnp.einsum('bsd,ed->bse', out, wo_w) + wo_b

    def _L0_ffn_ref(x, gate_W, W1, b1, W2, b2, Ws1, bs1, Ws2, bs2, route_scale):
        import jax, jax.numpy as jnp
        import numpy as np
        B, S, D, E, H, K = (4, 512, 256, 8, 128, 2)
        scores = jax.nn.sigmoid(x @ gate_W) * route_scale
        topk_scores, topk_idx = jax.lax.top_k(scores, K)
        topk_w = topk_scores / topk_scores.sum(-1, keepdims=True)
        onehot = jax.nn.one_hot(topk_idx, E, dtype=x.dtype)
        gate_full = jnp.einsum('bsk,bske->bse', topk_w, onehot)
        h = jax.nn.gelu(jnp.einsum('bsd,edh->bseh', x, W1) + b1, approximate=False)
        y = jnp.einsum('bseh,ehd->bsed', h, W2) + b2
        expert_out = jnp.einsum('bse,bsed->bsd', gate_full, y)
        shared = jax.nn.gelu(x @ Ws1 + bs1, approximate=False) @ Ws2 + bs2
        return expert_out + shared

    def _L1_attn_ref(x, Wq, bq, Wk, bk, Wv, bv, Wo, bo, g1, be1, W1, b1, W2, b2, g2, be2):
        import math
        import jax, jax.numpy as jnp
        import numpy as np
        H = 256
        NH = 16
        HD = H // NH
        FF = 1024
        EPS = 1e-12

        def _lin(key, fan_in, fan_out):
            k1, k2 = jax.random.split(key)
            bound = 1.0 / math.sqrt(fan_in)
            W = jax.random.uniform(k1, (fan_in, fan_out), jnp.float32, -bound, bound)
            b = jax.random.uniform(k2, (fan_out,), jnp.float32, -bound, bound)
            return (W, b)

        def _layernorm(x, g, b):
            mu = jnp.mean(x, axis=-1, keepdims=True)
            var = jnp.mean((x - mu) ** 2, axis=-1, keepdims=True)
            return (x - mu) * jax.lax.rsqrt(var + EPS) * g + b

        def _gelu(x):
            return x * 0.5 * (1.0 + jax.lax.erf(x / jnp.sqrt(jnp.float32(2.0))))
        B, S, _ = x.shape

        def heads(W, b):
            return (x @ W + b).reshape(B, S, NH, HD).transpose(0, 2, 1, 3)
        q, k, v = (heads(Wq, bq), heads(Wk, bk), heads(Wv, bv))
        eq = jax.nn.elu(q)
        ek = jax.nn.elu(k)
        qn = eq / jnp.linalg.norm(eq, axis=-1, keepdims=True)
        kn = ek / jnp.linalg.norm(ek, axis=-1, keepdims=True)
        kv = jnp.einsum('bhsd,bhse->bhde', kn, v)
        ctx = jnp.einsum('bhsd,bhde->bhse', qn, kv) / jnp.float32(math.sqrt(HD))
        ctx = ctx.transpose(0, 2, 1, 3).reshape(B, S, H)
        attn_out = _layernorm(ctx @ Wo + bo + x, g1, be1)
        h = _gelu(attn_out @ W1 + b1)
        out = _layernorm(h @ W2 + b2 + attn_out, g2, be2)
        return out

    def _L1_ffn_ref(x, router_w, w1, b1, w2, b2):
        import jax, jax.numpy as jnp
        import numpy as np
        N_EMBD = 256
        NUM_EXPERTS = 8
        TOP_K = 2

        def new_gelu(x):
            c = jnp.sqrt(2.0 / jnp.pi).astype(x.dtype)
            return 0.5 * x * (1.0 + jnp.tanh(c * (x + 0.044715 * x ** 3)))
        B, T, C = x.shape
        E = router_w.shape[0]
        x_flat = x.reshape(B * T, C)
        router_logits = x_flat @ router_w.T
        router_probs = jax.nn.softmax(router_logits, axis=-1)
        top_k_probs, top_k_idx = jax.lax.top_k(router_probs, TOP_K)
        top_k_probs = top_k_probs / (top_k_probs.sum(axis=-1, keepdims=True) + 1e-08)
        cw = (jax.nn.one_hot(top_k_idx, E, dtype=x.dtype) * top_k_probs[..., None]).sum(axis=1)
        output = jnp.zeros_like(x_flat)
        for e in range(E):
            h = new_gelu(x_flat @ w1[e].T + b1[e])
            out_e = h @ w2[e].T + b2[e]
            output = output + cw[:, e:e + 1] * out_e
        return output.reshape(B, T, C)
    h = _L0_tok_ref(x, L0_tok_W, L0_tok_b, L0_tok_cls_token, L0_tok_pos_embedding)
    h = jnp.concatenate([h, txt], axis=1)
    h = h + _L0_attn_ref(_layernorm(h, axis=-1), L0_attn_wq, L0_attn_wk, L0_attn_wv, L0_attn_wo_w, L0_attn_wo_b)
    h = h + _L0_ffn_ref(_layernorm(h, axis=-1), L0_ffn_gate_W, L0_ffn_W1, L0_ffn_b1, L0_ffn_W2, L0_ffn_b2, L0_ffn_Ws1, L0_ffn_bs1, L0_ffn_Ws2, L0_ffn_bs2, L0_ffn_route_scale)
    h = h + _L1_attn_ref(_layernorm(h, axis=-1), L1_attn_Wq, L1_attn_bq, L1_attn_Wk, L1_attn_bk, L1_attn_Wv, L1_attn_bv, L1_attn_Wo, L1_attn_bo, L1_attn_g1, L1_attn_be1, L1_attn_W1, L1_attn_b1, L1_attn_W2, L1_attn_b2, L1_attn_g2, L1_attn_be2)
    h = h + _L1_ffn_ref(_layernorm(h, axis=-1), L1_ffn_router_w, L1_ffn_w1, L1_ffn_b1, L1_ffn_w2, L1_ffn_b2)
    return h

_drawn_inputs = setup_inputs


def setup_inputs(seed=0):
    import zlib

    import numpy as np

    out = dict(_drawn_inputs(seed))
    spreads = {'L0_ffn_b1': (0.0, 0.8),
     'L0_ffn_b2': (0.0, 0.1),
     'L0_ffn_bs1': (0.0, 0.8),
     'L0_ffn_bs2': (0.0, 0.1),
     'L1_attn_g1': (1.0, 0.2),
     'L1_attn_be1': (0.0, 0.1),
     'L1_attn_g2': (1.0, 0.2),
     'L1_attn_be2': (0.0, 0.1),
     'L1_ffn_b1': (0.0, 0.741),
     'L1_ffn_b2': (0.0, 0.272)}
    factors = {'L0_tok_b': 7.731,
     'L0_attn_wo_b': 6.102,
     'L0_ffn_W1': 2.86,
     'L1_attn_bq': 8.0,
     'L1_attn_bk': 7.252,
     'L1_attn_bv': 6.478,
     'L1_attn_bo': 3.674,
     'L1_attn_b1': 8.0,
     'L1_attn_b2': 6.981}
    for name, (base, spread) in spreads.items():
        noise = np.random.default_rng([zlib.crc32(name.encode()), seed]).standard_normal(out[name].shape)
        drawn = base * np.exp(spread * noise) if base else spread * noise
        out[name] = jnp.asarray(drawn.astype(out[name].dtype))
    for name, factor in factors.items():
        out[name] = (out[name] * factor).astype(out[name].dtype)
    return out
```

```python
from contextlib import ExitStack

import numpy as np

import concourse.bass as bass
from concourse import mybir

ALU = mybir.AluOpType
ACT = mybir.ActivationFunctionType
AX_X = mybir.AxisListType.X
F32 = mybir.dt.float32
I32 = mybir.dt.int32
U32 = mybir.dt.uint32

P = 128
D = 256
C = D // P
NB = 32
PATCHES = 36
TXT = 32
S = 1 + PATCHES + TXT
N = NB * S
NT = -(-N // P)
LAST = N - (NT - 1) * P
G = 3
GW = G * P
NG = NT // G
NPT = NB * PATCHES // P
KP = 768 // P
HEADS = 16
HD = D // HEADS
E = 8
FF = 1024
KF = FF // P
PAIR = 2 * S
XW = PAIR * (NB // 2 + 2)
OPAD = PAIR
OW = OPAD + NT * P
NBLK = (2 * N + E * (P - 1)) // P
XBLK = NBLK + 2
BIG = 1.0e30


class Memory:

    def __init__(self, nc, ctx, cols):
        self.t = ctx.enter_context(nc.sbuf_tensor("memory", [P, cols], F32))
        self.cols, self.pos = cols, 0

    def at(self, pos):
        self.pos = pos

    def take(self, *dims):
        n = int(np.prod(dims))
        a, self.pos = self.pos, self.pos + n
        assert self.pos <= self.cols, (self.pos, self.cols)
        v = self.t[:, a:a + n]
        if len(dims) == 1:
            return v
        names = "abcd"[:len(dims)]
        kw = {names[j]: dims[j] for j in range(1, len(dims))}
        return v.rearrange(f"p ({' '.join(names)}) -> p {' '.join(names)}", **kw)


class Steps:

    def __init__(self, eng, sem, base):
        self.eng, self.sem, self.base, self.n = eng, sem, base, 0

    def __call__(self, ins):
        ins.then_inc(self.sem, 1)
        self.n += 1
        self.eng.wait_ge(self.sem, self.base + self.n)


def inner(ap, k):
    return ap.unsqueeze(len(ap.shape)).to_broadcast(list(ap.shape) + [k])


def spread(ap, k):
    s = list(ap.shape)
    return ap.unsqueeze(1).to_broadcast([s[0], k] + s[1:])


MOMENT_STEPS = 6
RSQRT_STEPS = 12


def moments(dve, link, stats, mean, var, tmp):
    link(dve.tensor_tensor(mean, stats[:, :, 1], stats[:, :, 4], ALU.add))
    link(dve.tensor_tensor(tmp, stats[:, :, 1], stats[:, :, 4], ALU.subtract))
    link(dve.tensor_tensor(var, stats[:, :, 2], stats[:, :, 5], ALU.add))
    link(dve.tensor_scalar(mean, mean, 0.5, None, ALU.mult))
    link(dve.scalar_tensor_tensor(out=tmp, in0=tmp, scalar=0.25, in1=tmp, op0=ALU.mult, op1=ALU.mult))
    link(dve.scalar_tensor_tensor(out=var, in0=var, scalar=1.0 / D, in1=tmp, op0=ALU.mult, op1=ALU.add))


def rsqrt(dve, link, v, eps, y, t, done=None):
    link(dve.tensor_scalar(v, v, eps, None, ALU.add))
    link(dve.tensor_scalar(t.bitcast(I32), v.bitcast(I32), 1, None, ALU.arith_shift_right))
    link(dve.tensor_scalar(y.bitcast(I32), t.bitcast(I32), -1.0, float(0x5F3759DF), ALU.mult, ALU.add))
    for k in range(3):
        link(dve.tensor_tensor(t, v, y, ALU.mult))
        link(dve.scalar_tensor_tensor(out=t, in0=t, scalar=-0.5, in1=y, op0=ALU.mult, op1=ALU.mult))
        ins = dve.scalar_tensor_tensor(out=y, in0=t, scalar=1.5, in1=y, op0=ALU.add, op1=ALU.mult)
        if k == 2 and done is not None:
            ins.then_inc(done, 1)
        else:
            link(ins)


def three(tile, i, u):
    return tile[:, bass.ds(i * (2 * G) + G * u, G), :]


def one(tile, i, u, j):
    return tile[:, bass.ds(i * (2 * G) + (G * u + j), 1), :].rearrange("p a d -> p (a d)")


def cols(tile, i, u):
    return tile[:, :, bass.ds(i * (2 * GW) + GW * u, GW)]


class Kernel:
    def __init__(self, nc, t, out, ctx):
        self.nc, self.t, self.out, self.ctx = nc, t, out, ctx
        self.sems = {}
        self.norm_base = {}
        m = self.mem = Memory(nc, ctx, 53100)
        self.h = m.take(NT, D)
        self.ident = m.take(P)
        self.head_mask = m.take(P)
        self.rank = m.take(E)
        self.top_rank = m.take(NT)
        self.lg = m.take(NT, E)
        self.xn = m.take(NT, D)
        self.keep_at = m.pos
        m.take(4 * NT + XBLK)
        self.zero = m.take(D)
        self.w1_at = m.pos
        self.w2_at = m.pos + C * E * FF
        self.work_at = self.w2_at + E * KF * D
        self.route_at = self.work_at
        self.w1 = m.take(C, E * FF)
        self.w2 = m.take(E * KF, D)
        m.at(self.w2_at)
        self.xT = m.take(C, XW)
        self.oT = m.take(C, OW)
        self.late_at = m.pos
        self.weights()

    def sem(self, name, n=None):
        if n is not None:
            return [self.sem(f"{name}{j}") for j in range(n)]
        if name not in self.sems:
            self.sems[name] = self.ctx.enter_context(self.nc.semaphore(name))
        return self.sems[name]

    def dram(self, name, shape, dt=F32):
        return self.nc.dram_tensor(name, shape, dt, kind="Internal").ap()

    def weights(self):
        m = self.mem
        m.at(self.w1_at)
        self.early = {}
        def w(name, *dims):
            v = m.take(*dims)
            self.early[name] = v
            return v
        self.wpatch = w("wpatch", KP, D)
        self.pos = w("pos", NPT, D)
        self.wqk0 = w("wqk0", 2, C, D)
        self.wv0 = w("wv0", C, D)
        self.wo0 = w("wo0", C, D)
        self.wo0_b = w("wo0_b", D)
        self.tok_b = w("tok_b", D)
        self.cos_sin = w("cos_sin", 2, S)
        self.sin_cos = w("sin_cos", 2, S)
        self.par_mask = w("par_mask", 2)
        self.e1 = w("e1", E + 1, C, P)
        self.e1_b = w("e1_b", E + 1)
        self.e2 = w("e2", E + 1, D)
        self.gate_w = w("gate_w", C, E)
        self.route_scale = w("route_scale", 1)
        assert m.pos <= self.w2_at
        self.early_end = m.pos
        m.at(self.late_at)
        self.wqk1 = w("wqk1", C, 2 * D)
        self.wv1 = w("wv1", C, D)
        self.bv1 = w("bv1", D)
        self.wo1 = w("wo1", C, D)
        self.f1 = w("f1", C, FF)
        self.f2 = w("f2", KF, D)
        assert m.pos <= self.work_at, (m.pos, self.work_at)
        m.at(self.work_at)
        self.bqk1 = w("bqk1", 2 * D)
        self.f1_b = w("f1_b", KF)
        self.bo1 = w("bo1", D)
        self.f2_b = w("f2_b", D)
        self.g1 = w("g1", D)
        self.be1 = w("be1", D)
        self.g2 = w("g2", D)
        self.be2 = w("be2", D)
        self.router = w("router", C, E)
        self.work_at = m.pos

    def embed(self):
        nc, m, t, sem = self.nc, self.mem, self.t, self.sem
        R = 3
        m.at(self.early_end)
        patches = [m.take(KP, P) for _ in range(R)]
        m.at(self.work_at)
        rows = [m.take(D) for _ in range(R)]
        cls = m.take(2, D)
        zero = self.zero
        tokens = self.dram("patch_tokens", [NPT * P, D])
        self.slots_in = self.dram("slots_in", [XBLK * P, D])
        self.filled = sem("slots_filled")
        stream = self.stream = self.dram("stream", [N, D])
        by_batch = stream.rearrange("(b s) d -> b s d", s=S)
        in_emb, in_rest, in_cls = sem("weights_in_embed"), sem("weights_in"), sem("cls_in")
        patch_in, mm, summed, stored = sem("patch_in", R), sem("patch_mm", R), sem("patch_summed", R), sem("patch_stored", R)
        biased, cls_sum, moved = sem("pos_biased"), sem("cls_summed"), sem("stream_written")
        cleared, self.h_in = sem("pads_cleared"), sem("h_in")

        with ExitStack() as ctx:
            acc = [ctx.enter_context(nc.psum_tensor(f"embed_acc{r}", [P, 512], F32)) for r in range(R)]
            block = ctx.enter_context(nc.Block())

            @block.sync
            def _(sp):
                first = ("wpatch", "pos", "tok_b")
                for name in first:
                    sp.dma_start(self.early[name], t[name]).then_inc(in_emb, 16)
                sp.dma_start(cls[0:NB], t["cls"]).then_inc(in_cls, 16)
                with sp.Fori(0, NPT // R) as i:
                    for r in range(R):
                        sp.wait_ge(mm[r], i)
                        sp.dma_start(patches[r], t["patches"][bass.ds(i * R + r, 1)].rearrange(
                            "a p k t -> (a p) k t")).then_inc(patch_in[r], 16)
                for name, view in self.early.items():
                    if name not in first:
                        sp.dma_start(view, t[name]).then_inc(in_rest, 16)
                for name, view in (("ident", self.ident), ("head_mask", self.head_mask), ("rank", self.rank)):
                    sp.dma_start(view, t[name]).then_inc(in_rest, 16)
                sp.dma_start(by_batch[:, 1 + PATCHES:, :], t["txt"]).then_inc(moved, 16)
                sp.wait_ge(cls_sum, 1)
                sp.dma_start(by_batch[:, 0, :], cls[0:NB, 0, :]).then_inc(moved, 16)
                for r in range(R):
                    sp.wait_ge(stored[r], 16 * (NPT // R))
                sp.dma_start(by_batch[:, 1:1 + PATCHES, :], tokens.rearrange("(b s) d -> b s d", s=PATCHES)).then_inc(moved, 16)
                sp.wait_ge(moved, 48)
                sp.wait_ge(cleared, 5)
                sp.dma_start(self.h[:, 0:NT - 1, :], stream[0:(NT - 1) * P, :].rearrange("(a p) d -> p a d", p=P)).then_inc(self.h_in, 16)
                sp.dma_start(self.h[0:LAST, NT - 1, :], stream[(NT - 1) * P:, :]).then_inc(self.h_in, 16)
                for a in range(XBLK // 4):
                    sp.dma_start(self.slots_in[a * 4 * P:(a + 1) * 4 * P, :].rearrange("(p b) d -> p b d", b=4),
                                 spread(zero, 4)).then_inc(self.filled, 16)
                sp.wait_ge(self.h_in, 32)
                sp.wait_ge(in_rest, 16 * (len(self.early) - len(first) + 3))

            @block.gpsimd
            def _(pool):
                pool.memset(zero, 0.0).then_inc(cleared, 1)
                pool.memset(self.h[:, NT - 1, :], 0.0).then_inc(cleared, 1)
                pool.memset(self.xT[:, :, NT * P:], 0.0).then_inc(cleared, 1)
                pool.memset(self.oT[:, :, 0:OPAD], 0.0).then_inc(cleared, 1)
                pool.memset(self.oT[:, :, OPAD + N:], 0.0).then_inc(cleared, 1)

            @block.tensor
            def _(pe):
                pe.wait_ge(in_emb, 48)
                with pe.Fori(0, NPT // R) as i:
                    for r in range(R):
                        pe.wait_ge(patch_in[r], 16 * i + 16)
                        pe.wait_ge(summed[r], i)
                        for k in range(KP):
                            last = pe.matmul(acc[r][:, 0:D], patches[r][:, k, :], self.wpatch[:, k, :],
                                             start=(k == 0), stop=(k == KP - 1))
                        last.then_inc(mm[r], 1)

            @block.vector
            def _(dve):
                dve.wait_ge(in_cls, 16)
                dve.tensor_tensor(cls[0:NB, 0, :], cls[0:NB, 0, :], cls[0:NB, 1, :], ALU.add).then_inc(cls_sum, 1)
                dve.wait_ge(in_emb, 48)
                dve.tensor_tensor(self.pos, self.pos, spread(self.tok_b, NPT), ALU.add).then_inc(biased, 1)
                dve.wait_ge(biased, 1)
                with dve.Fori(0, NPT // R) as i:
                    for r in range(R):
                        dve.wait_ge(mm[r], i + 1)
                        dve.wait_ge(stored[r], 16 * i)
                        dve.tensor_tensor(rows[r], acc[r][:, 0:D],
                                          self.pos[:, bass.ds(i * R + r, 1), :].rearrange("p a d -> p (a d)"),
                                          ALU.add).then_inc(summed[r], 1)

            @block.scalar
            def _(act):
                with act.Fori(0, NPT // R) as i:
                    for r in range(R):
                        act.wait_ge(summed[r], i + 1)
                        act.dma_start(tokens[bass.ds((i * R + r) * P, P), :], rows[r]).then_inc(stored[r], 16)

    def norm(self, rep, src, eps, gain=None, keep=None, turn=True, add_to=None, gate=None, logits=None, load=None):
        nc, m, sem = self.nc, self.mem, self.sem
        name = f"norm{rep}"
        m.at(self.work_at)
        z = [m.take(G, D) for _ in range(2)]
        zt = [m.take(C, GW) for _ in range(2)] if gate is not None else None
        stats = [m.take(G, 6) for _ in range(2)]
        mean = [m.take(G) for _ in range(2)]
        var, r, tmp = m.take(G), m.take(G), m.take(G)
        ready, turned, copied, kept = sem("norm_ready", 2), sem("norm_turned", 2), sem("norm_copied", 2), sem("norm_kept", 2)
        scaled, lg_mm, lg_read, step = sem("norm_scaled", 2), sem("norm_logits_mm", 2), sem("norm_logits_read", 2), sem("norm_step")
        base = self.norm_base
        per = 2 * (G + MOMENT_STEPS + RSQRT_STEPS)
        b = dict(base)
        def B(key):
            return b.get(key, 0)
        I = NG // 2
        with ExitStack() as ctx:
            if turn or gate is not None:
                flip = [ctx.enter_context(nc.psum_tensor(f"{name}_flip{u}", [P, C, 512], F32)) for u in range(2)]
            if gate is not None:
                lg = [ctx.enter_context(nc.psum_tensor(f"{name}_lg{u}", [P, 512], F32)) for u in range(2)]
            block = ctx.enter_context(nc.Block())

            if load is not None:
                @block.sync
                def _(sp):
                    load(sp)

            @block.vector
            def _(dve):
                with dve.Fori(0, I) as i:
                    link = Steps(dve, step, B("step") + i * per)
                    for u in range(2):
                        if turn or gate is not None:
                            dve.wait_ge(turned[u], B("turned") + i)
                        if keep is not None or add_to is not None:
                            dve.wait_ge(kept[u], B("kept") + i)
                        for j in range(G):
                            link(dve.bn_stats(stats[u][:, j, :], one(src, i, u, j)))
                        moments(dve, link, stats[u], mean[u], var, tmp)
                        rsqrt(dve, link, var, eps, r, tmp)
                        for j in range(G):
                            last = dve.tensor_scalar(z[u][:, j, :], one(src, i, u, j), mean[u][:, j:j + 1], r[:, j:j + 1],
                                                     ALU.subtract, ALU.mult)
                            last.then_inc(ready[u], 1)
                        dve.wait_ge(ready[u], B("ready") + (i + 1) * G)
                    assert link.n == per, (link.n, per)

            if gain is not None or add_to is not None or (gate is not None and turn):
                @block.gpsimd
                def _(pool):
                    with pool.Fori(0, I) as i:
                        for u in range(2):
                            pool.wait_ge(ready[u], B("ready") + (i + 1) * G)
                            if gain is not None:
                                pool.tensor_tensor(z[u], z[u], spread(gain[0], G), ALU.mult).then_inc(scaled[u], 1)
                                pool.wait_ge(scaled[u], B("scaled") + i * 2 + 1)
                                pool.tensor_tensor(z[u], z[u], spread(gain[1], G), ALU.add).then_inc(scaled[u], 1)
                                pool.wait_ge(scaled[u], B("scaled") + i * 2 + 2)
                            if add_to is not None:
                                pool.tensor_tensor(three(add_to, i, u), three(add_to, i, u), z[u], ALU.add).then_inc(kept[u], 1)
                            if gate is not None and turn:
                                pool.wait_ge(copied[u], B("copied") + i + 1)
                                pool.tensor_copy(cols(self.xT, i, u), zt[u]).then_inc(sem("norm_xT", 2)[u], 1)

            def z_done(eng, i, u):
                if gain is not None:
                    eng.wait_ge(scaled[u], B("scaled") + i * 2 + 2)
                else:
                    eng.wait_ge(ready[u], B("ready") + (i + 1) * G)

            if turn or gate is not None:
                @block.tensor
                def _(pe):
                    with pe.Fori(0, I) as i:
                        for u in range(2):
                            z_done(pe, i, u)
                            pe.wait_ge(copied[u], B("copied") + i)
                            for c in range(C):
                                for j in range(G):
                                    last = pe.transpose(flip[u][:, c, j * P:(j + 1) * P], z[u][:, j, c * P:(c + 1) * P], self.ident)
                            last.then_inc(turned[u], 1)
                            if gate is not None:
                                pe.wait_ge(copied[u], B("copied") + i + 1)
                                pe.wait_ge(lg_read[u], B("lg_read") + i)
                                for j in range(G):
                                    for c in range(C):
                                        last = pe.matmul(lg[u][:, j * E:(j + 1) * E], zt[u][:, c, j * P:(j + 1) * P], gate[:, c, :],
                                                         start=(c == 0), stop=(c == C - 1))
                                last.then_inc(lg_mm[u], 1)

            @block.scalar
            def _(act):
                with act.Fori(0, I) as i:
                    for u in range(2):
                        if keep is not None:
                            z_done(act, i, u)
                            act.activation(three(keep, i, u), z[u], ACT.Copy).then_inc(kept[u], 1)
                        if turn or gate is not None:
                            act.wait_ge(turned[u], B("turned") + i + 1)
                            if gate is not None:
                                act.wait_ge(lg_mm[u], B("lg_mm") + i)
                                if turn:
                                    act.wait_ge(sem("norm_xT", 2)[u], B("xT") + i)
                                act.activation(zt[u], flip[u][:, :, 0:GW], ACT.Copy).then_inc(copied[u], 1)
                            else:
                                act.activation(cols(self.xT, i, u), flip[u][:, :, 0:GW], ACT.Copy).then_inc(copied[u], 1)
                        if gate is not None:
                            act.wait_ge(lg_mm[u], B("lg_mm") + i + 1)
                            act.activation(three(logits, i, u), lg[u][:, 0:G * E].rearrange("p (j e) -> p j e", e=E),
                                           ACT.Copy).then_inc(lg_read[u], 1)
        def add(key, n):
            base[key] = base.get(key, 0) + n
        add("step", I * per); add("ready", I * G)
        if turn or gate is not None:
            add("turned", I); add("copied", I)
        if keep is not None or add_to is not None:
            add("kept", I)
        if gain is not None:
            add("scaled", 2 * I)
        if gate is not None:
            add("lg_mm", I); add("lg_read", I)
            if turn:
                add("xT", I)

    def rotate(self):
        nc, m, sem = self.nc, self.mem, self.sem
        R = 4
        W = R * S
        I = NB // R // 2
        self.qF = self.xn.rearrange("p a d -> p (a d)")[:, 0:C * N].rearrange("p (c n) -> p c n", c=C)
        m.at(self.early_end)
        self.kF = m.take(C, N)
        m.at(self.work_at)
        prod = [[m.take(2, R, S) for _ in range(2)] for _ in range(2)]
        mm, read, summed = sem("rot_mm", 2), sem("rot_read", 2), sem("rot_summed", 2)
        with ExitStack() as ctx:
            ps = [ctx.enter_context(nc.psum_tensor(f"rot{qk}", [P, 2, 512], F32)) for qk in range(2)]
            block = ctx.enter_context(nc.Block())

            @block.tensor
            def _(pe):
                with pe.Fori(0, 2 * I) as i:
                    for qk in range(2):
                        pe.wait_ge(read[qk], i)
                        for eo in range(2):
                            for c in range(C):
                                last = pe.matmul(ps[qk][:, eo, 0:W], self.wqk0[:, qk, c, eo * P:(eo + 1) * P],
                                                 self.xT[:, c, bass.ds(i * W, W)], start=(c == 0), stop=(c == C - 1))
                        last.then_inc(mm[qk], 1)

            @block.vector
            def _(dve):
                with dve.Fori(0, 2 * I) as i:
                    for qk in range(2):
                        dve.wait_ge(mm[qk], i + 1)
                        dve.wait_ge(summed[qk], i * 2)
                        for eo in range(2):
                            for k, tab in enumerate((self.cos_sin, self.sin_cos)):
                                last = dve.tensor_tensor(prod[qk][k][:, eo], ps[qk][:, eo, 0:W].rearrange("p (r s) -> p r s", s=S),
                                                         spread(tab[:, eo], R), ALU.mult)
                        last.then_inc(read[qk], 1)

            @block.gpsimd
            def _(pool):
                with pool.Fori(0, 2 * I) as i:
                    for qk, dst in enumerate((self.qF, self.kF)):
                        pool.wait_ge(read[qk], i + 1)
                        for k, op in ((0, ALU.subtract), (1, ALU.add)):
                            pool.tensor_tensor(dst[:, k, bass.ds(i * W, W)], prod[qk][k][:, 0].rearrange("p r s -> p (r s)"),
                                               prod[qk][k][:, 1].rearrange("p r s -> p (r s)"), op).then_inc(summed[qk], 1)

    def attention(self):
        nc, m, sem = self.nc, self.mem, self.sem
        H2 = 2 * C
        VW = HD + 1
        m.at(self.work_at)
        q = [m.take(C, S) for _ in range(2)]
        k2 = [m.take(C, 2, S) for _ in range(2)]
        x = [m.take(C, S) for _ in range(2)]
        va = [m.take(HEADS, VW) for _ in range(2)]
        on = m.take(HEADS, HD)
        top = m.take(4, H2)
        rsum = m.take(HEADS)
        prob = [m.take(4, H2, S) for _ in range(2)]
        pt = m.take(4, H2, S)
        staged, keyed = sem("x_staged"), sem("qk_staged")
        v_mm, v_read, s_mm, s_read = sem("v_mm"), sem("v_read"), sem("scores_mm"), sem("scores_read")
        exp_done, pt_mm = sem("exp_done"), sem("probs_turned", 2)
        pt_read, pv_mm, o_norm = sem("probs_copied", 2), sem("pv_mm"), sem("o_normed")
        ot_mm, ot_read, preset, step = sem("o_turned"), sem("o_copied"), sem("attn_preset"), sem("attn_step")

        with ExitStack() as ctx:
            sc = ctx.enter_context(nc.psum_tensor("scores", [P, 4, 512], F32))
            tp = [ctx.enter_context(nc.psum_tensor(f"turned_probs{j}", [P, 512], F32)) for j in range(2)]
            pj = ctx.enter_context(nc.psum_tensor("values", [P, 512], F32))
            ov = ctx.enter_context(nc.psum_tensor("out_values", [P, 512], F32))
            block = ctx.enter_context(nc.Block())
            ov_heads = ov[0:S, 0:HEADS * VW].rearrange("p (h w) -> p h w", w=VW)
            ov_turned = ov[:, HEADS * VW:HEADS * VW + C * S].rearrange("p (c s) -> p c s", s=S)
            sc_heads = sc[0:S, :, 0:H2 * S].rearrange("p g (j s) -> p g j s", s=S)

            @block.gpsimd
            def _(pool):
                def stage_x(n, u):
                    pool.tensor_copy(x[u], self.xT[:, :, bass.ds(n * S, S)]).then_inc(staged, 1)

                def stage_qk(n, u):
                    pool.tensor_copy(q[u], self.qF[:, :, bass.ds(n * S, S)]).then_inc(keyed, 1)
                    for par in range(2):
                        pool.tensor_tensor(k2[u][:, :, par, :], self.kF[:, :, bass.ds(n * S, S)],
                                           self.par_mask[:, par:par + 1].unsqueeze(2).to_broadcast([P, C, S]), ALU.mult).then_inc(keyed, 1)

                stage_qk(0, 0)
                stage_x(0, 0)
                stage_qk(1, 1)
                stage_x(1, 1)
                with pool.Fori(0, NB // 2 - 1) as i:
                    for u in range(2):
                        n = i * 2 + u
                        pool.wait_ge(s_mm, n + 1)
                        stage_qk(n + 2, u)
                        pool.wait_ge(v_mm, n + 1)
                        stage_x(n + 2, u)

            @block.tensor
            def _(pe):
                def values(n, u):
                    pe.wait_ge(staged, n + 1)
                    pe.wait_ge(v_read, n)
                    for c in range(C):
                        last = pe.matmul(pj[0:S, 0:D], x[u][:, c, :], self.wv0[:, c, :], start=(c == 0), stop=(c == C - 1))
                    last.then_inc(v_mm, 1)

                def scores(n, u):
                    pe.wait_ge(keyed, n * 3 + 3)
                    pe.wait_ge(s_read, n)
                    for c in range(C):
                        for g in range(4):
                            last = pe.matmul(sc[0:S, g, c * PAIR:(c + 1) * PAIR], q[u][32 * g:32 * g + 32, c, :],
                                             k2[u][32 * g:32 * g + 32, c, :, :].rearrange("p a s -> p (a s)"),
                                             start=True, stop=True)
                    last.then_inc(s_mm, 1)

                def turn_out(n):
                    pe.wait_ge(o_norm, n + 1)
                    for c in range(C):
                        last = pe.transpose(ov_turned[:, c, :], on[0:S, c * 8:(c + 1) * 8, :].rearrange("p h w -> p (h w)"),
                                            self.ident[0:S, 0:S])
                    last.then_inc(ot_mm, 1)

                def turn_probs(n, i, u, groups):
                    for g in groups:
                        pe.wait_ge(pt_read[g % 2], n * 2 + g // 2)
                        for j in range(H2):
                            last = pe.transpose(tp[g % 2][0:S, j * S:(j + 1) * S], prob[u][0:S, g, j, :], self.ident[0:S, 0:S])
                        last.then_inc(pt_mm[u], 1)

                def step_of(n, i, u, ahead_s, ahead_v):
                    if ahead_s:
                        scores(n + 1, 1 - u)
                    pe.wait_ge(exp_done, n + 1)
                    turn_probs(n, i, u, (0, 1))
                    turn_out(n - 1)
                    turn_probs(n, i, u, (2, 3))
                    if ahead_v:
                        values(n + 2, u)
                    pe.wait_ge(pt_read[0], n * 2 + 2)
                    pe.wait_ge(pt_read[1], n * 2 + 2)
                    pe.wait_ge(v_read, n + 1)
                    pe.wait_ge(ot_read, n + 1)
                    for g in range(4):
                        for j in range(H2):
                            head = 8 * (j // 2) + 2 * g + j % 2
                            last = pe.matmul(ov_heads[:, head, :], pt[0:S, g, j, :], va[u][0:S, head, :], start=True, stop=True)
                    last.then_inc(pv_mm, 1)

                scores(0, 0)
                values(0, 0)
                values(1, 1)
                pe.wait_ge(preset, 3)
                with pe.Fori(0, NB // 2 - 1) as i:
                    for u in range(2):
                        step_of(i * 2 + u, i, u, True, True)
                step_of(NB - 2, NB // 2 - 1, 0, True, False)
                step_of(NB - 1, NB // 2 - 1, 1, False, False)
                turn_out(NB - 1)

            @block.vector
            def _(dve):
                dve.memset(on[0:S], 0.0).then_inc(preset, 1)
                for u in range(2):
                    dve.memset(va[u][0:S], 1.0).then_inc(preset, 1)
                dve.wait_ge(s_mm, 1)
                dve.tensor_reduce(top[0:S], sc_heads, AX_X, ALU.max).then_inc(step, 1)
                dve.wait_ge(step, 1)
                dve.tensor_tensor(prob[0][0:S], sc_heads, inner(top[0:S], S), ALU.subtract).then_inc(s_read, 1)

                def step_of(n, i, u, ahead):
                    if ahead:
                        dve.wait_ge(s_mm, n + 2)
                        dve.tensor_reduce(top[0:S], sc_heads, AX_X, ALU.max).then_inc(step, 1)
                        dve.wait_ge(step, n * 2 + 2)
                        dve.wait_ge(pt_mm[1 - u], (i + u) * 4)
                        dve.tensor_tensor(prob[1 - u][0:S], sc_heads, inner(top[0:S], S), ALU.subtract).then_inc(s_read, 1)
                    dve.wait_ge(pv_mm, n + 1)
                    dve.reciprocal(rsum[0:S], ov_heads[:, :, HD]).then_inc(step, 1)
                    dve.wait_ge(step, n * 2 + (3 if ahead else 2))
                    dve.wait_ge(ot_mm, n + 1)
                    dve.tensor_tensor(on[0:S], ov_heads[:, :, 0:HD], inner(rsum[0:S], HD), ALU.mult).then_inc(o_norm, 1)

                with dve.Fori(0, NB // 2 - 1) as i:
                    for u in range(2):
                        step_of(i * 2 + u, i, u, True)
                step_of(NB - 2, NB // 2 - 1, 0, True)
                step_of(NB - 1, NB // 2 - 1, 1, False)

            @block.scalar
            def _(act):
                def exp(n, u):
                    act.wait_ge(s_read, n + 1)
                    act.activation(prob[u][0:S], prob[u][0:S], ACT.Exp, scale=1.0 / float(HD) ** 0.5).then_inc(exp_done, 1)

                def copy_v(n, u):
                    act.wait_ge(v_mm, n + 1)
                    act.activation(va[u][0:S, :, 0:HD], pj[0:S, 0:D].rearrange("p (h w) -> p h w", w=HD), ACT.Copy).then_inc(v_read, 1)

                def copy_out(n):
                    act.wait_ge(ot_mm, n + 2)
                    act.activation(self.oT[:, :, bass.ds(n * S + OPAD, S)], ov_turned, ACT.Copy).then_inc(ot_read, 1)

                def step_of(n, i, u, ahead_s, ahead_v):
                    for g in range(4):
                        if g == 2:
                            copy_out(n - 1)
                        act.wait_ge(pt_mm[u], i * 4 + g + 1)
                        if g == 0:
                            act.wait_ge(pv_mm, n)
                        act.activation(pt[0:S, g], tp[g % 2][0:S, 0:H2 * S].rearrange("p (j s) -> p j s", s=S), ACT.Copy).then_inc(pt_read[g % 2], 1)
                    if ahead_s:
                        exp(n + 1, 1 - u)
                    if ahead_v:
                        act.wait_ge(pv_mm, n + 1)
                        copy_v(n + 2, u)

                act.wait_ge(preset, 3)
                copy_v(0, 0)
                copy_v(1, 1)
                exp(0, 0)
                with act.Fori(0, NB // 2 - 1) as i:
                    for u in range(2):
                        step_of(i * 2 + u, i, u, True, True)
                step_of(NB - 2, NB // 2 - 1, 0, True, False)
                step_of(NB - 1, NB // 2 - 1, 1, False, False)
                copy_out(NB - 1)

    def project(self, rep, w, bias, acc, load=None):
        nc, m, sem = self.nc, self.mem, self.sem
        m.at(self.work_at)
        o = [m.take(C, GW) for _ in range(2)]
        staged, biased, mm, added = sem("o_staged", 2), sem("acc_biased", 2), sem("wo_mm", 2), sem("wo_added", 2)
        I = NG // 2
        B = rep * I
        with ExitStack() as ctx:
            ps = [ctx.enter_context(nc.psum_tensor(f"wo{rep}_{u}", [P, 1024], F32)) for u in range(2)]
            block = ctx.enter_context(nc.Block())

            if load is not None:
                @block.sync
                def _(sp):
                    load(sp)

            @block.gpsimd
            def _(pool):
                with pool.Fori(0, I) as i:
                    for u in range(2):
                        pool.wait_ge(mm[u], B + i)
                        pool.tensor_copy(o[u], self.oT[:, :, bass.ds(i * (2 * GW) + (OPAD + GW * u), GW)]).then_inc(staged[u], 1)
                        pool.tensor_tensor(three(acc, i, u), three(acc, i, u), spread(bias, G), ALU.add).then_inc(biased[u], 1)

            @block.tensor
            def _(pe):
                with pe.Fori(0, I) as i:
                    for u in range(2):
                        pe.wait_ge(staged[u], B + i + 1)
                        pe.wait_ge(added[u], B + i)
                        for j in range(G):
                            for c in range(C):
                                last = pe.matmul(ps[u][:, j * D:(j + 1) * D], o[u][:, c, j * P:(j + 1) * P], w[:, c, :],
                                                 start=(c == 0), stop=(c == C - 1))
                        last.then_inc(mm[u], 1)

            @block.vector
            def _(dve):
                with dve.Fori(0, I) as i:
                    for u in range(2):
                        dve.wait_ge(mm[u], B + i + 1)
                        dve.wait_ge(biased[u], B + i + 1)
                        dve.tensor_tensor(three(acc, i, u), ps[u][:, 0:G * D].rearrange("p (j d) -> p j d", d=D),
                                          three(acc, i, u), ALU.add).then_inc(added[u], 1)

    def choose(self, scores, first, second, best, tmp, dve, link):
        rank = self.rank.unsqueeze(1).to_broadcast([P, NT, E])
        for k, hot in enumerate((first, second)):
            link(dve.tensor_reduce(best[k], scores, AX_X, ALU.max))
            link(dve.tensor_tensor(tmp, scores, inner(best[k], E), ALU.is_equal))
            link(dve.tensor_tensor(tmp, tmp, rank, ALU.mult))
            link(dve.tensor_reduce(self.top_rank, tmp, AX_X, ALU.max))
            link(dve.tensor_tensor(hot, inner(self.top_rank, E), rank, ALU.is_equal))
            if k == 0:
                link(dve.tensor_scalar(tmp, hot, -BIG, None, ALU.mult))
                link(dve.tensor_tensor(scores, scores, tmp, ALU.add))

    def route_first(self):
        nc, m, sem = self.nc, self.mem, self.sem
        m.at(self.work_at)
        m.take(NT, E + 1)
        self.gates = m.take(NT, E + 1)
        kept = m.pos
        tmp, first, second = m.take(NT, E), m.take(NT, E), m.take(NT, E)
        best = [m.take(NT) for _ in range(2)]
        total = m.take(NT)
        self.route_end = kept
        exped, step, done = sem("route_exp"), sem("route_step"), sem("gates_ready")
        lg = self.lg
        with nc.Block() as block:
            @block.scalar
            def _(act):
                act.activation(lg, lg, ACT.Exp, scale=-1.0).then_inc(exped, 1)

            @block.vector
            def _(dve):
                link = Steps(dve, step, 0)
                link(dve.memset(self.gates, 1.0))
                dve.wait_ge(exped, 1)
                link(dve.tensor_scalar(lg, lg, 1.0, None, ALU.add))
                link(dve.reciprocal(lg, lg))
                link(dve.tensor_scalar(lg, lg, self.route_scale[:, 0:1], None, ALU.mult))
                self.choose(lg, first, second, best, tmp, dve, link)
                link(dve.tensor_tensor(total, best[0], best[1], ALU.add))
                link(dve.reciprocal(total, total))
                for b, hot in zip(best, (first, second)):
                    link(dve.tensor_tensor(b, b, total, ALU.mult))
                    link(dve.tensor_tensor(hot, hot, inner(b, E), ALU.mult))
                link(dve.tensor_tensor(self.gates[:, :, 0:E], first, second, ALU.add))

    def experts(self):
        nc, m, sem = self.nc, self.mem, self.sem
        X = E + 1
        R = 3
        m.at(self.route_end)
        hid = [m.take(GW) for _ in range(R)]
        gs = [m.take(G, X) for _ in range(2)]
        gt = [m.take(GW) for _ in range(2)]
        e2_b = m.take(D)
        b_in = sem("e2_b_in")
        gs_ready, gt_mm, gt_ready = sem("gate_staged", 2), sem("gate_turned", 2), sem("gate_copied", 2)
        up_mm, gelu, po_mm, po_read = sem("up_mm", R), sem("gelu_done", R), sem("down_mm", G), sem("down_read", G)
        I = NG // 2
        with ExitStack() as ctx:
            up = [ctx.enter_context(nc.psum_tensor(f"up{r}", [P, 512], F32)) for r in range(R)]
            po = [ctx.enter_context(nc.psum_tensor(f"down{j}", [P, 512], F32)) for j in range(G)]
            tg = ctx.enter_context(nc.psum_tensor("turned_gate", [P, 512], F32))
            block = ctx.enter_context(nc.Block())

            @block.sync
            def _(sp):
                sp.dma_start(e2_b[0:X], self.t["e2_b"]).then_inc(b_in, 16)

            @block.tensor
            def _(pe):
                pe.wait_ge(b_in, 16)
                with pe.Fori(0, I) as i:
                    for u in range(2):
                        it = i * 2 + u

                        def rise(e):
                            r = e % R
                            pe.wait_ge(gelu[r], it * R + e // R)
                            for c in range(C):
                                last = pe.matmul(up[r][:, 0:GW], self.e1[:, e, c, :], self.xT[:, c, bass.ds(i * (2 * GW) + GW * u, GW)],
                                                 start=(c == 0), stop=(c == C - 1))
                            last.then_inc(up_mm[r], 1)

                        def fall(e):
                            r = e % R
                            pe.wait_ge(gelu[r], it * R + e // R + 1)
                            for j in range(G):
                                pe.wait_ge(po_read[j], it * (X + 1) + e + 1)
                                last = pe.matmul(po[j][:, 0:D], hid[r][:, j * P:(j + 1) * P], self.e2[:, e, :], start=True, stop=True)
                                last.then_inc(po_mm[j], 1)

                        rise(0)
                        pe.wait_ge(gs_ready[u], i + 1)
                        if u == 0:
                            pe.wait_ge(gt_ready[1], i)
                        else:
                            pe.wait_ge(gt_ready[0], i + 1)
                        for j in range(G):
                            last = pe.transpose(tg[0:X, j * P:(j + 1) * P], gs[u][:, j, :], self.ident)
                        last.then_inc(gt_mm[u], 1)
                        rise(1)
                        pe.wait_ge(gt_ready[u], i + 1)
                        for j in range(G):
                            pe.wait_ge(po_read[j], it * (X + 1))
                            last = pe.matmul(po[j][:, 0:D], gt[u][0:X, j * P:(j + 1) * P], e2_b[0:X, :], start=True, stop=True)
                            last.then_inc(po_mm[j], 1)
                        for e in range(X):
                            fall(e)
                            if e + 2 < X:
                                rise(e + 2)

            @block.scalar
            def _(act):
                with act.Fori(0, I) as i:
                    for u in range(2):
                        it = i * 2 + u
                        for e in range(X):
                            r = e % R
                            act.wait_ge(up_mm[r], it * R + e // R + 1)
                            act.wait_ge(po_mm[G - 1], it * (X + 1) + (e - R + 2 if e >= R else 0))
                            act.activation(hid[r], up[r][:, 0:GW], ACT.Gelu, bias=self.e1_b[:, e:e + 1]).then_inc(gelu[r], 1)
                            if e == 0:
                                act.wait_ge(gt_mm[u], i + 1)
                                act.activation(gt[u][0:X], tg[0:X, 0:GW], ACT.Copy).then_inc(gt_ready[u], 1)

            @block.vector
            def _(dve):
                with dve.Fori(0, I) as i:
                    for u in range(2):
                        it = i * 2 + u
                        dve.tensor_copy(gs[u], self.gates[:, bass.ds(i * (2 * G) + G * u, G), :]).then_inc(gs_ready[u], 1)
                        dve.wait_ge(gs_ready[u], i + 1)
                        for r in range(X + 1):
                            for j in range(G):
                                dve.wait_ge(po_mm[j], it * (X + 1) + r + 1)
                                acc = one(self.h, i, u, j)
                                if r == 0:
                                    ins = dve.tensor_tensor(acc, po[j][:, 0:D], acc, ALU.add)
                                else:
                                    dve.wait_ge(po_read[j], it * (X + 1) + r)
                                    ins = dve.scalar_tensor_tensor(out=acc, in0=po[j][:, 0:D], scalar=gs[u][:, j, r - 1:r],
                                                                   in1=acc, op0=ALU.mult, op1=ALU.add)
                                ins.then_inc(po_read[j], 1)

    def linear_attention(self):
        nc, m, sem = self.nc, self.mem, self.sem
        NP = NB // 2
        QK = 2 * D
        m.at(self.early_end)
        qb = m.take(2, QK)
        kvm = m.take(2, C, P)
        qT = m.take(C, 2, S)
        x = [m.take(C, PAIR) for _ in range(2)]
        m.at(self.work_at)
        el = [m.take(2, QK) for _ in range(2)]
        ex = [m.take(2, QK) for _ in range(2)]
        vb = [m.take(2, D) for _ in range(2)]
        nrm, var, tmp = m.take(2, 2 * HEADS), m.take(2, 2 * HEADS), m.take(2, 2 * HEADS)
        staged, pj_mm, qk_read, v_read = sem("la_x_staged"), sem("la_proj_mm"), sem("la_qk_read"), sem("la_v_read")
        e_done, r_done, el_done, sq_done = sem("la_exp"), sem("la_relu"), sem("la_elu"), sem("la_square")
        rn_done, n_done, tkv_mm, kv_read = sem("la_norms"), sem("la_unit"), sem("la_kv_mm"), sem("la_kv_read")
        qT_read, c_mm, c_read, step, zeroed = sem("la_q_copied"), sem("la_ctx_mm"), sem("la_ctx_copied"), sem("la_step"), sem("la_zeroed")
        per = 2 * RSQRT_STEPS

        with ExitStack() as ctx:
            pq = [ctx.enter_context(nc.psum_tensor(f"la_qk{u}", [P, 2, 512], F32)) for u in range(2)]
            pv = ctx.enter_context(nc.psum_tensor("la_v", [P, 2, D], F32))
            pkv = ctx.enter_context(nc.psum_tensor("la_kv", [P, 2, C, P], F32))
            pt = ctx.enter_context(nc.psum_tensor("la_qT", [P, 512], F32))
            pc = ctx.enter_context(nc.psum_tensor("la_ctx", [P, 512], F32))
            block = ctx.enter_context(nc.Block())

            @block.gpsimd
            def _(pool):
                def stage(p, u):
                    pool.tensor_copy(x[u], self.xT[:, :, bass.ds(p * PAIR, PAIR)]).then_inc(staged, 1)

                pool.memset(el[1][0:S], 0.0).then_inc(zeroed, 1)
                pool.memset(vb[1][0:S], 0.0).then_inc(zeroed, 1)
                stage(0, 0)
                stage(1, 1)
                with pool.Fori(0, NP // 2) as i:
                    for u in range(2):
                        p = i * 2 + u
                        pool.wait_ge(pj_mm, p + 1)
                        stage(p + 2, u)
                        pool.wait_ge(rn_done, p + 1)
                        heads = el[u][0:S].rearrange("p b (h w) -> p (b h) w", w=HD)
                        pool.tensor_tensor(heads, heads, inner(nrm[0:S].rearrange("p b h -> p (b h)"), HD), ALU.mult).then_inc(n_done, 1)

            @block.tensor
            def _(pe):
                def proj(p, u):
                    pe.wait_ge(staged, p + 1)
                    for b in range(2):
                        for c in range(C):
                            pe.matmul(pq[u][0:S, b, :], x[u][:, c, b * S:(b + 1) * S], self.wqk1[:, c, :], start=(c == 0), stop=(c == C - 1))
                    pe.wait_ge(v_read, p)
                    for b in range(2):
                        for c in range(C):
                            last = pe.matmul(pv[0:S, b, :], x[u][:, c, b * S:(b + 1) * S], self.wv1[:, c, :], start=(c == 0), stop=(c == C - 1))
                    last.then_inc(pj_mm, 1)

                def turn_kv(p, u):
                    pe.wait_ge(n_done, p + 1)
                    pe.wait_ge(v_read, p + 1)
                    for c in range(C):
                        for b in range(2):
                            pe.transpose(pt[:, (c * 2 + b) * S:(c * 2 + b + 1) * S], el[u][0:S, b, c * P:(c + 1) * P], self.ident[0:S, 0:S])
                    for b in range(2):
                        for c in range(C):
                            last = pe.matmul(pkv[:, b, c, :], el[u][0:S, b, D + c * P:D + (c + 1) * P], vb[u][0:S, b, c * P:(c + 1) * P],
                                             start=True, stop=True)
                    last.then_inc(tkv_mm, 1)

                def context(p):
                    pe.wait_ge(kv_read, p + 2)
                    pe.wait_ge(qT_read, p + 2)
                    pe.wait_ge(c_read, p + 1)
                    for c in range(C):
                        for b in range(2):
                            last = pe.matmul(pc[:, (c * 2 + b) * S:(c * 2 + b + 1) * S], kvm[:, b, c, :], qT[:, c, b, :], start=True, stop=True)
                    last.then_inc(c_mm, 1)

                proj(0, 0)
                proj(1, 1)
                pe.wait_ge(zeroed, 2)
                with pe.Fori(0, NP // 2) as i:
                    for u in range(2):
                        p = i * 2 + u
                        turn_kv(p - 1, 1 - u)
                        pe.wait_ge(qk_read, p + 1)
                        proj(p + 2, u)
                        context(p - 1)
                turn_kv(NP - 1, 1)
                context(NP - 1)

            @block.vector
            def _(dve):
                def bias(p, u):
                    dve.wait_ge(pj_mm, p + 1)
                    dve.wait_ge(e_done, p)
                    dve.wait_ge(r_done, p)
                    dve.tensor_tensor(qb[0:S], pq[u][0:S], spread(self.bqk1, 2)[0:S], ALU.add).then_inc(qk_read, 1)
                    dve.wait_ge(tkv_mm, p)
                    dve.tensor_tensor(vb[u][0:S], pv[0:S], spread(self.bv1, 2)[0:S], ALU.add).then_inc(v_read, 1)
                    dve.wait_ge(qk_read, p + 1)
                    dve.tensor_scalar(el[u][0:S], qb[0:S], 0.0, -1.0, ALU.max, ALU.add).then_inc(r_done, 1)

                def mask():
                    dve.tensor_tensor(kvm, pkv[:, :, :, :], self.head_mask.unsqueeze(1).unsqueeze(1).to_broadcast([P, 2, C, P]), ALU.mult).then_inc(kv_read, 1)

                dve.wait_ge(zeroed, 2)
                bias(0, 0)
                with dve.Fori(0, NP // 2) as i:
                    link = Steps(dve, step, i * per)
                    for u in range(2):
                        p = i * 2 + u
                        dve.wait_ge(e_done, p + 1)
                        dve.wait_ge(r_done, p + 1)
                        dve.scalar_tensor_tensor(out=el[u][0:S].rearrange("p b d -> p (b d)"), in0=ex[u][0:S].rearrange("p b d -> p (b d)"),
                                                 scalar=1.0, in1=el[u][0:S].rearrange("p b d -> p (b d)"), op0=ALU.min, op1=ALU.add).then_inc(el_done, 1)
                        bias(p + 1, 1 - u)
                        dve.wait_ge(sq_done, p + 1)
                        dve.wait_ge(n_done, p)
                        link(dve.tensor_reduce(var[0:S], ex[u][0:S].rearrange("p b (h w) -> p b h w", w=HD), AX_X, ALU.add))
                        rsqrt(dve, link, var[0:S], 0.0, nrm[0:S], tmp[0:S], rn_done)
                        dve.wait_ge(tkv_mm, p + 1)
                        dve.wait_ge(c_mm, p)
                        mask()
                    assert link.n == per, (link.n, per)
                dve.wait_ge(tkv_mm, NP + 1)
                dve.wait_ge(c_mm, NP)
                mask()

            @block.scalar
            def _(act):
                def exp(p, u):
                    act.wait_ge(qk_read, p + 1)
                    act.activation(ex[u][0:S], qb[0:S], ACT.Exp).then_inc(e_done, 1)

                def copy_q(p):
                    act.wait_ge(tkv_mm, p + 2)
                    act.wait_ge(c_mm, p + 1)
                    act.activation(qT.rearrange("p c b s -> p (c b s)"), pt[:, 0:C * PAIR], ACT.Copy).then_inc(qT_read, 1)

                def copy_out(p):
                    act.wait_ge(c_mm, p + 2)
                    act.activation(self.oT[:, :, bass.ds(p * PAIR + OPAD, PAIR)], pc[:, 0:C * PAIR].rearrange("p (c s) -> p c s", c=C),
                                   ACT.Copy).then_inc(c_read, 1)

                exp(0, 0)
                with act.Fori(0, NP // 2) as i:
                    for u in range(2):
                        p = i * 2 + u
                        act.wait_ge(el_done, p + 1)
                        act.activation(ex[u][0:S], el[u][0:S], ACT.Square).then_inc(sq_done, 1)
                        copy_q(p - 1)
                        act.wait_ge(rn_done, p)
                        exp(p + 1, 1 - u)
                        copy_out(p - 1)
                copy_q(NP - 1)
                copy_out(NP - 1)

    def feed_forward(self):
        nc, m, sem = self.nc, self.mem, self.sem
        R = 4
        m.at(self.work_at)
        hid = [m.take(KF, GW) for _ in range(2)]
        up_mm, gelu, down_mm, down_read, biased = sem("ff_up_mm", R), sem("ff_gelu", R), sem("ff_down_mm", G), sem("ff_down_read", G), sem("ff_biased")
        I = NG // 2
        with ExitStack() as ctx:
            up = [ctx.enter_context(nc.psum_tensor(f"ff_up{r}", [P, 512], F32)) for r in range(R)]
            po = [ctx.enter_context(nc.psum_tensor(f"ff_down{j}", [P, 512], F32)) for j in range(G)]
            block = ctx.enter_context(nc.Block())

            @block.gpsimd
            def _(pool):
                with pool.Fori(0, I) as i:
                    for u in range(2):
                        pool.tensor_tensor(three(self.xn, i, u), three(self.xn, i, u), spread(self.f2_b, G), ALU.add).then_inc(biased, 1)

            @block.tensor
            def _(pe):
                with pe.Fori(0, I) as i:
                    for u in range(2):
                        it = i * 2 + u
                        for k in range(KF):
                            pe.wait_ge(gelu[k % R], it * (KF // R) + k // R)
                            for c in range(C):
                                last = pe.matmul(up[k % R][:, 0:GW], self.f1[:, c, k * P:(k + 1) * P],
                                                 self.xT[:, c, bass.ds(i * (2 * GW) + GW * u, GW)], start=(c == 0), stop=(c == C - 1))
                            last.then_inc(up_mm[k % R], 1)
                        for j in range(G):
                            pe.wait_ge(down_read[j], it)
                            for k in range(KF):
                                if j == 0:
                                    pe.wait_ge(gelu[k % R], it * (KF // R) + k // R + 1)
                                last = pe.matmul(po[j][:, 0:D], hid[u][:, k, j * P:(j + 1) * P], self.f2[:, k, :],
                                                 start=(k == 0), stop=(k == KF - 1))
                            last.then_inc(down_mm[j], 1)

            @block.scalar
            def _(act):
                with act.Fori(0, I) as i:
                    for u in range(2):
                        it = i * 2 + u
                        for k in range(KF):
                            act.wait_ge(up_mm[k % R], it * (KF // R) + k // R + 1)
                            act.activation(hid[u][:, k, :], up[k % R][:, 0:GW], ACT.Gelu, bias=self.f1_b[:, k:k + 1]).then_inc(gelu[k % R], 1)

            @block.vector
            def _(dve):
                with dve.Fori(0, I) as i:
                    for u in range(2):
                        it = i * 2 + u
                        dve.wait_ge(biased, it + 1)
                        for j in range(G):
                            dve.wait_ge(down_mm[j], it + 1)
                            acc = one(self.xn, i, u, j)
                            dve.tensor_tensor(acc, po[j][:, 0:D], acc, ALU.add).then_inc(down_read[j], 1)

    def route_second(self):
        nc, m, sem, t = self.nc, self.mem, self.sem, self.t
        m.at(self.keep_at)
        self.slot = [m.take(NT).bitcast(U32) for _ in range(2)]
        self.weight = [m.take(NT) for _ in range(2)]
        self.owner = m.take(XBLK).bitcast(U32)
        m.at(self.route_at)
        tmp, first, second, place = m.take(NT, E), m.take(NT, E), m.take(NT, E), m.take(NT, E)
        total, cnt, blocks, base, fin = m.take(NT), m.take(E), m.take(E), m.take(E), m.take(E)
        over, before, past = m.take(E, NT), m.take(E, E), m.take(XBLK, E)
        own = m.take(XBLK)
        hits = m.take(NT * E // 2).bitcast(mybir.dt.bfloat16).rearrange("p (a e) -> p a e", e=E)
        tri = m.take(P // 2).bitcast(mybir.dt.bfloat16)
        ones = m.take(P // 2).bitcast(mybir.dt.bfloat16)
        consts = {"tri": m.take(P), "valid": m.take(NT), "steps": m.take(NT), "lower": m.take(E, E), "blocks": m.take(XBLK)}
        c_in, exped, step = sem("route_consts_in"), sem("route2_exp"), sem("route2_step")
        hit, ranked, slots, placed = sem("hits_ready"), sem("ranks_mm"), sem("slots_ready"), sem("rows_placed")
        lg = self.lg
        with ExitStack() as ctx:
            rk = ctx.enter_context(nc.psum_tensor("ranks", [P, NT, E], F32))
            ct = ctx.enter_context(nc.psum_tensor("counts", [P, 512], F32))
            block = ctx.enter_context(nc.Block())

            @block.sync
            def _(sp):
                for name, view in consts.items():
                    sp.dma_start(view, t["r_" + name]).then_inc(c_in, 16)
                sp.wait_ge(self.filled, 16 * XBLK // 4)

            @block.scalar
            def _(act):
                act.wait_ge(step, 2)
                act.activation(lg, lg, ACT.Exp).then_inc(exped, 1)

            @block.vector
            def _(dve):
                link = Steps(dve, step, 0)
                link(dve.tensor_reduce(total, lg, AX_X, ALU.max))
                link(dve.tensor_tensor(lg, lg, inner(total, E), ALU.subtract))
                dve.wait_ge(exped, 1)
                link(dve.tensor_reduce(total, lg, AX_X, ALU.add))
                link(dve.reciprocal(total, total))
                link(dve.tensor_tensor(lg, lg, inner(total, E), ALU.mult))
                self.choose(lg, first, second, self.weight, tmp, dve, link)
                link(dve.tensor_tensor(total, self.weight[0], self.weight[1], ALU.add))
                link(dve.tensor_scalar(total, total, 1e-8, None, ALU.add))
                link(dve.reciprocal(total, total))
                for w in self.weight:
                    link(dve.tensor_tensor(w, w, total, ALU.mult))
                dve.wait_ge(c_in, 16 * len(consts))
                link(dve.tensor_tensor(tmp, first, second, ALU.add))
                link(dve.tensor_copy(tri, consts["tri"]))
                link(dve.memset(ones, 1.0))
                dve.tensor_tensor(hits, tmp, inner(consts["valid"], E), ALU.mult).then_inc(hit, 1)
                dve.wait_ge(ranked, 1)
                link(dve.tensor_copy(cnt, ct[:, 0:E]))
                link(dve.tensor_tensor(over, inner(cnt, NT), spread(consts["steps"], E), ALU.is_gt))
                link(dve.tensor_reduce(blocks, over, AX_X, ALU.add))
                link(dve.tensor_tensor(before, consts["lower"], spread(blocks, E), ALU.mult))
                link(dve.tensor_reduce(base, before, AX_X, ALU.add))
                link(dve.tensor_tensor(fin, base, blocks, ALU.add))
                link(dve.tensor_tensor(past, inner(consts["blocks"], E), spread(fin, XBLK), ALU.is_ge))
                link(dve.tensor_reduce(own, past, AX_X, ALU.add))
                link(dve.tensor_scalar(self.owner, own, float(E - 1), None, ALU.min))
                link(dve.tensor_scalar(base, base, float(P), None, ALU.mult))
                link(dve.tensor_tensor(place, rk[:, :, :], spread(base, NT), ALU.add))
                for k, hot in enumerate((first, second)):
                    link(dve.tensor_tensor(tmp, place, hot, ALU.mult))
                    link(dve.tensor_reduce(total, tmp, AX_X, ALU.add))
                    dve.tensor_copy(self.slot[k], total).then_inc(slots, 1)
                    dve.wait_ge(slots, k + 1)

            @block.tensor
            def _(pe):
                pe.wait_ge(hit, 1)
                pe.matmul(rk[:, :, :], tri, hits, start=True, stop=False)
                for a in range(1, NT):
                    pe.matmul(rk[:, a:, :], ones, hits[:, 0:NT - a, :], start=False, stop=(a == NT - 1))
                for a in range(NT):
                    last = pe.matmul(ct[:, 0:E], ones, hits[:, a, :], start=(a == 0), stop=(a == NT - 1))
                last.then_inc(ranked, 1)

            @block.gpsimd
            def _(pool):
                pool.wait_ge(slots, 2)
                pool.wait_ge(self.filled, 16 * XBLK // 4)
                for k in range(2):
                    for a in range(NT):
                        n = P if a < NT - 1 else LAST
                        pool.indirect_dma_start(
                            out=self.slots_in, out_offset=bass.IndirectOffsetOnAxis(ap=self.slot[k][0:n, a:a + 1], axis=0),
                            in_=self.xn[0:n, a, :], in_offset=None).then_inc(placed, 16)
                pool.wait_ge(placed, 16 * 2 * NT)

    def routed(self):
        nc, m, sem, t = self.nc, self.mem, self.sem, self.t
        m.at(self.route_at)
        w2_b = m.take(E, D)
        w1_b = m.take(E * KF)
        xg = [m.take(D) for _ in range(2)]
        xT = [m.take(C, P) for _ in range(2)]
        hb = [m.take(FF) for _ in range(2)]
        hT = [m.take(KF, P) for _ in range(2)]
        y = [m.take(D) for _ in range(2)]
        b_in, xg_in, tx_mm, xt_read = sem("moe_bias_in"), sem("slot_rows_in", 2), sem("slot_rows_turned"), sem("slot_rows_copied")
        g1_mm, h_read, th_mm, gl = sem("moe_up_mm"), sem("moe_up_copied"), sem("hidden_turned"), sem("moe_gelu", 2)
        g2_mm, y_read, stored = sem("moe_down_mm", 2), sem("moe_down_read"), sem("slot_rows_stored", 2)
        self.slots_out = self.dram("slots_out", [NBLK * P, D])
        HK = KF // 2
        with ExitStack() as ctx:
            px = ctx.enter_context(nc.psum_tensor("moe_xT", [P, 512], F32))
            p1 = [ctx.enter_context(nc.psum_tensor(f"moe_up{f}", [P, 512], F32)) for f in range(2)]
            pt = [ctx.enter_context(nc.psum_tensor(f"moe_hT{f}", [P, 512], F32)) for f in range(2)]
            p2 = ctx.enter_context(nc.psum_tensor("moe_down", [P, 512], F32))
            block = ctx.enter_context(nc.Block())

            def owner_of(eng, n):
                return eng.value_load(self.owner[0:1, bass.ds(n, 1)], min_val=0, max_val=E - 1)

            @block.sync
            def _(sp):
                sp.dma_start(w2_b, t["w2_b"].rearrange("p (e d) -> p e d", e=E)).then_inc(b_in, 16)
                sp.dma_start(w1_b, t["w1_b"]).then_inc(b_in, 16)

                def load(n, u):
                    sp.dma_start(xg[u], self.slots_in[bass.ds(n * P, P), :]).then_inc(xg_in[u], 16)

                load(0, 0)
                load(1, 1)
                with sp.Fori(0, NBLK // 2) as i:
                    for u in range(2):
                        n = i * 2 + u
                        sp.wait_ge(tx_mm, n + 1)
                        load(n + 2, u)
                        sp.wait_ge(y_read, n + 1)
                        sp.dma_start(self.slots_out[bass.ds(n * P, P), :], y[u]).then_inc(stored[u], 16)
                for u in range(2):
                    sp.wait_ge(stored[u], 16 * (NBLK // 2))
                    sp.wait_ge(xg_in[u], 16 * (XBLK // 2))

            @block.tensor
            def _(pe):
                def turn_x(n, i, u):
                    pe.wait_ge(xg_in[u], i * 16 + 16)
                    pe.wait_ge(xt_read, n)
                    for c in range(C):
                        last = pe.transpose(px[:, c * P:(c + 1) * P], xg[u][:, c * P:(c + 1) * P], self.ident)
                    last.then_inc(tx_mm, 1)

                def rise(n, u, free):
                    e = owner_of(pe, n)
                    pe.wait_ge(xt_read, n + 1)
                    for f in range(2):
                        if free:
                            pe.wait_ge(h_read, n * 2 - 1 + f)
                        for c in range(C):
                            last = pe.matmul(p1[f][:, :], xT[u][:, c, :], self.w1[:, c, bass.ds(e * FF + f * (FF // 2), FF // 2)],
                                             start=(c == 0), stop=(c == C - 1))
                        last.then_inc(g1_mm, 1)

                pe.wait_ge(self.w1_in, 16 * C)
                turn_x(0, 0, 0)
                rise(0, 0, False)
                turn_x(1, 0, 1)
                pe.wait_ge(self.w2_in, 16 * 2)
                with pe.Fori(0, NBLK // 2) as i:
                    for u in range(2):
                        n = i * 2 + u
                        for f in range(2):
                            pe.wait_ge(h_read, n * 2 + f + 1)
                            pe.wait_ge(gl[f], n * HK)
                            for k in range(HK):
                                a = (f * HK + k) * P
                                last = pe.transpose(pt[f][:, k * P:(k + 1) * P], hb[u][:, a:a + P], self.ident)
                            last.then_inc(th_mm, 1)
                        rise(n + 1, 1 - u, True)
                        turn_x(n + 2, i + 1, u)
                        e = owner_of(pe, n)
                        pe.wait_ge(y_read, n)
                        for k in range(KF):
                            if k % HK == 0:
                                pe.wait_ge(gl[k // HK], n * HK + HK)
                            last = pe.matmul(p2[:, 0:D], hT[u][:, k, :], self.w2[:, bass.ds(e * KF + k, 1), :].rearrange("p a d -> p (a d)"),
                                             start=(k == 0), stop=(k == KF - 1))
                        last.then_inc(g2_mm[u], 1)

            @block.vector
            def _(dve):
                def copy_h(n, u, f):
                    dve.wait_ge(g1_mm, n * 2 + f + 1)
                    dve.tensor_copy(hb[u][:, f * 512:(f + 1) * 512], p1[f][:, :]).then_inc(h_read, 1)

                dve.wait_ge(b_in, 32)
                for f in range(2):
                    copy_h(0, 0, f)
                with dve.Fori(0, NBLK // 2) as i:
                    for u in range(2):
                        n = i * 2 + u
                        dve.wait_ge(th_mm, n * 2)
                        for f in range(2):
                            copy_h(n + 1, 1 - u, f)
                        e = owner_of(dve, n)
                        dve.wait_ge(g2_mm[u], i + 1)
                        dve.wait_ge(stored[u], i * 16)
                        dve.tensor_tensor(y[u], p2[:, 0:D], w2_b[:, bass.ds(e, 1), :].rearrange("p a d -> p (a d)"), ALU.add).then_inc(y_read, 1)

            @block.scalar
            def _(act):
                def copy_x(n, u):
                    act.wait_ge(tx_mm, n + 1)
                    act.activation(xT[u], px[:, 0:D].rearrange("p (c n) -> p c n", c=C), ACT.Copy).then_inc(xt_read, 1)

                act.wait_ge(b_in, 32)
                copy_x(0, 0)
                copy_x(1, 1)
                with act.Fori(0, NBLK // 2) as i:
                    for u in range(2):
                        n = i * 2 + u
                        e = owner_of(act, n)
                        act.wait_ge(g2_mm[u], i)
                        for k in range(KF):
                            if k % HK == 0:
                                act.wait_ge(th_mm, n * 2 + k // HK + 1)
                            act.activation(hT[u][:, k, :], pt[k // HK][:, (k % HK) * P:(k % HK + 1) * P], ACT.Gelu_apprx_tanh,
                                           bias=w1_b[:, bass.ds(e * KF + k, 1)]).then_inc(gl[k // HK], 1)
                        act.wait_ge(g1_mm, n * 2 + 2)
                        copy_x(n + 2, u)

    def combine(self):
        nc, m, sem = self.nc, self.mem, self.sem
        R = 3
        m.at(self.route_at)
        got = [[m.take(D) for _ in range(2)] for _ in range(R)]
        got_in, mixed, stored = sem("choice_in", R), sem("choice_mixed", R), sem("out_stored")
        with nc.Block() as block:
            @block.gpsimd
            def _(pool):
                for a in range(NT):
                    n = P if a < NT - 1 else LAST
                    if a >= R:
                        pool.wait_ge(mixed[a % R], a // R * 2)
                    for k in range(2):
                        pool.indirect_dma_start(out=got[a % R][k][0:n], out_offset=None, in_=self.slots_out,
                                                in_offset=bass.IndirectOffsetOnAxis(ap=self.slot[k][0:n, a:a + 1], axis=0)
                                                ).then_inc(got_in[a % R], 16)

            @block.vector
            def _(dve):
                for a in range(NT):
                    n = P if a < NT - 1 else LAST
                    dve.wait_ge(got_in[a % R], 32 * (a // R + 1))
                    for k in range(2):
                        dve.scalar_tensor_tensor(out=self.h[0:n, a, :], in0=got[a % R][k][0:n], scalar=self.weight[k][0:n, a:a + 1],
                                                 in1=self.h[0:n, a, :], op0=ALU.mult, op1=ALU.add).then_inc(mixed[a % R], 1)
                        dve.wait_ge(mixed[a % R], a // R * 2 + k + 1)

            @block.sync
            def _(sp):
                for a in range(NT):
                    n = P if a < NT - 1 else LAST
                    sp.wait_ge(mixed[a % R], a // R * 2 + 2)
                    sp.dma_start(self.out[a * P:a * P + n, :], self.h[0:n, a, :]).then_inc(stored, 16)
                sp.wait_ge(stored, 16 * NT)

    def load_w1(self, sp):
        self.w1_in = self.sem("moe_w1_in")
        for c in range(C):
            sp.dma_start(self.w1[:, c, :], self.t["w1"][:, c, :]).then_inc(self.w1_in, 16)

    def load_w2(self, sp):
        self.w2_in = self.sem("moe_w2_in")
        half = E * KF // 2
        for j in range(2):
            sp.dma_start(self.w2[:, j * half:(j + 1) * half, :], self.t["w2"][:, j * half:(j + 1) * half, :]).then_inc(self.w2_in, 16)

    def run(self):
        self.embed()
        self.norm(0, self.h, 1e-5)
        self.rotate()
        self.attention()
        self.project(0, self.wo0, self.wo0_b, self.h)
        self.norm(1, self.h, 1e-5, gate=self.gate_w, logits=self.lg)
        self.route_first()
        self.experts()
        self.norm(2, self.h, 1e-5, keep=self.xn)
        self.linear_attention()
        self.project(1, self.wo1, self.bo1, self.xn, load=self.load_w1)
        self.norm(3, self.xn, 1e-12, gain=(self.g1, self.be1), keep=self.xn)
        self.feed_forward()
        self.norm(4, self.xn, 1e-12, gain=(self.g2, self.be2), turn=False, add_to=self.h, load=self.load_w2)
        self.norm(5, self.h, 1e-5, keep=self.xn, turn=False, gate=self.router, logits=self.lg)
        self.route_second()
        self.routed()
        self.combine()


def build(nc, dram, out):
    with ExitStack() as ctx:
        Kernel(nc, dram, out, ctx).run()


def layout(inp):
    f = {k: np.asarray(v) for k, v in inp.items()}
    a = {}

    def rows(v):
        return np.ascontiguousarray(np.broadcast_to(v.reshape(1, -1), (P, v.size)))

    def chunks(v):
        return np.ascontiguousarray(v.reshape(-1, P, v.shape[-1]).transpose(1, 0, 2))

    x = f["x"].reshape(NB, 3, 6, 16, 6, 16).transpose(1, 3, 5, 0, 2, 4).reshape(KP, P, NPT, P)
    a["patches"] = np.ascontiguousarray(x.transpose(2, 1, 0, 3))
    a["txt"] = f["txt"]
    a["wpatch"] = chunks(f["L0_tok_W"].T)
    pos = f["L0_tok_pos_embedding"][0]
    a["pos"] = np.ascontiguousarray(np.tile(pos[1:], (NB, 1)).reshape(NPT, P, D).transpose(1, 0, 2))
    a["tok_b"] = rows(f["L0_tok_b"])
    cls = np.stack([f["L0_tok_cls_token"][0, 0], pos[0]])
    a["cls"] = np.ascontiguousarray(np.broadcast_to(cls[None], (NB, 2, D)))
    turn = np.concatenate([np.arange(0, D, 2), np.arange(1, D, 2)])
    a["wqk0"] = np.ascontiguousarray(np.stack([chunks(f["L0_attn_wq"][turn].T), chunks(f["L0_attn_wk"][turn].T)], 1))
    a["wv0"] = chunks(f["L0_attn_wv"].T)
    a["wo0"] = chunks(f["L0_attn_wo_w"].T)
    a["wo0_b"] = rows(f["L0_attn_wo_b"])
    freq = np.exp(np.arange(0, D, 2, dtype=np.float32) * np.float32(-np.log(10000.0) / D))
    angle = (freq[:, None] * np.arange(S, dtype=np.float32)[None]).astype(np.float32)
    cos, sin = np.cos(angle).astype(np.float32), np.sin(angle).astype(np.float32)
    a["cos_sin"], a["sin_cos"] = np.stack([cos, sin], 1), np.stack([sin, cos], 1)
    par = (np.arange(P) // HD % 2)
    a["par_mask"] = np.stack([par == 0, par == 1], 1).astype(np.float32)
    e1 = np.concatenate([f["L0_ffn_W1"], f["L0_ffn_Ws1"][None]])
    a["e1"] = np.ascontiguousarray(e1.reshape(E + 1, C, P, P).transpose(2, 0, 1, 3))
    a["e1_b"] = np.ascontiguousarray(np.concatenate([f["L0_ffn_b1"], f["L0_ffn_bs1"][None]]).T)
    e2 = np.concatenate([f["L0_ffn_W2"], f["L0_ffn_Ws2"][None]])
    a["e2"] = np.ascontiguousarray(e2.transpose(1, 0, 2))
    a["e2_b"] = np.ascontiguousarray(np.concatenate([f["L0_ffn_b2"], f["L0_ffn_bs2"][None]]))
    a["gate_w"] = chunks(f["L0_ffn_gate_W"])
    a["route_scale"] = rows(f["L0_ffn_route_scale"].reshape(1))
    a["wqk1"] = chunks(np.concatenate([f["L1_attn_Wq"], f["L1_attn_Wk"]], 1))
    a["wv1"] = chunks(f["L1_attn_Wv"])
    a["bqk1"] = rows(np.concatenate([f["L1_attn_bq"], f["L1_attn_bk"]]))
    a["bv1"] = rows(f["L1_attn_bv"])
    a["wo1"] = chunks(f["L1_attn_Wo"])
    a["f1"] = chunks(f["L1_attn_W1"])
    a["f2"] = chunks(f["L1_attn_W2"])
    a["f1_b"] = np.ascontiguousarray(f["L1_attn_b1"].reshape(KF, P).T)
    for name, key in (("bo1", "bo"), ("f2_b", "b2"), ("g1", "g1"), ("be1", "be1"), ("g2", "g2"), ("be2", "be2")):
        a[name] = rows(f[f"L1_attn_{key}"])
    a["router"] = chunks(f["L1_ffn_router_w"].T)
    a["w1"] = np.ascontiguousarray(f["L1_ffn_w1"].reshape(E * FF, C, P).transpose(2, 1, 0))
    a["w2"] = np.ascontiguousarray(f["L1_ffn_w2"].transpose(0, 2, 1).reshape(E * KF, P, D).transpose(1, 0, 2))
    a["w1_b"] = np.ascontiguousarray(f["L1_ffn_b1"].reshape(E * KF, P).T)
    a["w2_b"] = rows(f["L1_ffn_b2"])
    same = (np.arange(P)[:, None] // HD == np.arange(P)[None] // HD)
    a["head_mask"] = (same / float(HD) ** 0.5).astype(np.float32)
    a["rank"] = rows(np.arange(E, 0, -1).astype(np.float32))
    a["r_tri"] = np.triu(np.ones((P, P), np.float32), 1)
    a["r_valid"] = (np.arange(NT)[None] * P + np.arange(P)[:, None] < N).astype(np.float32)
    a["r_steps"] = rows(np.arange(NT, dtype=np.float32) * P)
    a["r_lower"] = np.ascontiguousarray(np.broadcast_to(np.tril(np.ones((E, E), np.float32), -1), (P, E, E)))
    a["r_blocks"] = rows(np.arange(XBLK, dtype=np.float32))
    a["ident"] = np.eye(P, dtype=np.float32)
    return {k: np.ascontiguousarray(v) for k, v in a.items()}


def kernel(**inputs):
    import concourse.bacc as bacc
    from concourse.bass_utils import run_bass_kernel_spmd

    arrays = layout(inputs)
    nc = bacc.Bacc("TRN2", target_bir_lowering=False, num_devices=1)
    dram = {}
    for key, a in arrays.items():
        dram[key] = nc.dram_tensor(f"in_{key}_dram", a.shape, mybir.dt.from_np(a.dtype), kind="ExternalInput").ap()
    out = nc.dram_tensor("out_0_dram", [N, D], F32, kind="ExternalOutput").ap()
    build(nc, dram, out)
    feed = {f"in_{key}_dram": a for key, a in arrays.items()}
    result = run_bass_kernel_spmd(nc, [feed], core_ids=[0]).results[0]
    return result["out_0_dram"].reshape(NB, S, D)
```

```python
from contextlib import ExitStack

import numpy as np

import concourse.bass as bass
from concourse import mybir

ALU = mybir.AluOpType
ACT = mybir.ActivationFunctionType
AX_X = mybir.AxisListType.X
F32 = mybir.dt.float32
I32 = mybir.dt.int32
U32 = mybir.dt.uint32

P = 128
D = 256
C = D // P
NB = 32
PATCHES = 36
TXT = 32
S = 1 + PATCHES + TXT
N = NB * S
NT = -(-N // P)
LAST = N - (NT - 1) * P
G = 3
GW = G * P
NG = NT // G
NPT = NB * PATCHES // P
KP = 768 // P
HEADS = 16
HD = D // HEADS
HALF = 64 // HD
E = 8
FF = 1024
KF = FF // P
PAIR = 2 * S
XW = PAIR * (NB // 2 + 2)
OPAD = PAIR
OW = OPAD + NT * P
NBLK = (2 * N + E * (P - 1)) // P
XBLK = NBLK + 2
BIG = 1.0e30


class Memory:

    def __init__(self, nc, ctx, cols):
        self.t = ctx.enter_context(nc.sbuf_tensor("memory", [P, cols], F32))
        self.cols, self.pos = cols, 0

    def at(self, pos):
        self.pos = pos

    def take(self, *dims):
        n = int(np.prod(dims))
        a, self.pos = self.pos, self.pos + n
        assert self.pos <= self.cols, (self.pos, self.cols)
        v = self.t[:, a:a + n]
        if len(dims) == 1:
            return v
        names = "abcd"[:len(dims)]
        kw = {names[j]: dims[j] for j in range(1, len(dims))}
        return v.rearrange(f"p ({' '.join(names)}) -> p {' '.join(names)}", **kw)


class Steps:

    def __init__(self, eng, sem, base):
        self.eng, self.sem, self.base, self.n = eng, sem, base, 0

    def __call__(self, ins):
        ins.then_inc(self.sem, 1)
        self.n += 1
        self.eng.wait_ge(self.sem, self.base + self.n)


def inner(ap, k):
    return ap.unsqueeze(len(ap.shape)).to_broadcast(list(ap.shape) + [k])


def spread(ap, k):
    s = list(ap.shape)
    return ap.unsqueeze(1).to_broadcast([s[0], k] + s[1:])


MOMENT_STEPS = 6
RSQRT_STEPS = 12


def moments(dve, link, stats, mean, var, tmp):
    link(dve.tensor_tensor(mean, stats[:, :, 1], stats[:, :, 4], ALU.add))
    link(dve.tensor_tensor(tmp, stats[:, :, 1], stats[:, :, 4], ALU.subtract))
    link(dve.tensor_tensor(var, stats[:, :, 2], stats[:, :, 5], ALU.add))
    link(dve.tensor_scalar(mean, mean, 0.5, None, ALU.mult))
    link(dve.scalar_tensor_tensor(out=tmp, in0=tmp, scalar=0.25, in1=tmp, op0=ALU.mult, op1=ALU.mult))
    link(dve.scalar_tensor_tensor(out=var, in0=var, scalar=1.0 / D, in1=tmp, op0=ALU.mult, op1=ALU.add))


def rsqrt(dve, link, v, eps, y, t, done=None):
    link(dve.tensor_scalar(v, v, eps, None, ALU.add))
    link(dve.tensor_scalar(t.bitcast(I32), v.bitcast(I32), 1, None, ALU.arith_shift_right))
    link(dve.tensor_scalar(y.bitcast(I32), t.bitcast(I32), -1.0, float(0x5F3759DF), ALU.mult, ALU.add))
    for k in range(3):
        link(dve.tensor_tensor(t, v, y, ALU.mult))
        link(dve.scalar_tensor_tensor(out=t, in0=t, scalar=-0.5, in1=y, op0=ALU.mult, op1=ALU.mult))
        ins = dve.scalar_tensor_tensor(out=y, in0=t, scalar=1.5, in1=y, op0=ALU.add, op1=ALU.mult)
        if k == 2 and done is not None:
            ins.then_inc(done, 1)
        else:
            link(ins)


def three(tile, i, u):
    return tile[:, bass.ds(i * (2 * G) + G * u, G), :]


def one(tile, i, u, j):
    return tile[:, bass.ds(i * (2 * G) + (G * u + j), 1), :].rearrange("p a d -> p (a d)")


def cols(tile, i, u):
    return tile[:, :, bass.ds(i * (2 * GW) + GW * u, GW)]


class Kernel:
    def __init__(self, nc, t, out, ctx):
        self.nc, self.t, self.out, self.ctx = nc, t, out, ctx
        self.sems = {}
        self.zeroed = []
        self.norm_base = {}
        self.stats_count = 0
        m = self.mem = Memory(nc, ctx, 53100)
        self.h = m.take(NT, D)
        self.ident = m.take(P)
        self.head_mask = m.take(P)
        self.rank = m.take(E)
        self.top_rank = m.take(NT)
        self.lg = m.take(NT, E)
        self.stats = m.take(NT, 6)
        self.xn = m.take(NT, D)
        self.keep_at = m.pos
        m.take(2 * NT + 3 * XBLK)
        self.w1_at = m.pos
        self.w2_at = m.pos + C * E * FF
        self.work_at = self.w2_at + E * KF * D
        self.route_at = self.work_at
        self.w1 = m.take(C, E * FF)
        self.w2 = m.take(E * KF, D)
        m.at(self.w2_at)
        self.xT = m.take(C, XW)
        self.oT = m.take(C, OW)
        self.late_at = m.pos
        self.weights()

    def sem(self, name, n=None):
        if n is not None:
            return [self.sem(f"{name}{j}") for j in range(n)]
        if name not in self.sems:
            self.sems[name] = self.nc.alloc_semaphore(name)
        return self.sems[name]

    def retire(self, *prefixes):
        for handle in self.zeroed:
            self.nc.release_semaphore(handle)
        self.zeroed = [self.sems.pop(name) for name in list(self.sems) if name.startswith(prefixes)]
        for handle in self.zeroed:
            self.nc.gpsimd.sem_clear(handle)

    def dram(self, name, shape, dt=F32):
        return self.nc.dram_tensor(name, shape, dt, kind="Internal").ap()

    def weights(self):
        m = self.mem
        m.at(self.w1_at)
        self.early = {}
        def w(name, *dims):
            v = m.take(*dims)
            self.early[name] = v
            return v
        self.wpatch = w("wpatch", KP, D)
        self.pos = w("pos", NPT, D)
        self.wqk0 = w("wqk0", 2, C, D)
        self.wv0 = w("wv0", C, D)
        self.wo0 = w("wo0", C, D)
        self.wo0_b = w("wo0_b", D)
        self.tok_b = w("tok_b", D)
        self.cos_sin = w("cos_sin", 2, S)
        self.sin_cos = w("sin_cos", 2, S)
        self.own_mask = w("own_mask", 2, HALF)
        self.e1 = w("e1", E + 1, C, P)
        self.e1_b = w("e1_b", E + 1)
        self.e2 = w("e2", E + 1, D)
        self.gate_w = w("gate_w", C, E)
        self.route_scale = w("route_scale", 1)
        assert m.pos <= self.w2_at
        self.early_end = m.pos
        m.at(self.late_at)
        self.wqk1 = w("wqk1", C, 2 * D)
        self.wv1 = w("wv1", C, D)
        self.bv1 = w("bv1", D)
        self.wo1 = w("wo1", C, D)
        self.f1 = w("f1", C, FF)
        self.f2 = w("f2", KF, D)
        assert m.pos <= self.work_at, (m.pos, self.work_at)
        m.at(self.work_at)
        self.bqk1 = w("bqk1", 2 * D)
        self.f1_b = w("f1_b", KF)
        self.bo1 = w("bo1", D)
        self.f2_b = w("f2_b", D)
        self.g1 = w("g1", D)
        self.be1 = w("be1", D)
        self.g2 = w("g2", D)
        self.be2 = w("be2", D)
        self.router = w("router", C, E)
        self.work_at = m.pos

    def embed(self):
        nc, m, t, sem = self.nc, self.mem, self.t, self.sem
        R = 3
        m.at(self.early_end)
        patches = [m.take(KP, P) for _ in range(R)]
        m.at(self.work_at)
        rows = [m.take(D) for _ in range(R)]
        cls = m.take(2, D)
        tokens = self.dram("patch_tokens", [NPT * P, D])
        stream = self.stream = self.dram("stream", [N, D])
        by_batch = stream.rearrange("(b s) d -> b s d", s=S)
        first = ("wpatch", "pos", "tok_b")
        self.soon = ("wqk0", "cos_sin", "sin_cos", "own_mask", "wv0")
        in_emb, in_pos, in_cls = sem("weights_in_embed"), sem("pos_in"), sem("cls_in")
        self.soon_in, self.rest_in = sem("soon_weights_in"), sem("weights_in")
        patch_in, mm, summed, stored = sem("patch_in", R), sem("patch_mm", R), sem("patch_summed", R), sem("patch_stored", R)
        biased, cls_sum, moved = sem("pos_biased"), sem("cls_summed"), sem("stream_written")
        cleared, self.h_in = sem("pads_cleared"), sem("h_in")

        with ExitStack() as ctx:
            acc = [ctx.enter_context(nc.psum_tensor(f"embed_acc{r}", [P, 512], F32)) for r in range(R)]
            block = ctx.enter_context(nc.Block())

            @block.sync
            def _(sp):
                sp.dma_start(self.early["wpatch"], t["wpatch"]).then_inc(in_emb, 16)
                sp.dma_start(cls[0:NB], t["cls"]).then_inc(in_cls, 16)
                with sp.Fori(0, NPT // R) as i:
                    for r in range(R):
                        sp.wait_ge(mm[r], i)
                        sp.dma_start(patches[r], t["patches"][bass.ds(i * R + r, 1)].rearrange(
                            "a p k t -> (a p) k t")).then_inc(patch_in[r], 16)
                sp.dma_start(by_batch[:, 1 + PATCHES:, :], t["txt"]).then_inc(moved, 16)
                sp.wait_ge(cls_sum, 1)
                sp.dma_start(by_batch[:, 0, :], cls[0:NB, 0, :]).then_inc(moved, 16)
                for r in range(R):
                    sp.wait_ge(stored[r], 16 * (NPT // R))
                sp.dma_start(by_batch[:, 1:1 + PATCHES, :], tokens.rearrange("(b s) d -> b s d", s=PATCHES)).then_inc(moved, 16)
                sp.wait_ge(moved, 48)
                sp.wait_ge(cleared, 4)
                sp.dma_start(self.h[:, 0:NT - 1, :], stream[0:(NT - 1) * P, :].rearrange("(a p) d -> p a d", p=P)).then_inc(self.h_in, 16)
                sp.dma_start(self.h[0:LAST, NT - 1, :], stream[(NT - 1) * P:, :]).then_inc(self.h_in, 16)
                for name in self.soon:
                    sp.dma_start(self.early[name], t[name]).then_inc(self.soon_in, 16)
                for name, view in self.early.items():
                    if name not in first + self.soon:
                        sp.dma_start(view, t[name]).then_inc(self.rest_in, 16)
                for name, view in (("head_mask", self.head_mask), ("rank", self.rank)):
                    sp.dma_start(view, t[name]).then_inc(self.rest_in, 16)
                self.rest_count = len(self.early) - len(first) - len(self.soon) + 2
                sp.wait_ge(self.h_in, 32)

            @block.gpsimd
            def _(pool):
                pool.memset(self.h[:, NT - 1, :], 0.0).then_inc(cleared, 1)
                pool.memset(self.xT[:, :, NT * P:], 0.0).then_inc(cleared, 1)
                pool.memset(self.oT[:, :, 0:OPAD], 0.0).then_inc(cleared, 1)
                pool.memset(self.oT[:, :, OPAD + N:], 0.0).then_inc(cleared, 1)

            @block.tensor
            def _(pe):
                pe.wait_ge(in_emb, 16)
                with pe.Fori(0, NPT // R) as i:
                    for r in range(R):
                        pe.wait_ge(patch_in[r], 16 * i + 16)
                        pe.wait_ge(summed[r], i)
                        for k in range(KP):
                            last = pe.matmul(acc[r][:, 0:D], patches[r][:, k, :], self.wpatch[:, k, :],
                                             start=(k == 0), stop=(k == KP - 1))
                        last.then_inc(mm[r], 1)

            @block.vector
            def _(dve):
                dve.wait_ge(in_cls, 16)
                dve.tensor_tensor(cls[0:NB, 0, :], cls[0:NB, 0, :], cls[0:NB, 1, :], ALU.add).then_inc(cls_sum, 1)
                dve.wait_ge(in_pos, 48)
                dve.tensor_tensor(self.pos, self.pos, spread(self.tok_b, NPT), ALU.add).then_inc(biased, 1)
                dve.wait_ge(biased, 1)
                with dve.Fori(0, NPT // R) as i:
                    for r in range(R):
                        dve.wait_ge(mm[r], i + 1)
                        dve.wait_ge(stored[r], 16 * i)
                        dve.tensor_tensor(rows[r], acc[r][:, 0:D],
                                          self.pos[:, bass.ds(i * R + r, 1), :].rearrange("p a d -> p (a d)"),
                                          ALU.add).then_inc(summed[r], 1)

            @block.scalar
            def _(act):
                for name, view in (("pos", self.pos), ("tok_b", self.tok_b), ("ident", self.ident)):
                    act.dma_start(view, t[name]).then_inc(in_pos, 16)
                with act.Fori(0, NPT // R) as i:
                    for r in range(R):
                        act.wait_ge(summed[r], i + 1)
                        act.dma_start(tokens[bass.ds((i * R + r) * P, P), :], rows[r]).then_inc(stored[r], 16)

    def tile_stats(self, dve, src, i, u):
        for j in range(G):
            dve.bn_stats(one(self.stats, i, u, j), one(src, i, u, j)).then_inc(self.sem("stats_done"), 1)

    def norm(self, rep, src, eps, gain=None, keep=None, turn=True, add_to=None, gate=None, logits=None, load=None,
             ready_stats=True):
        nc, m, sem = self.nc, self.mem, self.sem
        name = f"norm{rep}"
        m.at(self.work_at)
        z = [m.take(G, D) for _ in range(2)]
        zt = [m.take(C, GW) for _ in range(2)] if gate is not None else None
        mean, var, r, tmp = m.take(NT), m.take(NT), m.take(NT), m.take(NT)
        ready, turned, copied, kept = sem("norm_ready", 2), sem("norm_turned", 2), sem("norm_copied", 2), sem("norm_kept", 2)
        lg_mm, lg_read, step, scaled = sem("norm_logits_mm", 2), sem("norm_logits_read", 2), sem("norm_step"), sem("norm_scaled")
        stats_done = sem("stats_done")
        base = self.norm_base
        b = dict(base)
        def B(key):
            return b.get(key, 0)
        I = NG // 2
        with ExitStack() as ctx:
            if turn or gate is not None:
                flip = [ctx.enter_context(nc.psum_tensor(f"{name}_flip{u}", [P, C, 512], F32)) for u in range(2)]
            if gate is not None:
                lg = [ctx.enter_context(nc.psum_tensor(f"{name}_lg{u}", [P, 512], F32)) for u in range(2)]
            block = ctx.enter_context(nc.Block())

            if load is not None:
                @block.sync
                def _(sp):
                    load(sp)

            @block.vector
            def _(dve):
                if not ready_stats:
                    with dve.Fori(0, I) as i:
                        for u in range(2):
                            self.tile_stats(dve, src, i, u)
                    self.stats_count += NT
                dve.wait_ge(stats_done, self.stats_count)
                link = Steps(dve, step, B("step"))
                moments(dve, link, self.stats, mean, var, tmp)
                rsqrt(dve, link, var, eps, r, tmp)
                base["step"] = B("step") + link.n
                with dve.Fori(0, I) as i:
                    for u in range(2):
                        if turn or gate is not None:
                            dve.wait_ge(turned[u], B("turned") + i)
                        if keep is not None or add_to is not None:
                            dve.wait_ge(kept[u], B("kept") + i)
                        for j in range(G):
                            at = bass.ds(i * (2 * G) + (G * u + j), 1)
                            if gain is None:
                                dve.tensor_scalar(z[u][:, j, :], one(src, i, u, j), mean[:, at], r[:, at],
                                                  ALU.subtract, ALU.mult).then_inc(ready[u], 1)
                            else:
                                dve.scalar_tensor_tensor(out=z[u][:, j, :], in0=one(src, i, u, j), scalar=mean[:, at],
                                                         in1=gain[0], op0=ALU.subtract, op1=ALU.mult).then_inc(scaled, 1)
                        if gain is not None:
                            for j in range(G):
                                at = bass.ds(i * (2 * G) + (G * u + j), 1)
                                dve.wait_ge(scaled, B("scaled") + i * (2 * G) + (G * u + j + 1))
                                dve.scalar_tensor_tensor(out=z[u][:, j, :], in0=z[u][:, j, :], scalar=r[:, at],
                                                         in1=gain[1], op0=ALU.mult, op1=ALU.add).then_inc(ready[u], 1)
                        if add_to is not None and u == 1:
                            dve.wait_ge(kept[0], B("kept") + i + 1)
                            self.tile_stats(dve, add_to, i, 0)
                    if add_to is not None:
                        dve.wait_ge(kept[1], B("kept") + i + 1)
                        self.tile_stats(dve, add_to, i, 1)

            if add_to is not None or (gate is not None and turn):
                @block.gpsimd
                def _(pool):
                    with pool.Fori(0, I) as i:
                        for u in range(2):
                            if add_to is not None:
                                pool.wait_ge(ready[u], B("ready") + (i + 1) * G)
                                pool.tensor_tensor(three(add_to, i, u), three(add_to, i, u), z[u], ALU.add).then_inc(kept[u], 1)
                            if gate is not None and turn:
                                pool.wait_ge(copied[u], B("copied") + i + 1)
                                pool.tensor_copy(cols(self.xT, i, u), zt[u]).then_inc(sem("norm_xT", 2)[u], 1)

            if turn or gate is not None:
                @block.tensor
                def _(pe):
                    with pe.Fori(0, I) as i:
                        for u in range(2):
                            pe.wait_ge(copied[u], B("copied") + i)
                            for j in range(G):
                                pe.wait_ge(ready[u], B("ready") + i * G + (j + 1))
                                for c in range(C):
                                    last = pe.transpose(flip[u][:, c, j * P:(j + 1) * P], z[u][:, j, c * P:(c + 1) * P], self.ident)
                            last.then_inc(turned[u], 1)
                            if gate is not None:
                                pe.wait_ge(copied[u], B("copied") + i + 1)
                                pe.wait_ge(lg_read[u], B("lg_read") + i)
                                for j in range(G):
                                    for c in range(C):
                                        last = pe.matmul(lg[u][:, j * E:(j + 1) * E], zt[u][:, c, j * P:(j + 1) * P], gate[:, c, :],
                                                         start=(c == 0), stop=(c == C - 1))
                                last.then_inc(lg_mm[u], 1)

            @block.scalar
            def _(act):
                with act.Fori(0, I) as i:
                    for u in range(2):
                        if turn or gate is not None:
                            act.wait_ge(turned[u], B("turned") + i + 1)
                            if gate is not None:
                                act.wait_ge(lg_mm[u], B("lg_mm") + i)
                                if turn:
                                    act.wait_ge(sem("norm_xT", 2)[u], B("xT") + i)
                                act.activation(zt[u], flip[u][:, :, 0:GW], ACT.Copy).then_inc(copied[u], 1)
                            else:
                                act.activation(cols(self.xT, i, u), flip[u][:, :, 0:GW], ACT.Copy).then_inc(copied[u], 1)
                        if keep is not None:
                            act.wait_ge(ready[u], B("ready") + (i + 1) * G)
                            act.activation(three(keep, i, u), z[u], ACT.Copy).then_inc(kept[u], 1)
                        if gate is not None:
                            act.wait_ge(lg_mm[u], B("lg_mm") + i + 1)
                            act.activation(three(logits, i, u), lg[u][:, 0:G * E].rearrange("p (j e) -> p j e", e=E),
                                           ACT.Copy).then_inc(lg_read[u], 1)
        def add(key, n):
            base[key] = base.get(key, 0) + n
        add("ready", I * G)
        if turn or gate is not None:
            add("turned", I); add("copied", I)
        if keep is not None or add_to is not None:
            add("kept", I)
        if add_to is not None:
            self.stats_count += NT
        if gain is not None:
            add("scaled", NT)
        if gate is not None:
            add("lg_mm", I); add("lg_read", I)
            if turn:
                add("xT", I)

    def rotate(self):
        nc, m, sem = self.nc, self.mem, self.sem
        R = 4
        W = R * S
        I = NB // R // 2
        self.qF = self.xn.rearrange("p a d -> p (a d)")[:, 0:C * N].rearrange("p (c n) -> p c n", c=C)
        m.at(self.early_end)
        self.kF = m.take(C, N)
        m.at(self.work_at)
        prod = [[m.take(2, R, S) for _ in range(2)] for _ in range(2)]
        mm, read, summed = sem("rot_mm", 2), sem("rot_read", 2), sem("rot_summed", 2)
        with ExitStack() as ctx:
            ps = [ctx.enter_context(nc.psum_tensor(f"rot{qk}", [P, 2, 512], F32)) for qk in range(2)]
            block = ctx.enter_context(nc.Block())

            @block.tensor
            def _(pe):
                with pe.Fori(0, 2 * I) as i:
                    for qk in range(2):
                        pe.wait_ge(read[qk], i)
                        for eo in range(2):
                            for c in range(C):
                                last = pe.matmul(ps[qk][:, eo, 0:W], self.wqk0[:, qk, c, eo * P:(eo + 1) * P],
                                                 self.xT[:, c, bass.ds(i * W, W)], start=(c == 0), stop=(c == C - 1))
                        last.then_inc(mm[qk], 1)

            @block.vector
            def _(dve):
                with dve.Fori(0, 2 * I) as i:
                    for qk in range(2):
                        dve.wait_ge(mm[qk], i + 1)
                        dve.wait_ge(summed[qk], i * 2)
                        for eo in range(2):
                            for k, tab in enumerate((self.cos_sin, self.sin_cos)):
                                last = dve.tensor_tensor(prod[qk][k][:, eo], ps[qk][:, eo, 0:W].rearrange("p (r s) -> p r s", s=S),
                                                         spread(tab[:, eo], R), ALU.mult)
                        last.then_inc(read[qk], 1)

            @block.gpsimd
            def _(pool):
                with pool.Fori(0, 2 * I) as i:
                    for qk, dst in enumerate((self.qF, self.kF)):
                        pool.wait_ge(read[qk], i + 1)
                        for k, op in ((0, ALU.subtract), (1, ALU.add)):
                            pool.tensor_tensor(dst[:, k, bass.ds(i * W, W)], prod[qk][k][:, 0].rearrange("p r s -> p (r s)"),
                                               prod[qk][k][:, 1].rearrange("p r s -> p (r s)"), op).then_inc(summed[qk], 1)

    def attention(self):
        nc, m, sem = self.nc, self.mem, self.sem
        H2 = HALF
        VW = HD + 1
        m.at(self.work_at)
        q = [m.take(C, S) for _ in range(2)]
        k2 = [m.take(C, 2, HALF, S) for _ in range(2)]
        x = [m.take(C, S) for _ in range(2)]
        va = [m.take(HEADS, VW) for _ in range(2)]
        on = m.take(HEADS, HD)
        top = m.take(4, H2)
        rsum = m.take(HEADS)
        prob = [m.take(4, H2, S) for _ in range(2)]
        pt = m.take(4, H2, S)
        staged, keyed = sem("x_staged"), sem("qk_staged")
        v_mm, v_read, s_mm, s_read = sem("v_mm"), sem("v_read"), sem("scores_mm"), sem("scores_read")
        exp_done, pt_mm = sem("exp_done"), sem("probs_turned", 2)
        pt_read, pv_mm, o_norm = sem("probs_copied", 2), sem("pv_mm"), sem("o_normed")
        ot_mm, ot_read, preset, step = sem("o_turned"), sem("o_copied"), sem("attn_preset"), sem("attn_step")

        with ExitStack() as ctx:
            sc = ctx.enter_context(nc.psum_tensor("scores", [P, 4, 512], F32))
            tp = [ctx.enter_context(nc.psum_tensor(f"turned_probs{j}", [P, 512], F32)) for j in range(2)]
            pj = ctx.enter_context(nc.psum_tensor("values", [P, 512], F32))
            ov = ctx.enter_context(nc.psum_tensor("out_values", [P, 512], F32))
            block = ctx.enter_context(nc.Block())
            ov_heads = ov[0:S, 0:HEADS * VW].rearrange("p (h w) -> p h w", w=VW)
            ov_turned = ov[:, HEADS * VW:HEADS * VW + C * S].rearrange("p (c s) -> p c s", s=S)
            sc_heads = sc[0:S, :, 0:H2 * S].rearrange("p g (j s) -> p g j s", s=S)

            @block.sync
            def _(sp):
                sp.wait_ge(self.rest_in, 16 * self.rest_count)

            @block.gpsimd
            def _(pool):
                def stage_x(n, u):
                    pool.tensor_copy(x[u], self.xT[:, :, bass.ds(n * S, S)]).then_inc(staged, 1)

                def stage_qk(n, u):
                    pool.tensor_copy(q[u], self.qF[:, :, bass.ds(n * S, S)]).then_inc(keyed, 1)
                    for c in range(C):
                        pool.tensor_tensor(k2[u][:, c].rearrange("p r h s -> p (r h) s"), spread(self.kF[:, c, bass.ds(n * S, S)], 2 * HALF),
                                           inner(self.own_mask.rearrange("p r h -> p (r h)"), S), ALU.mult).then_inc(keyed, 1)

                stage_qk(0, 0)
                stage_x(0, 0)
                stage_qk(1, 1)
                stage_x(1, 1)
                with pool.Fori(0, NB // 2 - 1) as i:
                    for u in range(2):
                        n = i * 2 + u
                        pool.wait_ge(s_mm, n + 1)
                        stage_qk(n + 2, u)
                        pool.wait_ge(v_mm, n + 1)
                        stage_x(n + 2, u)

            @block.tensor
            def _(pe):
                def values(n, u):
                    pe.wait_ge(staged, n + 1)
                    pe.wait_ge(v_read, n)
                    for c in range(C):
                        last = pe.matmul(pj[0:S, 0:D], x[u][:, c, :], self.wv0[:, c, :], start=(c == 0), stop=(c == C - 1))
                    last.then_inc(v_mm, 1)

                def scores(n, u):
                    pe.wait_ge(keyed, n * 3 + 3)
                    pe.wait_ge(s_read, n)
                    for c in range(C):
                        for r in range(2):
                            last = pe.matmul(sc[0:S, 2 * c + r, 0:HALF * S], q[u][:, c, :],
                                             k2[u][:, c, r, :, :].rearrange("p a s -> p (a s)"),
                                             start=True, stop=True)
                    last.then_inc(s_mm, 1)

                def turn_out(n):
                    pe.wait_ge(o_norm, n + 1)
                    for c in range(C):
                        last = pe.transpose(ov_turned[:, c, :], on[0:S, c * 8:(c + 1) * 8, :].rearrange("p h w -> p (h w)"),
                                            self.ident[0:S, 0:S])
                    last.then_inc(ot_mm, 1)

                def turn_probs(n, i, u, groups):
                    for g in groups:
                        pe.wait_ge(pt_read[g % 2], n * 2 + g // 2)
                        for j in range(H2):
                            last = pe.transpose(tp[g % 2][0:S, j * S:(j + 1) * S], prob[u][0:S, g, j, :], self.ident[0:S, 0:S])
                        last.then_inc(pt_mm[u], 1)

                def step_of(n, i, u, ahead_s, ahead_v):
                    if ahead_s:
                        scores(n + 1, 1 - u)
                    pe.wait_ge(exp_done, n + 1)
                    turn_probs(n, i, u, (0, 1))
                    turn_out(n - 1)
                    turn_probs(n, i, u, (2, 3))
                    if ahead_v:
                        values(n + 2, u)
                    pe.wait_ge(pt_read[0], n * 2 + 2)
                    pe.wait_ge(pt_read[1], n * 2 + 2)
                    pe.wait_ge(v_read, n + 1)
                    pe.wait_ge(ot_read, n + 1)
                    for g in range(4):
                        for j in range(H2):
                            head = HALF * g + j
                            last = pe.matmul(ov_heads[:, head, :], pt[0:S, g, j, :], va[u][0:S, head, :], start=True, stop=True)
                    last.then_inc(pv_mm, 1)

                scores(0, 0)
                values(0, 0)
                values(1, 1)
                pe.wait_ge(preset, 3)
                with pe.Fori(0, NB // 2 - 1) as i:
                    for u in range(2):
                        step_of(i * 2 + u, i, u, True, True)
                step_of(NB - 2, NB // 2 - 1, 0, True, False)
                step_of(NB - 1, NB // 2 - 1, 1, False, False)
                turn_out(NB - 1)

            @block.vector
            def _(dve):
                dve.memset(on[0:S], 0.0).then_inc(preset, 1)
                for u in range(2):
                    dve.memset(va[u][0:S], 1.0).then_inc(preset, 1)
                dve.wait_ge(s_mm, 1)
                dve.tensor_reduce(top[0:S], sc_heads, AX_X, ALU.max).then_inc(step, 1)
                dve.wait_ge(step, 1)
                dve.tensor_tensor(prob[0][0:S], sc_heads, inner(top[0:S], S), ALU.subtract).then_inc(s_read, 1)

                def step_of(n, i, u, ahead):
                    if ahead:
                        dve.wait_ge(s_mm, n + 2)
                        dve.tensor_reduce(top[0:S], sc_heads, AX_X, ALU.max).then_inc(step, 1)
                        dve.wait_ge(step, n * 2 + 2)
                        dve.wait_ge(pt_mm[1 - u], (i + u) * 4)
                        dve.tensor_tensor(prob[1 - u][0:S], sc_heads, inner(top[0:S], S), ALU.subtract).then_inc(s_read, 1)
                    dve.wait_ge(pv_mm, n + 1)
                    dve.reciprocal(rsum[0:S], ov_heads[:, :, HD]).then_inc(step, 1)
                    dve.wait_ge(step, n * 2 + (3 if ahead else 2))
                    dve.wait_ge(ot_mm, n + 1)
                    dve.tensor_tensor(on[0:S], ov_heads[:, :, 0:HD], inner(rsum[0:S], HD), ALU.mult).then_inc(o_norm, 1)

                with dve.Fori(0, NB // 2 - 1) as i:
                    for u in range(2):
                        step_of(i * 2 + u, i, u, True)
                step_of(NB - 2, NB // 2 - 1, 0, True)
                step_of(NB - 1, NB // 2 - 1, 1, False)

            @block.scalar
            def _(act):
                def exp(n, u):
                    act.wait_ge(s_read, n + 1)
                    act.activation(prob[u][0:S], prob[u][0:S], ACT.Exp, scale=1.0 / float(HD) ** 0.5).then_inc(exp_done, 1)

                def copy_v(n, u):
                    act.wait_ge(v_mm, n + 1)
                    act.activation(va[u][0:S, :, 0:HD], pj[0:S, 0:D].rearrange("p (h w) -> p h w", w=HD), ACT.Copy).then_inc(v_read, 1)

                def copy_out(n):
                    act.wait_ge(ot_mm, n + 2)
                    act.activation(self.oT[:, :, bass.ds(n * S + OPAD, S)], ov_turned, ACT.Copy).then_inc(ot_read, 1)

                def step_of(n, i, u, ahead_s, ahead_v):
                    for g in range(4):
                        if g == 2:
                            copy_out(n - 1)
                        act.wait_ge(pt_mm[u], i * 4 + g + 1)
                        if g == 0:
                            act.wait_ge(pv_mm, n)
                        act.activation(pt[0:S, g], tp[g % 2][0:S, 0:H2 * S].rearrange("p (j s) -> p j s", s=S), ACT.Copy).then_inc(pt_read[g % 2], 1)
                    if ahead_s:
                        exp(n + 1, 1 - u)
                    if ahead_v:
                        act.wait_ge(pv_mm, n + 1)
                        copy_v(n + 2, u)

                act.wait_ge(preset, 3)
                copy_v(0, 0)
                copy_v(1, 1)
                exp(0, 0)
                with act.Fori(0, NB // 2 - 1) as i:
                    for u in range(2):
                        step_of(i * 2 + u, i, u, True, True)
                step_of(NB - 2, NB // 2 - 1, 0, True, False)
                step_of(NB - 1, NB // 2 - 1, 1, False, False)
                copy_out(NB - 1)

    def project(self, rep, w, bias, acc, load=None):
        nc, m, sem = self.nc, self.mem, self.sem
        m.at(self.work_at)
        o = [m.take(C, GW) for _ in range(2)]
        staged, biased, mm, added = sem("o_staged", 2), sem("acc_biased", 2), sem("wo_mm", 2), sem("wo_added", 2)
        I = NG // 2
        B = rep * I
        with ExitStack() as ctx:
            ps = [ctx.enter_context(nc.psum_tensor(f"wo{rep}_{u}", [P, 1024], F32)) for u in range(2)]
            block = ctx.enter_context(nc.Block())

            if load is not None:
                @block.sync
                def _(sp):
                    load(sp)

            @block.gpsimd
            def _(pool):
                with pool.Fori(0, I) as i:
                    for u in range(2):
                        pool.tensor_tensor(three(acc, i, u), three(acc, i, u), spread(bias, G), ALU.add).then_inc(biased[u], 1)

            @block.scalar
            def _(act):
                with act.Fori(0, I) as i:
                    for u in range(2):
                        act.wait_ge(mm[u], B + i)
                        act.activation(o[u], self.oT[:, :, bass.ds(i * (2 * GW) + (OPAD + GW * u), GW)], ACT.Copy).then_inc(staged[u], 1)

            @block.tensor
            def _(pe):
                with pe.Fori(0, I) as i:
                    for u in range(2):
                        pe.wait_ge(staged[u], B + i + 1)
                        pe.wait_ge(added[u], B + i)
                        for j in range(G):
                            for c in range(C):
                                last = pe.matmul(ps[u][:, j * D:(j + 1) * D], o[u][:, c, j * P:(j + 1) * P], w[:, c, :],
                                                 start=(c == 0), stop=(c == C - 1))
                        last.then_inc(mm[u], 1)

            @block.vector
            def _(dve):
                with dve.Fori(0, I) as i:
                    for u in range(2):
                        dve.wait_ge(mm[u], B + i + 1)
                        dve.wait_ge(biased[u], B + i + 1)
                        dve.tensor_tensor(three(acc, i, u), ps[u][:, 0:G * D].rearrange("p (j d) -> p j d", d=D),
                                          three(acc, i, u), ALU.add).then_inc(added[u], 1)
                        dve.wait_ge(added[u], B + i + 1)
                        self.tile_stats(dve, acc, i, u)
        self.stats_count += NT

    def choose(self, scores, first, second, best, tmp, dve, link):
        rank = self.rank.unsqueeze(1).to_broadcast([P, NT, E])
        for k, hot in enumerate((first, second)):
            link(dve.tensor_reduce(best[k], scores, AX_X, ALU.max))
            link(dve.tensor_tensor(tmp, scores, inner(best[k], E), ALU.is_equal))
            link(dve.tensor_tensor(tmp, tmp, rank, ALU.mult))
            link(dve.tensor_reduce(self.top_rank, tmp, AX_X, ALU.max))
            link(dve.tensor_tensor(hot, inner(self.top_rank, E), rank, ALU.is_equal))
            if k == 0:
                link(dve.tensor_scalar(tmp, hot, -BIG, None, ALU.mult))
                link(dve.tensor_tensor(scores, scores, tmp, ALU.add))

    def route_first(self):
        nc, m, sem = self.nc, self.mem, self.sem
        m.at(self.work_at)
        m.take(NT, E + 1)
        self.gates = m.take(NT, E + 1)
        kept = m.pos
        tmp, first, second = m.take(NT, E), m.take(NT, E), m.take(NT, E)
        best = [m.take(NT) for _ in range(2)]
        total = m.take(NT)
        self.route_end = kept
        exped, step, done = sem("route_exp"), sem("route_step"), sem("gates_ready")
        lg = self.lg
        with nc.Block() as block:
            @block.scalar
            def _(act):
                act.activation(lg, lg, ACT.Exp, scale=-1.0).then_inc(exped, 1)

            @block.vector
            def _(dve):
                link = Steps(dve, step, 0)
                link(dve.memset(self.gates, 1.0))
                dve.wait_ge(exped, 1)
                link(dve.tensor_scalar(lg, lg, 1.0, None, ALU.add))
                link(dve.reciprocal(lg, lg))
                link(dve.tensor_scalar(lg, lg, self.route_scale[:, 0:1], None, ALU.mult))
                self.choose(lg, first, second, best, tmp, dve, link)
                link(dve.tensor_tensor(total, best[0], best[1], ALU.add))
                link(dve.reciprocal(total, total))
                for b, hot in zip(best, (first, second)):
                    link(dve.tensor_tensor(b, b, total, ALU.mult))
                    link(dve.tensor_tensor(hot, hot, inner(b, E), ALU.mult))
                link(dve.tensor_tensor(self.gates[:, :, 0:E], first, second, ALU.add))

    def experts(self):
        nc, m, sem = self.nc, self.mem, self.sem
        X = E + 1
        R = 3
        m.at(self.route_end)
        hid = [m.take(GW) for _ in range(R)]
        gs = [m.take(G, X) for _ in range(2)]
        gt = [m.take(GW) for _ in range(2)]
        e2_b = m.take(D)
        b_in, stats_done = sem("e2_b_in"), sem("stats_done")
        gs_ready, gt_mm, gt_ready = sem("gate_staged", 2), sem("gate_turned", 2), sem("gate_copied", 2)
        up_mm, gelu, po_mm, po_read = sem("up_mm", R), sem("gelu_done", R), sem("down_mm", G), sem("down_read", G)
        I = NG // 2
        with ExitStack() as ctx:
            up = [ctx.enter_context(nc.psum_tensor(f"up{r}", [P, 512], F32)) for r in range(R)]
            po = [ctx.enter_context(nc.psum_tensor(f"down{j}", [P, 512], F32)) for j in range(G)]
            tg = ctx.enter_context(nc.psum_tensor("turned_gate", [P, 512], F32))
            block = ctx.enter_context(nc.Block())

            @block.sync
            def _(sp):
                sp.dma_start(e2_b[0:X], self.t["e2_b"]).then_inc(b_in, 16)

            @block.tensor
            def _(pe):
                pe.wait_ge(b_in, 16)
                with pe.Fori(0, I) as i:
                    for u in range(2):
                        it = i * 2 + u

                        def rise(e):
                            r = e % R
                            pe.wait_ge(gelu[r], it * R + e // R)
                            for c in range(C):
                                last = pe.matmul(up[r][:, 0:GW], self.e1[:, e, c, :], self.xT[:, c, bass.ds(i * (2 * GW) + GW * u, GW)],
                                                 start=(c == 0), stop=(c == C - 1))
                            last.then_inc(up_mm[r], 1)

                        def fall(e):
                            r = e % R
                            pe.wait_ge(gelu[r], it * R + e // R + 1)
                            for j in range(G):
                                pe.wait_ge(po_read[j], it * (X + 1) + e + 1)
                                last = pe.matmul(po[j][:, 0:D], hid[r][:, j * P:(j + 1) * P], self.e2[:, e, :], start=True, stop=True)
                                last.then_inc(po_mm[j], 1)

                        rise(0)
                        pe.wait_ge(gs_ready[u], i + 1)
                        if u == 0:
                            pe.wait_ge(gt_ready[1], i)
                        else:
                            pe.wait_ge(gt_ready[0], i + 1)
                        for j in range(G):
                            last = pe.transpose(tg[0:X, j * P:(j + 1) * P], gs[u][:, j, :], self.ident)
                        last.then_inc(gt_mm[u], 1)
                        rise(1)
                        pe.wait_ge(gt_ready[u], i + 1)
                        for j in range(G):
                            pe.wait_ge(po_read[j], it * (X + 1))
                            last = pe.matmul(po[j][:, 0:D], gt[u][0:X, j * P:(j + 1) * P], e2_b[0:X, :], start=True, stop=True)
                            last.then_inc(po_mm[j], 1)
                        for e in range(X):
                            fall(e)
                            if e + 2 < X:
                                rise(e + 2)

            @block.scalar
            def _(act):
                with act.Fori(0, I) as i:
                    for u in range(2):
                        it = i * 2 + u
                        for e in range(X):
                            r = e % R
                            act.wait_ge(up_mm[r], it * R + e // R + 1)
                            act.wait_ge(po_mm[G - 1], it * (X + 1) + (e - R + 2 if e >= R else 0))
                            act.activation(hid[r], up[r][:, 0:GW], ACT.Gelu, bias=self.e1_b[:, e:e + 1]).then_inc(gelu[r], 1)
                            if e == 0:
                                act.wait_ge(gt_mm[u], i + 1)
                                act.activation(gt[u][0:X], tg[0:X, 0:GW], ACT.Copy).then_inc(gt_ready[u], 1)

            @block.vector
            def _(dve):
                with dve.Fori(0, I) as i:
                    for u in range(2):
                        it = i * 2 + u
                        dve.tensor_copy(gs[u], self.gates[:, bass.ds(i * (2 * G) + G * u, G), :]).then_inc(gs_ready[u], 1)
                        dve.wait_ge(gs_ready[u], i + 1)
                        for r in range(X + 1):
                            for j in range(G):
                                dve.wait_ge(po_mm[j], it * (X + 1) + r + 1)
                                acc = one(self.h, i, u, j)
                                if r == 0:
                                    ins = dve.tensor_tensor(acc, po[j][:, 0:D], acc, ALU.add)
                                else:
                                    dve.wait_ge(po_read[j], it * (X + 1) + r)
                                    ins = dve.scalar_tensor_tensor(out=acc, in0=po[j][:, 0:D], scalar=gs[u][:, j, r - 1:r],
                                                                   in1=acc, op0=ALU.mult, op1=ALU.add)
                                ins.then_inc(po_read[j], 1)
                        for j in range(G):
                            dve.wait_ge(po_read[j], (it + 1) * (X + 1))
                            dve.bn_stats(one(self.stats, i, u, j), one(self.h, i, u, j)).then_inc(stats_done, 1)
        self.stats_count += NT

    def linear_attention(self):
        nc, m, sem = self.nc, self.mem, self.sem
        NP = NB // 2
        QK = 2 * D
        m.at(self.early_end)
        qb = m.take(2, QK)
        kvm = m.take(2, C, P)
        qT = m.take(C, 2, S)
        x = [m.take(C, PAIR) for _ in range(2)]
        m.at(self.work_at)
        el = [m.take(2, QK) for _ in range(2)]
        ex = [m.take(2, QK) for _ in range(2)]
        vb = [m.take(2, D) for _ in range(2)]
        nrm, var, tmp = m.take(2, 2 * HEADS), m.take(2, 2 * HEADS), m.take(2, 2 * HEADS)
        staged, pj_mm, qk_read, v_read = sem("la_x_staged"), sem("la_proj_mm"), sem("la_qk_read"), sem("la_v_read")
        e_done, r_done, el_done, sq_done = sem("la_exp"), sem("la_relu"), sem("la_elu"), sem("la_square")
        rn_done, n_done, tkv_mm, kv_read = sem("la_norms"), sem("la_unit"), sem("la_kv_mm"), sem("la_kv_read")
        qT_read, c_mm, c_read, step, zeroed = sem("la_q_copied"), sem("la_ctx_mm"), sem("la_ctx_copied"), sem("la_step"), sem("la_zeroed")
        per = 2 * RSQRT_STEPS

        with ExitStack() as ctx:
            pq = [ctx.enter_context(nc.psum_tensor(f"la_qk{u}", [P, 2, 512], F32)) for u in range(2)]
            pv = ctx.enter_context(nc.psum_tensor("la_v", [P, 2, D], F32))
            pkv = ctx.enter_context(nc.psum_tensor("la_kv", [P, 2, C, P], F32))
            pt = ctx.enter_context(nc.psum_tensor("la_qT", [P, 512], F32))
            pc = ctx.enter_context(nc.psum_tensor("la_ctx", [P, 512], F32))
            block = ctx.enter_context(nc.Block())

            @block.gpsimd
            def _(pool):
                def stage(p, u):
                    pool.tensor_copy(x[u], self.xT[:, :, bass.ds(p * PAIR, PAIR)]).then_inc(staged, 1)

                pool.memset(el[1][0:S], 0.0).then_inc(zeroed, 1)
                pool.memset(vb[1][0:S], 0.0).then_inc(zeroed, 1)
                stage(0, 0)
                stage(1, 1)
                with pool.Fori(0, NP // 2) as i:
                    for u in range(2):
                        p = i * 2 + u
                        pool.wait_ge(pj_mm, p + 1)
                        stage(p + 2, u)
                        pool.wait_ge(rn_done, p + 1)
                        heads = el[u][0:S].rearrange("p b (h w) -> p (b h) w", w=HD)
                        pool.tensor_tensor(heads, heads, inner(nrm[0:S].rearrange("p b h -> p (b h)"), HD), ALU.mult).then_inc(n_done, 1)

            @block.tensor
            def _(pe):
                def proj(p, u):
                    pe.wait_ge(staged, p + 1)
                    for b in range(2):
                        for c in range(C):
                            pe.matmul(pq[u][0:S, b, :], x[u][:, c, b * S:(b + 1) * S], self.wqk1[:, c, :], start=(c == 0), stop=(c == C - 1))
                    pe.wait_ge(v_read, p)
                    for b in range(2):
                        for c in range(C):
                            last = pe.matmul(pv[0:S, b, :], x[u][:, c, b * S:(b + 1) * S], self.wv1[:, c, :], start=(c == 0), stop=(c == C - 1))
                    last.then_inc(pj_mm, 1)

                def turn_kv(p, u):
                    pe.wait_ge(n_done, p + 1)
                    pe.wait_ge(v_read, p + 1)
                    for c in range(C):
                        for b in range(2):
                            pe.transpose(pt[:, (c * 2 + b) * S:(c * 2 + b + 1) * S], el[u][0:S, b, c * P:(c + 1) * P], self.ident[0:S, 0:S])
                    for b in range(2):
                        for c in range(C):
                            last = pe.matmul(pkv[:, b, c, :], el[u][0:S, b, D + c * P:D + (c + 1) * P], vb[u][0:S, b, c * P:(c + 1) * P],
                                             start=True, stop=True)
                    last.then_inc(tkv_mm, 1)

                def context(p):
                    pe.wait_ge(kv_read, p + 2)
                    pe.wait_ge(qT_read, p + 2)
                    pe.wait_ge(c_read, p + 1)
                    for c in range(C):
                        for b in range(2):
                            last = pe.matmul(pc[:, (c * 2 + b) * S:(c * 2 + b + 1) * S], kvm[:, b, c, :], qT[:, c, b, :], start=True, stop=True)
                    last.then_inc(c_mm, 1)

                proj(0, 0)
                proj(1, 1)
                pe.wait_ge(zeroed, 2)
                with pe.Fori(0, NP // 2) as i:
                    for u in range(2):
                        p = i * 2 + u
                        turn_kv(p - 1, 1 - u)
                        pe.wait_ge(qk_read, p + 1)
                        proj(p + 2, u)
                        context(p - 1)
                turn_kv(NP - 1, 1)
                context(NP - 1)

            @block.vector
            def _(dve):
                def bias(p, u):
                    dve.wait_ge(pj_mm, p + 1)
                    dve.wait_ge(e_done, p)
                    dve.wait_ge(r_done, p)
                    dve.tensor_tensor(qb[0:S], pq[u][0:S], spread(self.bqk1, 2)[0:S], ALU.add).then_inc(qk_read, 1)
                    dve.wait_ge(tkv_mm, p)
                    dve.tensor_tensor(vb[u][0:S], pv[0:S], spread(self.bv1, 2)[0:S], ALU.add).then_inc(v_read, 1)
                    dve.wait_ge(qk_read, p + 1)
                    dve.tensor_scalar(el[u][0:S], qb[0:S], 0.0, -1.0, ALU.max, ALU.add).then_inc(r_done, 1)

                def mask():
                    dve.tensor_tensor(kvm, pkv[:, :, :, :], self.head_mask.unsqueeze(1).unsqueeze(1).to_broadcast([P, 2, C, P]), ALU.mult).then_inc(kv_read, 1)

                dve.wait_ge(zeroed, 2)
                bias(0, 0)
                with dve.Fori(0, NP // 2) as i:
                    link = Steps(dve, step, i * per)
                    for u in range(2):
                        p = i * 2 + u
                        dve.wait_ge(e_done, p + 1)
                        dve.wait_ge(r_done, p + 1)
                        dve.scalar_tensor_tensor(out=el[u][0:S].rearrange("p b d -> p (b d)"), in0=ex[u][0:S].rearrange("p b d -> p (b d)"),
                                                 scalar=1.0, in1=el[u][0:S].rearrange("p b d -> p (b d)"), op0=ALU.min, op1=ALU.add).then_inc(el_done, 1)
                        bias(p + 1, 1 - u)
                        dve.wait_ge(sq_done, p + 1)
                        dve.wait_ge(n_done, p)
                        link(dve.tensor_reduce(var[0:S], ex[u][0:S].rearrange("p b (h w) -> p b h w", w=HD), AX_X, ALU.add))
                        rsqrt(dve, link, var[0:S], 0.0, nrm[0:S], tmp[0:S], rn_done)
                        dve.wait_ge(tkv_mm, p + 1)
                        dve.wait_ge(c_mm, p)
                        mask()
                    assert link.n == per, (link.n, per)
                dve.wait_ge(tkv_mm, NP + 1)
                dve.wait_ge(c_mm, NP)
                mask()

            @block.scalar
            def _(act):
                def exp(p, u):
                    act.wait_ge(qk_read, p + 1)
                    act.activation(ex[u][0:S], qb[0:S], ACT.Exp).then_inc(e_done, 1)

                def copy_q(p):
                    act.wait_ge(tkv_mm, p + 2)
                    act.wait_ge(c_mm, p + 1)
                    act.activation(qT.rearrange("p c b s -> p (c b s)"), pt[:, 0:C * PAIR], ACT.Copy).then_inc(qT_read, 1)

                def copy_out(p):
                    act.wait_ge(c_mm, p + 2)
                    act.activation(self.oT[:, :, bass.ds(p * PAIR + OPAD, PAIR)], pc[:, 0:C * PAIR].rearrange("p (c s) -> p c s", c=C),
                                   ACT.Copy).then_inc(c_read, 1)

                exp(0, 0)
                with act.Fori(0, NP // 2) as i:
                    for u in range(2):
                        p = i * 2 + u
                        act.wait_ge(el_done, p + 1)
                        act.activation(ex[u][0:S], el[u][0:S], ACT.Square).then_inc(sq_done, 1)
                        copy_q(p - 1)
                        act.wait_ge(rn_done, p)
                        exp(p + 1, 1 - u)
                        copy_out(p - 1)
                copy_q(NP - 1)
                copy_out(NP - 1)

    def feed_forward(self):
        nc, m, sem = self.nc, self.mem, self.sem
        R = 4
        m.at(self.work_at)
        hid = [m.take(KF, GW) for _ in range(2)]
        up_mm, gelu, down_mm, down_read, biased = sem("ff_up_mm", R), sem("ff_gelu", R), sem("ff_down_mm", G), sem("ff_down_read", G), sem("ff_biased")
        stats_done = sem("stats_done")
        I = NG // 2
        with ExitStack() as ctx:
            up = [ctx.enter_context(nc.psum_tensor(f"ff_up{r}", [P, 512], F32)) for r in range(R)]
            po = [ctx.enter_context(nc.psum_tensor(f"ff_down{j}", [P, 512], F32)) for j in range(G)]
            block = ctx.enter_context(nc.Block())

            @block.gpsimd
            def _(pool):
                with pool.Fori(0, I) as i:
                    for u in range(2):
                        pool.tensor_tensor(three(self.xn, i, u), three(self.xn, i, u), spread(self.f2_b, G), ALU.add).then_inc(biased, 1)

            @block.tensor
            def _(pe):
                with pe.Fori(0, I) as i:
                    for u in range(2):
                        it = i * 2 + u
                        for k in range(KF):
                            pe.wait_ge(gelu[k % R], it * (KF // R) + k // R)
                            for c in range(C):
                                last = pe.matmul(up[k % R][:, 0:GW], self.f1[:, c, k * P:(k + 1) * P],
                                                 self.xT[:, c, bass.ds(i * (2 * GW) + GW * u, GW)], start=(c == 0), stop=(c == C - 1))
                            last.then_inc(up_mm[k % R], 1)
                        for j in range(G):
                            pe.wait_ge(down_read[j], it)
                            for k in range(KF):
                                if j == 0:
                                    pe.wait_ge(gelu[k % R], it * (KF // R) + k // R + 1)
                                last = pe.matmul(po[j][:, 0:D], hid[u][:, k, j * P:(j + 1) * P], self.f2[:, k, :],
                                                 start=(k == 0), stop=(k == KF - 1))
                            last.then_inc(down_mm[j], 1)

            @block.scalar
            def _(act):
                with act.Fori(0, I) as i:
                    for u in range(2):
                        it = i * 2 + u
                        for k in range(KF):
                            act.wait_ge(up_mm[k % R], it * (KF // R) + k // R + 1)
                            act.activation(hid[u][:, k, :], up[k % R][:, 0:GW], ACT.Gelu, bias=self.f1_b[:, k:k + 1]).then_inc(gelu[k % R], 1)

            @block.vector
            def _(dve):
                with dve.Fori(0, I) as i:
                    for u in range(2):
                        it = i * 2 + u
                        dve.wait_ge(biased, it + 1)
                        for j in range(G):
                            dve.wait_ge(down_mm[j], it + 1)
                            acc = one(self.xn, i, u, j)
                            dve.tensor_tensor(acc, po[j][:, 0:D], acc, ALU.add).then_inc(down_read[j], 1)
                        for j in range(G):
                            dve.wait_ge(down_read[j], it + 1)
                            dve.bn_stats(one(self.stats, i, u, j), one(self.xn, i, u, j)).then_inc(stats_done, 1)
        self.stats_count += NT

    def route_second(self):
        nc, m, sem, t = self.nc, self.mem, self.sem, self.t
        m.at(self.keep_at)
        self.source, self.target = m.take(XBLK).bitcast(U32), m.take(XBLK).bitcast(U32)
        self.weight = [m.take(NT) for _ in range(2)]
        self.owner = m.take(XBLK).bitcast(U32)
        m.at(self.route_at)
        tmp, first, second, place = m.take(NT, E), m.take(NT, E), m.take(NT, E), m.take(NT, E)
        total, cnt, blocks, base, fin = m.take(NT), m.take(E), m.take(E), m.take(E), m.take(E)
        over, before, past = m.take(E, NT), m.take(E, E), m.take(XBLK, E)
        own = m.take(XBLK)
        hits = m.take(NT * E // 2).bitcast(mybir.dt.bfloat16).rearrange("p (a e) -> p a e", e=E)
        tri = m.take(P // 2).bitcast(mybir.dt.bfloat16)
        ones = m.take(P // 2).bitcast(mybir.dt.bfloat16)
        consts = {"tri": m.take(P), "valid": m.take(NT), "steps": m.take(NT), "lower": m.take(E, E), "blocks": m.take(XBLK),
                  "places": m.take(P), "row": m.take(2), "tile": m.take(NT)}
        slot, at, blk, match = m.take(NT), m.take(NT), m.take(NT), m.take(NT, XBLK)
        at_hot = [m.take(NT * P // 2).bitcast(mybir.dt.bfloat16).rearrange("p (a n) -> p a n", n=P) for _ in range(2)]
        rows = [m.take(NT * XBLK).bitcast(mybir.dt.bfloat16).rearrange("p (a g b) -> p a g b", g=2, b=XBLK) for _ in range(2)]
        row = m.take(XBLK)
        c_in, exped, step = sem("route_consts_in"), sem("route2_exp"), sem("route2_step")
        hit, ranked, hot_ready, table_mm = sem("hits_ready"), sem("ranks_mm"), sem("slot_rows_ready"), sem("slot_table_mm")
        xn_out = sem("xn_in_dram")
        self.xn_rows = self.dram("xn_rows", [NT * P, D])
        lg = self.lg
        with ExitStack() as ctx:
            rk = ctx.enter_context(nc.psum_tensor("ranks", [P, NT, E], F32))
            ct = ctx.enter_context(nc.psum_tensor("counts", [P, 512], F32))
            table = ctx.enter_context(nc.psum_tensor("slot_table", [P, 2, XBLK], F32))
            block = ctx.enter_context(nc.Block())

            @block.sync
            def _(sp):
                for name, view in consts.items():
                    sp.dma_start(view, t["r_" + name]).then_inc(c_in, 16)
                sp.dma_start(self.xn_rows.rearrange("(a p) d -> p a d", p=P), self.xn).then_inc(xn_out, 16)
                sp.wait_ge(xn_out, 16)

            @block.scalar
            def _(act):
                act.wait_ge(step, 2)
                act.activation(lg, lg, ACT.Exp).then_inc(exped, 1)

            @block.vector
            def _(dve):
                link = Steps(dve, step, 0)
                link(dve.tensor_reduce(total, lg, AX_X, ALU.max))
                link(dve.tensor_tensor(lg, lg, inner(total, E), ALU.subtract))
                dve.wait_ge(exped, 1)
                link(dve.tensor_reduce(total, lg, AX_X, ALU.add))
                link(dve.reciprocal(total, total))
                link(dve.tensor_tensor(lg, lg, inner(total, E), ALU.mult))
                self.choose(lg, first, second, self.weight, tmp, dve, link)
                link(dve.tensor_tensor(total, self.weight[0], self.weight[1], ALU.add))
                link(dve.tensor_scalar(total, total, 1e-8, None, ALU.add))
                link(dve.reciprocal(total, total))
                for w in self.weight:
                    link(dve.tensor_tensor(w, w, total, ALU.mult))
                dve.wait_ge(c_in, 16 * len(consts))
                link(dve.tensor_tensor(tmp, first, second, ALU.add))
                link(dve.tensor_copy(tri, consts["tri"]))
                link(dve.memset(ones, 1.0))
                dve.tensor_tensor(hits, tmp, inner(consts["valid"], E), ALU.mult).then_inc(hit, 1)
                dve.wait_ge(ranked, 1)
                link(dve.tensor_copy(cnt, ct[:, 0:E]))
                link(dve.tensor_tensor(over, inner(cnt, NT), spread(consts["steps"], E), ALU.is_gt))
                link(dve.tensor_reduce(blocks, over, AX_X, ALU.add))
                link(dve.tensor_tensor(before, consts["lower"], spread(blocks, E), ALU.mult))
                link(dve.tensor_reduce(base, before, AX_X, ALU.add))
                link(dve.tensor_tensor(fin, base, blocks, ALU.add))
                link(dve.tensor_tensor(past, inner(consts["blocks"], E), spread(fin, XBLK), ALU.is_ge))
                link(dve.tensor_reduce(own, past, AX_X, ALU.add))
                link(dve.tensor_scalar(self.owner, own, float(E - 1), None, ALU.min))
                link(dve.tensor_scalar(base, base, float(P), None, ALU.mult))
                link(dve.tensor_tensor(place, rk[:, :, :], spread(base, NT), ALU.add))
                for k, hot in enumerate((first, second)):
                    link(dve.tensor_tensor(tmp, place, hot, ALU.mult))
                    link(dve.tensor_reduce(slot, tmp, AX_X, ALU.add))
                    link(dve.tensor_copy(at.bitcast(I32), slot))
                    link(dve.tensor_scalar(at.bitcast(I32), at.bitcast(I32), P - 1, None, ALU.bitwise_and))
                    link(dve.tensor_copy(at, at.bitcast(I32)))
                    link(dve.tensor_tensor(blk, slot, at, ALU.subtract))
                    link(dve.tensor_scalar(blk, blk, 1.0 / P, 1.0, ALU.mult, ALU.add))
                    link(dve.tensor_tensor(blk, blk, consts["valid"], ALU.mult))
                    link(dve.tensor_scalar(blk, blk, -1.0, None, ALU.add))
                    link(dve.tensor_tensor(match, inner(blk, XBLK), spread(consts["blocks"], NT), ALU.is_equal))
                    dve.tensor_scalar(rows[k][:, :, 0, :], match, consts["row"][:, k:k + 1], None, ALU.mult).then_inc(hot_ready, 1)
                    dve.tensor_tensor(rows[k][:, :, 1, :], match, inner(consts["tile"], XBLK), ALU.mult).then_inc(hot_ready, 1)
                    dve.tensor_tensor(at_hot[k], inner(at, P), spread(consts["places"], NT), ALU.is_equal).then_inc(hot_ready, 1)
                    dve.wait_ge(hot_ready, 3 * k + 3)
                dve.wait_ge(table_mm, 1)
                link(dve.tensor_copy(row, table[:, 0, :]))
                link(dve.scalar_tensor_tensor(out=row, in0=table[:, 1, :], scalar=2.0 * P, in1=row, op0=ALU.mult, op1=ALU.add))
                link(dve.tensor_copy(self.target, row))
                link(dve.tensor_scalar(row, row, -1.0, 0.0, ALU.add, ALU.max))
                link(dve.tensor_copy(self.source, row))
                link(dve.tensor_scalar(self.source, self.source, 1, None, ALU.logical_shift_right))

            @block.tensor
            def _(pe):
                pe.wait_ge(hit, 1)
                pe.matmul(rk[:, :, :], tri, hits, start=True, stop=False)
                for a in range(1, NT):
                    pe.matmul(rk[:, a:, :], ones, hits[:, 0:NT - a, :], start=False, stop=(a == NT - 1))
                for a in range(NT):
                    last = pe.matmul(ct[:, 0:E], ones, hits[:, a, :], start=(a == 0), stop=(a == NT - 1))
                last.then_inc(ranked, 1)
                for k in range(2):
                    pe.wait_ge(hot_ready, 3 * k + 3)
                    for a in range(NT):
                        last = pe.matmul(table[:, :, :], at_hot[k][:, a, :], rows[k][:, a], start=(k + a == 0), stop=(k == 1 and a == NT - 1))
                last.then_inc(table_mm, 1)

    def routed(self):
        nc, m, sem, t = self.nc, self.mem, self.sem, self.t
        m.at(self.route_at)
        w2_b = m.take(E, D)
        w1_b = m.take(E * KF)
        xg = [m.take(D) for _ in range(2)]
        xT = [m.take(C, P) for _ in range(2)]
        ws = [m.take(C, FF) for _ in range(2)]
        hT = [m.take(KF, P) for _ in range(2)]
        y = [m.take(D) for _ in range(2)]
        b_in, xg_in, tx_mm, xt_read = sem("moe_bias_in"), sem("slot_rows_in", 2), sem("slot_rows_turned"), sem("slot_rows_copied")
        ws_ready, up_mm, gl = sem("moe_w1_staged"), sem("moe_up_mm"), sem("moe_gelu", 2)
        down_mm, y_read, stored = sem("moe_down_mm", 2), sem("moe_down_read"), sem("choices_stored", 2)
        self.choices = self.dram("choices", [1 + 2 * NT * P, D])
        HK = KF // 2
        with ExitStack() as ctx:
            px = ctx.enter_context(nc.psum_tensor("moe_xT", [P, 512], F32))
            p1 = [[ctx.enter_context(nc.psum_tensor(f"moe_up{v}{f}", [P, 512], F32)) for f in range(2)] for v in range(2)]
            p2 = ctx.enter_context(nc.psum_tensor("moe_down", [P, 512], F32))
            block = ctx.enter_context(nc.Block())

            def owner_of(eng, n):
                return eng.value_load(self.owner[0:1, bass.ds(n, 1)], min_val=0, max_val=E - 1)

            @block.sync
            def _(sp):
                sp.dma_start(w2_b, t["w2_b"].rearrange("p (e d) -> p e d", e=E)).then_inc(b_in, 16)
                sp.dma_start(w1_b, t["w1_b"]).then_inc(b_in, 16)

            @block.gpsimd
            def _(pool):
                def load(n):
                    pool.indirect_dma_start(out=xg[n % 2], out_offset=None, in_=self.xn_rows,
                                            in_offset=bass.IndirectOffsetOnAxis(ap=self.source[:, n:n + 1], axis=0)).then_inc(xg_in[n % 2], 16)

                load(0)
                load(1)
                pool.wait_ge(tx_mm, 1)
                load(2)
                for n in range(NBLK):
                    if n + 3 < XBLK:
                        pool.wait_ge(tx_mm, n + 2)
                        load(n + 3)
                    pool.wait_ge(y_read, n + 1)
                    if n >= 1:
                        pool.wait_ge(stored[(n - 1) % 2], 16 * ((n - 1) // 2 + 1))
                    pool.indirect_dma_start(out=self.choices, out_offset=bass.IndirectOffsetOnAxis(ap=self.target[:, n:n + 1], axis=0),
                                            in_=y[n % 2], in_offset=None).then_inc(stored[n % 2], 16)
                for u in range(2):
                    pool.wait_ge(stored[u], 16 * (NBLK // 2))
                    pool.wait_ge(xg_in[u], 16 * (XBLK // 2))

            @block.tensor
            def _(pe):
                def turn_x(n, i, u):
                    pe.wait_ge(xg_in[u], i * 16 + 16)
                    pe.wait_ge(xt_read, n)
                    for c in range(C):
                        last = pe.transpose(px[:, c * P:(c + 1) * P], xg[u][:, c * P:(c + 1) * P], self.ident)
                    last.then_inc(tx_mm, 1)

                def rise(n, u):
                    pe.wait_ge(xt_read, n + 1)
                    pe.wait_ge(ws_ready, n + 1)
                    for k in range(KF):
                        for c in range(C):
                            last = pe.matmul(p1[u][k // HK][:, (k % HK) * P:(k % HK + 1) * P], ws[u][:, c, k * P:(k + 1) * P],
                                             xT[u][:, c, :], start=(c == 0), stop=(c == C - 1))
                        if k % HK == HK - 1:
                            last.then_inc(up_mm, 1)

                turn_x(0, 0, 0)
                rise(0, 0)
                turn_x(1, 0, 1)
                pe.wait_ge(self.w2_in, 16 * 2)
                with pe.Fori(0, NBLK // 2) as i:
                    owners = [owner_of(pe, i * 2 + u) for u in range(2)]
                    for u in range(2):
                        n = i * 2 + u
                        e = owners[u]
                        rise(n + 1, 1 - u)
                        turn_x(n + 2, i + 1, u)
                        pe.wait_ge(y_read, n)
                        for k in range(KF):
                            if k % HK == 0:
                                pe.wait_ge(gl[k // HK], n * HK + HK)
                            last = pe.matmul(p2[:, 0:D], hT[u][:, k, :], self.w2[:, bass.ds(e * KF + k, 1), :].rearrange("p a d -> p (a d)"),
                                             start=(k == 0), stop=(k == KF - 1))
                        last.then_inc(down_mm[u], 1)

            @block.vector
            def _(dve):
                def stage(n, u):
                    e = owner_of(dve, n)
                    dve.tensor_copy(ws[u], self.w1[:, :, bass.ds(e * FF, FF)]).then_inc(ws_ready, 1)

                dve.wait_ge(self.w1_in, 16 * C)
                stage(0, 0)
                stage(1, 1)
                dve.wait_ge(b_in, 32)
                with dve.Fori(0, NBLK // 2) as i:
                    for u in range(2):
                        n = i * 2 + u
                        dve.wait_ge(up_mm, n * 2 + 2)
                        stage(n + 2, u)
                        e = owner_of(dve, n)
                        dve.wait_ge(down_mm[u], i + 1)
                        dve.wait_ge(stored[u], i * 16)
                        dve.tensor_tensor(y[u], p2[:, 0:D], w2_b[:, bass.ds(e, 1), :].rearrange("p a d -> p (a d)"), ALU.add).then_inc(y_read, 1)

            @block.scalar
            def _(act):
                def copy_x(n, u):
                    act.wait_ge(tx_mm, n + 1)
                    act.activation(xT[u], px[:, 0:D].rearrange("p (c n) -> p c n", c=C), ACT.Copy).then_inc(xt_read, 1)

                act.wait_ge(b_in, 32)
                copy_x(0, 0)
                copy_x(1, 1)
                with act.Fori(0, NBLK // 2) as i:
                    for u in range(2):
                        n = i * 2 + u
                        e = owner_of(act, n)
                        act.wait_ge(down_mm[u], i)
                        for k in range(KF):
                            if k % HK == 0:
                                act.wait_ge(up_mm, n * 2 + k // HK + 1)
                            act.activation(hT[u][:, k, :], p1[u][k // HK][:, (k % HK) * P:(k % HK + 1) * P], ACT.Gelu_apprx_tanh,
                                           bias=w1_b[:, bass.ds(e * KF + k, 1)]).then_inc(gl[k // HK], 1)
                        copy_x(n + 2, u)

    def combine(self):
        nc, m, sem = self.nc, self.mem, self.sem
        R = 3
        m.at(self.route_at)
        got = [m.take(2, D) for _ in range(R)]
        got_in, mixed, stored = sem("choice_in", R), sem("choice_mixed", R), sem("out_stored")
        with nc.Block() as block:
            @block.scalar
            def _(act):
                for a in range(NT):
                    n = P if a < NT - 1 else LAST
                    if a >= R:
                        act.wait_ge(mixed[a % R], a // R * 2)
                    act.dma_start(got[a % R][0:n], self.choices[1 + 2 * a * P:1 + 2 * (a * P + n), :].rearrange(
                        "(p k) d -> p k d", k=2)).then_inc(got_in[a % R], 16)

            @block.vector
            def _(dve):
                for a in range(NT):
                    n = P if a < NT - 1 else LAST
                    dve.wait_ge(got_in[a % R], 16 * (a // R + 1))
                    for k in range(2):
                        dve.scalar_tensor_tensor(out=self.h[0:n, a, :], in0=got[a % R][0:n, k, :], scalar=self.weight[k][0:n, a:a + 1],
                                                 in1=self.h[0:n, a, :], op0=ALU.mult, op1=ALU.add).then_inc(mixed[a % R], 1)
                        dve.wait_ge(mixed[a % R], a // R * 2 + k + 1)

            @block.sync
            def _(sp):
                for a in range(NT):
                    n = P if a < NT - 1 else LAST
                    sp.wait_ge(mixed[a % R], a // R * 2 + 2)
                    sp.dma_start(self.out[a * P:a * P + n, :], self.h[0:n, a, :]).then_inc(stored, 16)
                sp.wait_ge(stored, 16 * NT)

    def load_w1(self, sp):
        self.w1_in = self.sem("moe_w1_in")
        for c in range(C):
            sp.dma_start(self.w1[:, c, :], self.t["w1"][:, c, :]).then_inc(self.w1_in, 16)

    def load_w2(self, sp):
        self.w2_in = self.sem("moe_w2_in")
        half = E * KF // 2
        for j in range(2):
            sp.dma_start(self.w2[:, j * half:(j + 1) * half, :], self.t["w2"][:, j * half:(j + 1) * half, :]).then_inc(self.w2_in, 16)

    def run(self):
        self.embed()
        self.retire("patch_")
        self.norm(0, self.h, 1e-5, ready_stats=False,
                  load=lambda sp: sp.wait_ge(self.soon_in, 16 * len(self.soon)))
        self.rotate()
        self.retire("rot_")
        self.attention()
        self.project(0, self.wo0, self.wo0_b, self.h)
        self.norm(1, self.h, 1e-5, gate=self.gate_w, logits=self.lg)
        self.route_first()
        self.experts()
        self.norm(2, self.h, 1e-5, keep=self.xn)
        self.linear_attention()
        self.project(1, self.wo1, self.bo1, self.xn, load=self.load_w1)
        self.norm(3, self.xn, 1e-12, gain=(self.g1, self.be1), keep=self.xn)
        self.feed_forward()
        self.norm(4, self.xn, 1e-12, gain=(self.g2, self.be2), turn=False, add_to=self.h, load=self.load_w2)
        self.norm(5, self.h, 1e-5, keep=self.xn, turn=False, gate=self.router, logits=self.lg)
        self.route_second()
        self.routed()
        self.combine()


def build(nc, dram, out):
    with ExitStack() as ctx:
        Kernel(nc, dram, out, ctx).run()


def layout(inp):
    f = {k: np.asarray(v) for k, v in inp.items()}
    a = {}

    def rows(v):
        return np.ascontiguousarray(np.broadcast_to(v.reshape(1, -1), (P, v.size)))

    def chunks(v):
        return np.ascontiguousarray(v.reshape(-1, P, v.shape[-1]).transpose(1, 0, 2))

    x = f["x"].reshape(NB, 3, 6, 16, 6, 16).transpose(1, 3, 5, 0, 2, 4).reshape(KP, P, NPT, P)
    a["patches"] = np.ascontiguousarray(x.transpose(2, 1, 0, 3))
    a["txt"] = f["txt"]
    a["wpatch"] = chunks(f["L0_tok_W"].T)
    pos = f["L0_tok_pos_embedding"][0]
    a["pos"] = np.ascontiguousarray(np.tile(pos[1:], (NB, 1)).reshape(NPT, P, D).transpose(1, 0, 2))
    a["tok_b"] = rows(f["L0_tok_b"])
    cls = np.stack([f["L0_tok_cls_token"][0, 0], pos[0]])
    a["cls"] = np.ascontiguousarray(np.broadcast_to(cls[None], (NB, 2, D)))
    turn = np.concatenate([np.arange(0, D, 2), np.arange(1, D, 2)])
    a["wqk0"] = np.ascontiguousarray(np.stack([chunks(f["L0_attn_wq"][turn].T), chunks(f["L0_attn_wk"][turn].T)], 1))
    a["wv0"] = chunks(f["L0_attn_wv"].T)
    a["wo0"] = chunks(f["L0_attn_wo_w"].T)
    a["wo0_b"] = rows(f["L0_attn_wo_b"])
    freq = np.exp(np.arange(0, D, 2, dtype=np.float32) * np.float32(-np.log(10000.0) / D))
    angle = (freq[:, None] * np.arange(S, dtype=np.float32)[None]).astype(np.float32)
    cos, sin = np.cos(angle).astype(np.float32), np.sin(angle).astype(np.float32)
    a["cos_sin"], a["sin_cos"] = np.stack([cos, sin], 1), np.stack([sin, cos], 1)
    a["own_mask"] = (np.arange(P)[:, None] // HD == np.arange(2 * HALF)[None]).astype(np.float32).reshape(P, 2, HALF)
    e1 = np.concatenate([f["L0_ffn_W1"], f["L0_ffn_Ws1"][None]])
    a["e1"] = np.ascontiguousarray(e1.reshape(E + 1, C, P, P).transpose(2, 0, 1, 3))
    a["e1_b"] = np.ascontiguousarray(np.concatenate([f["L0_ffn_b1"], f["L0_ffn_bs1"][None]]).T)
    e2 = np.concatenate([f["L0_ffn_W2"], f["L0_ffn_Ws2"][None]])
    a["e2"] = np.ascontiguousarray(e2.transpose(1, 0, 2))
    a["e2_b"] = np.ascontiguousarray(np.concatenate([f["L0_ffn_b2"], f["L0_ffn_bs2"][None]]))
    a["gate_w"] = chunks(f["L0_ffn_gate_W"])
    a["route_scale"] = rows(f["L0_ffn_route_scale"].reshape(1))
    a["wqk1"] = chunks(np.concatenate([f["L1_attn_Wq"], f["L1_attn_Wk"]], 1))
    a["wv1"] = chunks(f["L1_attn_Wv"])
    a["bqk1"] = rows(np.concatenate([f["L1_attn_bq"], f["L1_attn_bk"]]))
    a["bv1"] = rows(f["L1_attn_bv"])
    a["wo1"] = chunks(f["L1_attn_Wo"])
    a["f1"] = chunks(f["L1_attn_W1"])
    a["f2"] = chunks(f["L1_attn_W2"])
    a["f1_b"] = np.ascontiguousarray(f["L1_attn_b1"].reshape(KF, P).T)
    for name, key in (("bo1", "bo"), ("f2_b", "b2"), ("g1", "g1"), ("be1", "be1"), ("g2", "g2"), ("be2", "be2")):
        a[name] = rows(f[f"L1_attn_{key}"])
    a["router"] = chunks(f["L1_ffn_router_w"].T)
    a["w1"] = np.ascontiguousarray(f["L1_ffn_w1"].reshape(E * FF, C, P).transpose(2, 1, 0))
    a["w2"] = np.ascontiguousarray(f["L1_ffn_w2"].transpose(0, 2, 1).reshape(E * KF, P, D).transpose(1, 0, 2))
    a["w1_b"] = np.ascontiguousarray(f["L1_ffn_b1"].reshape(E * KF, P).T)
    a["w2_b"] = rows(f["L1_ffn_b2"])
    same = (np.arange(P)[:, None] // HD == np.arange(P)[None] // HD)
    a["head_mask"] = (same / float(HD) ** 0.5).astype(np.float32)
    a["rank"] = rows(np.arange(E, 0, -1).astype(np.float32))
    a["r_tri"] = np.triu(np.ones((P, P), np.float32), 1)
    a["r_valid"] = (np.arange(NT)[None] * P + np.arange(P)[:, None] < N).astype(np.float32)
    a["r_steps"] = rows(np.arange(NT, dtype=np.float32) * P)
    a["r_lower"] = np.ascontiguousarray(np.broadcast_to(np.tril(np.ones((E, E), np.float32), -1), (P, E, E)))
    a["r_blocks"] = rows(np.arange(XBLK, dtype=np.float32))
    a["r_places"] = rows(np.arange(P, dtype=np.float32))
    a["r_row"] = (2 * np.arange(P)[:, None] + np.arange(1, 3)[None]).astype(np.float32)
    a["r_tile"] = rows(np.arange(NT, dtype=np.float32))
    a["ident"] = np.eye(P, dtype=np.float32)
    return {k: np.ascontiguousarray(v) for k, v in a.items()}


def kernel(**inputs):
    import concourse.bacc as bacc
    from concourse.bass_utils import run_bass_kernel_spmd

    arrays = layout(inputs)
    nc = bacc.Bacc("TRN2", target_bir_lowering=False, num_devices=1)
    dram = {}
    for key, a in arrays.items():
        dram[key] = nc.dram_tensor(f"in_{key}_dram", a.shape, mybir.dt.from_np(a.dtype), kind="ExternalInput").ap()
    out = nc.dram_tensor("out_0_dram", [N, D], F32, kind="ExternalOutput").ap()
    build(nc, dram, out)
    feed = {f"in_{key}_dram": a for key, a in arrays.items()}
    result = run_bass_kernel_spmd(nc, [feed], core_ids=[0]).results[0]
    return result["out_0_dram"].reshape(NB, S, D)
```

```python
from contextlib import ExitStack

import numpy as np

import concourse.bass as bass
from concourse import mybir

ALU = mybir.AluOpType
ACT = mybir.ActivationFunctionType
AX_X = mybir.AxisListType.X
F32 = mybir.dt.float32
F32R = mybir.dt.float32r
I32 = mybir.dt.int32
U32 = mybir.dt.uint32

P = 128
D = 256
C = D // P
NB = 32
PATCHES = 36
TXT = 32
S = 1 + PATCHES + TXT
N = NB * S
NT = -(-N // P)
LAST = N - (NT - 1) * P
G = 3
GW = G * P
NG = NT // G
NPT = NB * PATCHES // P
KP = 768 // P
HEADS = 16
HD = D // HEADS
HALF = 64 // HD
E = 8
FF = 1024
KF = FF // P
PAIR = 2 * S
XW = NT * P + GW
OPAD = PAIR
OW = OPAD + NT * P
NBLK = (2 * N + E * (P - 1)) // P
XBLK = NBLK + 2
BIG = 1.0e30


class Memory:

    def __init__(self, nc, ctx, cols):
        self.nc, self.cols, self.pos, self.count = nc, cols, 0, 0
        self.base = -(-nc.sbuf_base // 32) * 32
        ctx.enter_context(nc.sbuf_tensor("memory", [P, cols], F32))

    def at(self, pos):
        self.pos = pos

    def place(self, dtype, dims):
        n = int(np.prod(dims))
        assert self.pos + n <= self.cols, (self.pos, n, self.cols)
        self.count += 1
        v = self.nc.alloc_sbuf_tensor_at(f"place{self.count}", [P, n], dtype, offset=self.base + 4 * self.pos)[:, :]
        if len(dims) == 1:
            return v
        names = "abcd"[:len(dims)]
        kw = {names[j]: dims[j] for j in range(1, len(dims))}
        return v.rearrange(f"p ({' '.join(names)}) -> p {' '.join(names)}", **kw)

    def step(self, dims):
        self.pos += -(-int(np.prod(dims)) // 8) * 8

    def take(self, *dims):
        v = self.place(F32, dims)
        self.step(dims)
        return v

    def take_rounded(self, *dims):
        v = self.place(F32R, dims)
        self.step(dims)
        return v

    def both(self, *dims):
        v = self.place(F32, dims), self.place(F32R, dims)
        self.step(dims)
        return v


class Steps:

    def __init__(self, eng, sem, base):
        self.eng, self.sem, self.base, self.n = eng, sem, base, 0

    def __call__(self, ins):
        self.mark(ins)
        self.wait()

    def mark(self, ins):
        ins.then_inc(self.sem, 1)
        self.n += 1

    def wait(self):
        self.eng.wait_ge(self.sem, self.base + self.n)


def leading(eng, out, x):
    return eng.tensor_copy(out, x)


def product(pe, out, a, b, start, stop):
    for j, (x, y) in enumerate(((0, 0), (1, 0), (0, 1))):
        last = pe.matmul(out, a[x], b[y], start=start and j == 0, stop=stop and j == 2)
    return last


def inner(ap, k):
    return ap.unsqueeze(len(ap.shape)).to_broadcast(list(ap.shape) + [k])


def spread(ap, k):
    s = list(ap.shape)
    return ap.unsqueeze(1).to_broadcast([s[0], k] + s[1:])


RSQRT_PARTS = 11


def moments(dve, link, stats, eps, mean, var, tmp):
    link.mark(dve.tensor_tensor(mean, stats[:, :, 1], stats[:, :, 4], ALU.add))
    link.mark(dve.tensor_tensor(tmp, stats[:, :, 1], stats[:, :, 4], ALU.subtract))
    link(dve.tensor_tensor(var, stats[:, :, 2], stats[:, :, 5], ALU.add))
    link.mark(dve.tensor_scalar(mean, mean, 0.5, None, ALU.mult))
    link.mark(dve.scalar_tensor_tensor(out=tmp, in0=tmp, scalar=0.25, in1=tmp, op0=ALU.mult, op1=ALU.mult))
    link(dve.tensor_scalar(var, var, 1.0 / D, eps, ALU.mult, ALU.add))
    link(dve.tensor_tensor(var, var, tmp, ALU.add))


def rsqrt_part(dve, k, v, y, t):
    if k == 0:
        return dve.tensor_scalar(t.bitcast(I32), v.bitcast(I32), 1, None, ALU.arith_shift_right)
    if k == 1:
        return dve.tensor_scalar(y.bitcast(I32), t.bitcast(I32), -1.0, float(0x5F3759DF), ALU.mult, ALU.add)
    if k % 3 == 2:
        return dve.tensor_tensor(t, v, y, ALU.mult)
    if k % 3 == 0:
        return dve.scalar_tensor_tensor(out=t, in0=t, scalar=-0.5, in1=y, op0=ALU.mult, op1=ALU.mult)
    return dve.scalar_tensor_tensor(out=y, in0=t, scalar=1.5, in1=y, op0=ALU.add, op1=ALU.mult)


def rsqrt(dve, link, v, y, t):
    for k in range(RSQRT_PARTS):
        link(rsqrt_part(dve, k, v, y, t))


def three(tile, i, u):
    return tile[:, bass.ds(i * (2 * G) + G * u, G), :]


def one(tile, i, u, j):
    return tile[:, bass.ds(i * (2 * G) + (G * u + j), 1), :].rearrange("p a d -> p (a d)")


def cols(tile, i, u):
    return tile[:, :, bass.ds(i * (2 * GW) + GW * u, GW)]


class Kernel:
    def __init__(self, nc, t, out, ctx):
        self.nc, self.t, self.out, self.ctx = nc, t, out, ctx
        self.sems = {}
        self.zeroed = []
        self.norm_base = {}
        self.stats_count = 0
        m = self.mem = Memory(nc, ctx, 53100)
        self.h = m.take(NT, D)
        self.ident = m.take(P)
        self.head_mask = m.take(P)
        self.rank = m.take(E)
        self.top_rank = m.take(NT)
        self.lg = m.take(NT, E)
        self.stats = m.take(NT, 6)
        self.xn_at = m.pos
        self.xn = m.take(NT, D)
        self.keep_at = m.pos
        m.at(m.pos + 256)
        self.w1_at = m.pos
        self.w2_at = m.pos + C * E * FF
        self.work_at = self.w2_at + E * KF * D
        self.route_at = self.work_at
        self.w1 = m.take(C, E * FF)
        self.w2 = m.take(E * KF, D)
        m.at(self.w2_at)
        m.at(self.w1_at + (C - 1) * E * FF)
        self.f1_hi, self.f2_hi = m.take_rounded(C, FF), m.take_rounded(KF, D)
        self.la_at = m.pos
        m.at(self.w1_at + (C - 1) * E * FF)
        self.wqk1_hi, self.wv1_hi = m.take_rounded(C, 2 * D), m.take_rounded(C, D)
        m.at(self.w2_at)
        self.xT, self.xT_lo = m.both(C, XW)
        self.oT = m.take(C, OW)
        self.late_at = m.pos
        self.weights()

    def sem(self, name, n=None):
        if n is not None:
            return [self.sem(f"{name}{j}") for j in range(n)]
        if name not in self.sems:
            self.sems[name] = self.nc.alloc_semaphore(name)
        return self.sems[name]

    def retire(self, *prefixes):
        for handle in self.zeroed:
            self.nc.release_semaphore(handle)
        self.zeroed = [self.sems.pop(name) for name in list(self.sems) if name.startswith(prefixes)]
        for handle in self.zeroed:
            self.nc.gpsimd.sem_clear(handle)

    def dram(self, name, shape, dt=F32):
        return self.nc.dram_tensor(name, shape, dt, kind="Internal").ap()

    def weights(self):
        m = self.mem
        m.at(self.w1_at)
        self.early = {}
        def w(name, *dims):
            v = m.take(*dims)
            self.early[name] = v
            return v

        def w2(name, *dims):
            v = m.both(*dims)
            self.early[name] = v[0]
            return v
        self.wpatch = w("wpatch", KP, D)
        self.pos = w("pos", NPT, D)
        self.wqk0 = w("wqk0", 2, C, D)
        self.wv0 = w("wv0", C, D)
        self.wo0 = w("wo0", C, D)
        self.wo0_b = w("wo0_b", D)
        self.tok_b = w("tok_b", D)
        self.cos_sin = w("cos_sin", 2, S)
        self.sin_cos = w("sin_cos", 2, S)
        self.own_mask = w("own_mask", 2, HALF)
        self.e1, self.e1_lo = w2("e1", E + 1, C, P)
        self.e1_b = w("e1_b", E + 1)
        self.e2, self.e2_lo = w2("e2", E + 1, D)
        self.gate_w = w("gate_w", C, E)
        self.route_scale = w("route_scale", 1)
        assert m.pos <= self.w2_at
        self.early_end = m.pos
        self.e1_hi, self.e2_hi = m.take_rounded(E + 1, C, P), m.take_rounded(E + 1, D)
        assert m.pos <= self.w2_at
        m.at(self.late_at)
        self.wqk1, self.wqk1_lo = w2("wqk1", C, 2 * D)
        self.wv1, self.wv1_lo = w2("wv1", C, D)
        self.bv1 = w("bv1", D)
        self.f1, self.f1_lo = w2("f1", C, FF)
        self.f2, self.f2_lo = w2("f2", KF, D)
        assert m.pos <= self.work_at, (m.pos, self.work_at)
        m.at(self.work_at)
        self.wo1 = w("wo1", C, D)
        self.bqk1 = w("bqk1", 2 * D)
        self.f1_b = w("f1_b", KF)
        self.bo1 = w("bo1", D)
        self.f2_b = w("f2_b", D)
        self.g1 = w("g1", D)
        self.be1 = w("be1", D)
        self.g2 = w("g2", D)
        self.be2 = w("be2", D)
        self.router = w("router", C, E)
        self.work_at = m.pos

    def embed(self):
        nc, m, t, sem = self.nc, self.mem, self.t, self.sem
        R = 3
        m.at(self.early_end)
        patches = [m.take(KP, P) for _ in range(R)]
        m.at(self.work_at)
        rows = [m.take(D) for _ in range(R)]
        cls = m.take(2, D)
        tokens = self.dram("patch_tokens", [NPT * P, D])
        stream = self.stream = self.dram("stream", [N, D])
        by_batch = stream.rearrange("(b s) d -> b s d", s=S)
        self.soon = ("wqk0", "cos_sin", "sin_cos", "own_mask", "wv0")
        in_emb, in_pos, in_cls = sem("weights_in_embed"), sem("pos_in"), sem("cls_in")
        self.soon_in, self.rest_in = sem("soon_weights_in"), sem("weights_in")
        patch_in, mm, summed, stored = sem("patch_in", R), sem("patch_mm", R), sem("patch_summed", R), sem("patch_stored", R)
        biased, cls_sum, moved = sem("pos_biased"), sem("cls_summed"), sem("stream_written")
        patches_moved = sem("tokens_moved")
        cleared, h_in, stats_done = sem("pads_cleared"), sem("h_in", NPT // R), sem("stats_done")
        whole = [(0, 0)]
        for k in range(NPT // R):
            batches = (k + 1) * R * P // PATCHES
            whole.append((batches, batches * S // P if batches < NB else NT))

        with ExitStack() as ctx:
            acc = [ctx.enter_context(nc.psum_tensor(f"embed_acc{r}", [P, 512], F32)) for r in range(R)]
            block = ctx.enter_context(nc.Block())

            @block.sync
            def _(sp):
                sp.dma_start(self.early["wpatch"], t["wpatch"]).then_inc(in_emb, 16)
                sp.dma_start(cls[0:NB], t["cls"]).then_inc(in_cls, 16)
                with sp.Fori(0, NPT // R) as i:
                    for r in range(R):
                        sp.wait_ge(mm[r], i)
                        sp.dma_start(patches[r], t["patches"][bass.ds(i * R + r, 1)].rearrange(
                            "a p k t -> (a p) k t")).then_inc(patch_in[r], 16)

            @block.gpsimd
            def _(pool):
                pool.memset(self.h[:, NT - 1, :], 0.0).then_inc(cleared, 1)
                pool.memset(self.xT[:, :, NT * P:], 0.0).then_inc(cleared, 1)
                pool.memset(self.oT[:, :, 0:OPAD], 0.0).then_inc(cleared, 1)
                pool.memset(self.oT[:, :, OPAD + N:], 0.0).then_inc(cleared, 1)
                for k in range(NPT // R):
                    (b0, a0), (b1, a1) = whole[k], whole[k + 1]
                    for r in range(R):
                        pool.wait_ge(stored[r], 16 * (k + 1))
                    pool.dma_start(by_batch[b0:b1, 1:1 + PATCHES, :],
                                   tokens[b0 * PATCHES:b1 * PATCHES, :].rearrange("(b s) d -> b s d", s=PATCHES)).then_inc(patches_moved, 16)
                    pool.wait_ge(moved, 32)
                    pool.wait_ge(patches_moved, 16 * (k + 1))
                    a2 = min(a1, NT - 1)
                    pool.dma_start(self.h[:, a0:a2, :], stream[a0 * P:a2 * P, :].rearrange("(a p) d -> p a d", p=P)).then_inc(h_in[k], 16)
                    if a1 == NT:
                        pool.wait_ge(cleared, 4)
                        pool.dma_start(self.h[0:LAST, NT - 1, :], stream[(NT - 1) * P:, :]).then_inc(h_in[k], 16)

            @block.tensor
            def _(pe):
                pe.wait_ge(in_emb, 16)
                with pe.Fori(0, NPT // R) as i:
                    for r in range(R):
                        pe.wait_ge(patch_in[r], 16 * i + 16)
                        pe.wait_ge(summed[r], i)
                        for k in range(KP):
                            last = pe.matmul(acc[r][:, 0:D], patches[r][:, k, :], self.wpatch[:, k, :],
                                             start=(k == 0), stop=(k == KP - 1))
                        last.then_inc(mm[r], 1)

            @block.vector
            def _(dve):
                dve.wait_ge(in_cls, 16)
                dve.tensor_tensor(cls[0:NB, 0, :], cls[0:NB, 0, :], cls[0:NB, 1, :], ALU.add).then_inc(cls_sum, 1)
                dve.wait_ge(in_pos, 48)
                dve.tensor_tensor(self.pos, self.pos, spread(self.tok_b, NPT), ALU.add).then_inc(biased, 1)
                dve.wait_ge(biased, 1)
                with dve.Fori(0, NPT // R) as i:
                    for r in range(R):
                        dve.wait_ge(mm[r], i + 1)
                        dve.wait_ge(stored[r], 16 * i)
                        dve.tensor_tensor(rows[r], acc[r][:, 0:D],
                                          self.pos[:, bass.ds(i * R + r, 1), :].rearrange("p a d -> p (a d)"),
                                          ALU.add).then_inc(summed[r], 1)
                for k in range(NPT // R):
                    a0, a1 = whole[k][1], whole[k + 1][1]
                    dve.wait_ge(h_in[k], 32 if a1 == NT else 16)
                    for a in range(a0, a1):
                        dve.bn_stats(self.stats[:, a, :], self.h[:, a, :]).then_inc(stats_done, 1)

            @block.scalar
            def _(act):
                for name, view in (("pos", self.pos), ("tok_b", self.tok_b), ("ident", self.ident)):
                    act.dma_start(view, t[name]).then_inc(in_pos, 16)
                act.dma_start(by_batch[:, 1 + PATCHES:, :], t["txt"]).then_inc(moved, 16)
                act.wait_ge(cls_sum, 1)
                act.dma_start(by_batch[:, 0, :], cls[0:NB, 0, :]).then_inc(moved, 16)
                with act.Fori(0, NPT // R) as i:
                    for r in range(R):
                        act.wait_ge(summed[r], i + 1)
                        act.dma_start(tokens[bass.ds((i * R + r) * P, P), :], rows[r]).then_inc(stored[r], 16)
        self.stats_count += NT

    def load_weights(self, sp):
        first, t = ("wpatch", "pos", "tok_b", "ident"), self.t
        for name in self.soon:
            sp.dma_start(self.early[name], t[name]).then_inc(self.soon_in, 16)
        rest = {name: view for name, view in self.early.items() if name not in first + self.soon}
        rest["head_mask"], rest["rank"] = self.head_mask, self.rank
        for name, view in rest.items():
            sp.dma_start(view, t[name]).then_inc(self.rest_in, 16)
        self.rest_count = len(rest)
        sp.wait_ge(self.soon_in, 16 * len(self.soon))

    def tile_stats(self, dve, src, i, u):
        for j in range(G):
            dve.bn_stats(one(self.stats, i, u, j), one(src, i, u, j)).then_inc(self.sem("stats_done"), 1)

    def norm(self, rep, src, eps, gain=None, keep=None, turn=True, add_to=None, gate=None, logits=None, load=None,
             rest=(), split=()):
        nc, m, sem = self.nc, self.mem, self.sem
        name = f"norm{rep}"
        m.at(self.work_at)
        z = [m.take(G, D) for _ in range(2)]
        zt = [m.take(C, GW) for _ in range(2)] if gate is not None else None
        mean, var, r, tmp, spare = m.take(NT), m.take(NT), m.take(NT), m.take(NT), m.take(8)
        ready, turned, copied, kept = sem("norm_ready", 2), sem("norm_turned", 2), sem("norm_copied", 2), sem("norm_kept", 2)
        lg_mm, lg_read, step, scaled = sem("norm_logits_mm", 2), sem("norm_logits_read", 2), sem("norm_step"), sem("norm_scaled")
        stats_done = sem("stats_done")
        base = self.norm_base
        b = dict(base)
        def B(key):
            return b.get(key, 0)
        I = NG // 2
        with ExitStack() as ctx:
            if turn or gate is not None:
                flip = [ctx.enter_context(nc.psum_tensor(f"{name}_flip{u}", [P, C, 512], F32)) for u in range(2)]
            if gate is not None:
                lg = [ctx.enter_context(nc.psum_tensor(f"{name}_lg{u}", [P, 512], F32)) for u in range(2)]
            block = ctx.enter_context(nc.Block())

            if load is not None:
                @block.sync
                def _(sp):
                    load(sp)

            @block.vector
            def _(dve):
                for x, x_hi, _ in split:
                    leading(dve, x_hi, x).then_inc(sem("norm_split_cut"), 1)
                dve.wait_ge(stats_done, self.stats_count)
                link = Steps(dve, step, B("step"))
                moments(dve, link, self.stats, eps, mean, var, tmp)
                rsqrt(dve, link, var, r, tmp)
                base["step"] = B("step") + link.n
                with dve.Fori(0, I) as i:
                    for u in range(2):
                        if turn or gate is not None:
                            dve.wait_ge(turned[u], B("turned") + i)
                        if keep is not None or add_to is not None:
                            dve.wait_ge(kept[u], B("kept") + i)
                        for j in range(G):
                            at = bass.ds(i * (2 * G) + (G * u + j), 1)
                            if gain is None:
                                dve.tensor_scalar(z[u][:, j, :], one(src, i, u, j), mean[:, at], r[:, at],
                                                  ALU.subtract, ALU.mult).then_inc(ready[u], 1)
                            else:
                                dve.scalar_tensor_tensor(out=z[u][:, j, :], in0=one(src, i, u, j), scalar=mean[:, at],
                                                         in1=gain[0], op0=ALU.subtract, op1=ALU.mult).then_inc(scaled, 1)
                        if gain is not None:
                            for j in range(G):
                                at = bass.ds(i * (2 * G) + (G * u + j), 1)
                                dve.wait_ge(scaled, B("scaled") + i * (2 * G) + (G * u + j + 1))
                                dve.scalar_tensor_tensor(out=z[u][:, j, :], in0=z[u][:, j, :], scalar=r[:, at],
                                                         in1=gain[1], op0=ALU.mult, op1=ALU.add).then_inc(ready[u], 1)
                        if add_to is not None and u == 1:
                            dve.wait_ge(kept[0], B("kept") + i + 1)
                            self.tile_stats(dve, add_to, i, 0)
                    if add_to is not None:
                        dve.wait_ge(kept[1], B("kept") + i + 1)
                        self.tile_stats(dve, add_to, i, 1)

            if rest or split:
                @block.gpsimd
                def _(pool):
                    if split:
                        pool.memset(self.xT[:, :, NT * P:], 0.0)
                        pool.wait_ge(sem("norm_split_cut"), len(split))
                    for x, x_hi, x_lo in rest + split:
                        pool.tensor_tensor(x_lo, x, x_hi.bitcast(F32), ALU.subtract)

            if add_to is not None or (gate is not None and turn):
                @block.gpsimd
                def _(pool):
                    with pool.Fori(0, I) as i:
                        for u in range(2):
                            if add_to is not None:
                                pool.wait_ge(ready[u], B("ready") + (i + 1) * G)
                                pool.tensor_tensor(three(add_to, i, u), three(add_to, i, u), z[u], ALU.add).then_inc(kept[u], 1)
                            if gate is not None and turn:
                                pool.wait_ge(copied[u], B("copied") + i + 1)
                                pool.tensor_copy(cols(self.xT, i, u), zt[u]).then_inc(sem("norm_xT", 2)[u], 1)

            if turn or gate is not None:
                @block.tensor
                def _(pe):
                    with pe.Fori(0, I) as i:
                        for u in range(2):
                            pe.wait_ge(copied[u], B("copied") + i)
                            for j in range(G):
                                pe.wait_ge(ready[u], B("ready") + i * G + (j + 1))
                                for c in range(C):
                                    last = pe.transpose(flip[u][:, c, j * P:(j + 1) * P], z[u][:, j, c * P:(c + 1) * P], self.ident)
                            last.then_inc(turned[u], 1)
                        if gate is not None:
                            for u in range(2):
                                pe.wait_ge(copied[u], B("copied") + i + 1)
                                pe.wait_ge(lg_read[u], B("lg_read") + i)
                                for j in range(G):
                                    for c in range(C):
                                        last = pe.matmul(lg[u][:, j * E:(j + 1) * E], zt[u][:, c, j * P:(j + 1) * P], gate[:, c, :],
                                                         start=(c == 0), stop=(c == C - 1))
                                last.then_inc(lg_mm[u], 1)

            @block.scalar
            def _(act):
                if rep == 0:
                    act.activation(spare, self.ident[:, 0:8], ACT.Copy)
                with act.Fori(0, I) as i:
                    for u in range(2):
                        if turn or gate is not None:
                            act.wait_ge(turned[u], B("turned") + i + 1)
                            if gate is not None:
                                act.wait_ge(lg_mm[u], B("lg_mm") + i)
                                if turn:
                                    act.wait_ge(sem("norm_xT", 2)[u], B("xT") + i)
                                act.activation(zt[u], flip[u][:, :, 0:GW], ACT.Copy).then_inc(copied[u], 1)
                            else:
                                act.activation(cols(self.xT, i, u), flip[u][:, :, 0:GW], ACT.Copy).then_inc(copied[u], 1)
                        if keep is not None:
                            act.wait_ge(ready[u], B("ready") + (i + 1) * G)
                            act.activation(three(keep, i, u), z[u], ACT.Copy).then_inc(kept[u], 1)
                    if gate is not None:
                        for u in range(2):
                            act.wait_ge(lg_mm[u], B("lg_mm") + i + 1)
                            act.activation(three(logits, i, u), lg[u][:, 0:G * E].rearrange("p (j e) -> p j e", e=E),
                                           ACT.Copy).then_inc(lg_read[u], 1)
        def add(key, n):
            base[key] = base.get(key, 0) + n
        add("ready", I * G)
        if turn or gate is not None:
            add("turned", I); add("copied", I)
        if keep is not None or add_to is not None:
            add("kept", I)
        if add_to is not None:
            self.stats_count += NT
        if gain is not None:
            add("scaled", NT)
        if gate is not None:
            add("lg_mm", I); add("lg_read", I)
            if turn:
                add("xT", I)

    def rotate(self):
        nc, m, sem = self.nc, self.mem, self.sem
        R = 4
        W = R * S
        I = NB // R // 2
        self.qF = self.xn.rearrange("p a d -> p (a d)")[:, 0:C * N].rearrange("p (c n) -> p c n", c=C)
        m.at(self.early_end)
        self.kF = m.take(C, N)
        m.at(self.work_at)
        prod = [[m.take(2, R, S) for _ in range(2)] for _ in range(2)]
        mm, read, summed = sem("rot_mm", 2), sem("rot_read", 2), sem("rot_summed", 2)
        with ExitStack() as ctx:
            ps = [ctx.enter_context(nc.psum_tensor(f"rot{qk}", [P, 2, 512], F32)) for qk in range(2)]
            block = ctx.enter_context(nc.Block())

            @block.tensor
            def _(pe):
                with pe.Fori(0, 2 * I) as i:
                    for qk in range(2):
                        pe.wait_ge(read[qk], i)
                        for eo in range(2):
                            for c in range(C):
                                last = pe.matmul(ps[qk][:, eo, 0:W], self.wqk0[:, qk, c, eo * P:(eo + 1) * P],
                                                 self.xT[:, c, bass.ds(i * W, W)], start=(c == 0), stop=(c == C - 1))
                        last.then_inc(mm[qk], 1)

            @block.vector
            def _(dve):
                with dve.Fori(0, 2 * I) as i:
                    for qk in range(2):
                        dve.wait_ge(mm[qk], i + 1)
                        dve.wait_ge(summed[qk], i * 2)
                        for eo in range(2):
                            for k, tab in enumerate((self.cos_sin, self.sin_cos)):
                                last = dve.tensor_tensor(prod[qk][k][:, eo], ps[qk][:, eo, 0:W].rearrange("p (r s) -> p r s", s=S),
                                                         spread(tab[:, eo], R), ALU.mult)
                        last.then_inc(read[qk], 1)

            @block.gpsimd
            def _(pool):
                with pool.Fori(0, 2 * I) as i:
                    for qk, dst in enumerate((self.qF, self.kF)):
                        pool.wait_ge(read[qk], i + 1)
                        for k, op in ((0, ALU.subtract), (1, ALU.add)):
                            pool.tensor_tensor(dst[:, k, bass.ds(i * W, W)], prod[qk][k][:, 0].rearrange("p r s -> p (r s)"),
                                               prod[qk][k][:, 1].rearrange("p r s -> p (r s)"), op).then_inc(summed[qk], 1)

    def attention(self):
        nc, m, sem = self.nc, self.mem, self.sem
        H2 = HALF
        VW = HD + 1
        m.at(self.work_at)
        q = [m.take(C, S) for _ in range(2)]
        k2 = [m.take(C, 2, HALF, S) for _ in range(2)]
        x = [m.take(C, S) for _ in range(2)]
        va = [m.take(HEADS, VW) for _ in range(2)]
        on = m.take(HEADS, HD)
        top = m.take(4, H2)
        rsum = m.take(HEADS)
        prob = [m.take(4, H2, S) for _ in range(2)]
        pt = m.take(4, H2, S)
        staged, keyed = sem("x_staged"), sem("qk_staged")
        v_mm, v_read, s_mm, s_read = sem("v_mm"), sem("v_read"), sem("scores_mm"), sem("scores_read")
        exp_done, pt_mm = sem("exp_done"), sem("probs_turned", 2)
        pt_read, pv_mm, o_norm = sem("probs_copied", 2), sem("pv_mm"), sem("o_normed")
        ot_mm, ot_read, preset, step = sem("o_turned"), sem("o_copied"), sem("attn_preset"), sem("attn_step")

        with ExitStack() as ctx:
            sc = ctx.enter_context(nc.psum_tensor("scores", [P, 4, 512], F32))
            tp = [ctx.enter_context(nc.psum_tensor(f"turned_probs{j}", [P, 512], F32)) for j in range(2)]
            pj = ctx.enter_context(nc.psum_tensor("values", [P, 512], F32))
            ov = ctx.enter_context(nc.psum_tensor("out_values", [P, 512], F32))
            block = ctx.enter_context(nc.Block())
            ov_heads = ov[0:S, 0:HEADS * VW].rearrange("p (h w) -> p h w", w=VW)
            ov_turned = ov[:, HEADS * VW:HEADS * VW + C * S].rearrange("p (c s) -> p c s", s=S)
            sc_heads = sc[0:S, :, 0:H2 * S].rearrange("p g (j s) -> p g j s", s=S)

            @block.sync
            def _(sp):
                sp.wait_ge(self.rest_in, 16 * self.rest_count)

            @block.gpsimd
            def _(pool):
                def stage_x(n, u):
                    pool.tensor_copy(x[u], self.xT[:, :, bass.ds(n * S, S)]).then_inc(staged, 1)

                def stage_qk(n, u):
                    pool.tensor_copy(q[u], self.qF[:, :, bass.ds(n * S, S)]).then_inc(keyed, 1)
                    for c in range(C):
                        pool.tensor_tensor(k2[u][:, c].rearrange("p r h s -> p (r h) s"), spread(self.kF[:, c, bass.ds(n * S, S)], 2 * HALF),
                                           inner(self.own_mask.rearrange("p r h -> p (r h)"), S), ALU.mult).then_inc(keyed, 1)

                stage_qk(0, 0)
                stage_x(0, 0)
                stage_qk(1, 1)
                stage_x(1, 1)
                with pool.Fori(0, NB // 2 - 1) as i:
                    for u in range(2):
                        n = i * 2 + u
                        pool.wait_ge(s_mm, n + 1)
                        stage_qk(n + 2, u)
                        pool.wait_ge(v_mm, n + 1)
                        stage_x(n + 2, u)

            @block.tensor
            def _(pe):
                def values(n, u):
                    pe.wait_ge(staged, n + 1)
                    pe.wait_ge(v_read, n)
                    for c in range(C):
                        last = pe.matmul(pj[0:S, 0:D], x[u][:, c, :], self.wv0[:, c, :], start=(c == 0), stop=(c == C - 1))
                    last.then_inc(v_mm, 1)

                def scores(n, u):
                    pe.wait_ge(keyed, n * 3 + 3)
                    pe.wait_ge(s_read, n)
                    for c in range(C):
                        for r in range(2):
                            last = pe.matmul(sc[0:S, 2 * c + r, 0:HALF * S], q[u][:, c, :],
                                             k2[u][:, c, r, :, :].rearrange("p a s -> p (a s)"),
                                             start=True, stop=True)
                    last.then_inc(s_mm, 1)

                def turn_out(n):
                    pe.wait_ge(o_norm, n + 1)
                    for c in range(C):
                        last = pe.transpose(ov_turned[:, c, :], on[0:S, c * 8:(c + 1) * 8, :].rearrange("p h w -> p (h w)"),
                                            self.ident[0:S, 0:S])
                    last.then_inc(ot_mm, 1)

                def turn_probs(n, i, u, groups):
                    for g in groups:
                        pe.wait_ge(pt_read[g % 2], n * 2 + g // 2)
                        for j in range(H2):
                            last = pe.transpose(tp[g % 2][0:S, j * S:(j + 1) * S], prob[u][0:S, g, j, :], self.ident[0:S, 0:S])
                        last.then_inc(pt_mm[u], 1)

                def step_of(n, i, u, ahead_s, ahead_v):
                    if ahead_s:
                        scores(n + 1, 1 - u)
                    pe.wait_ge(exp_done, n + 1)
                    turn_probs(n, i, u, (0, 1))
                    turn_out(n - 1)
                    turn_probs(n, i, u, (2, 3))
                    if ahead_v:
                        values(n + 2, u)
                    pe.wait_ge(pt_read[0], n * 2 + 2)
                    pe.wait_ge(pt_read[1], n * 2 + 2)
                    pe.wait_ge(v_read, n + 1)
                    pe.wait_ge(ot_read, n + 1)
                    for g in range(4):
                        for j in range(H2):
                            head = HALF * g + j
                            last = pe.matmul(ov_heads[:, head, :], pt[0:S, g, j, :], va[u][0:S, head, :], start=True, stop=True)
                    last.then_inc(pv_mm, 1)

                scores(0, 0)
                values(0, 0)
                values(1, 1)
                pe.wait_ge(preset, 3)
                with pe.Fori(0, NB // 2 - 1) as i:
                    for u in range(2):
                        step_of(i * 2 + u, i, u, True, True)
                step_of(NB - 2, NB // 2 - 1, 0, True, False)
                step_of(NB - 1, NB // 2 - 1, 1, False, False)
                turn_out(NB - 1)

            @block.vector
            def _(dve):
                dve.memset(on[0:S], 0.0).then_inc(preset, 1)
                for u in range(2):
                    dve.memset(va[u][0:S], 1.0).then_inc(preset, 1)
                dve.wait_ge(s_mm, 1)
                dve.tensor_reduce(top[0:S], sc_heads, AX_X, ALU.max).then_inc(step, 1)
                dve.wait_ge(step, 1)
                dve.tensor_tensor(prob[0][0:S], sc_heads, inner(top[0:S], S), ALU.subtract).then_inc(s_read, 1)

                def step_of(n, i, u, ahead):
                    if ahead:
                        dve.wait_ge(s_mm, n + 2)
                        dve.tensor_reduce(top[0:S], sc_heads, AX_X, ALU.max).then_inc(step, 1)
                        dve.wait_ge(step, n * 2 + 2)
                        dve.wait_ge(pt_mm[1 - u], (i + u) * 4)
                        dve.tensor_tensor(prob[1 - u][0:S], sc_heads, inner(top[0:S], S), ALU.subtract).then_inc(s_read, 1)
                    dve.wait_ge(pv_mm, n + 1)
                    dve.reciprocal(rsum[0:S], ov_heads[:, :, HD]).then_inc(step, 1)
                    dve.wait_ge(step, n * 2 + (3 if ahead else 2))
                    dve.wait_ge(ot_mm, n + 1)
                    dve.tensor_tensor(on[0:S], ov_heads[:, :, 0:HD], inner(rsum[0:S], HD), ALU.mult).then_inc(o_norm, 1)

                with dve.Fori(0, NB // 2 - 1) as i:
                    for u in range(2):
                        step_of(i * 2 + u, i, u, True)
                step_of(NB - 2, NB // 2 - 1, 0, True)
                step_of(NB - 1, NB // 2 - 1, 1, False)

            @block.scalar
            def _(act):
                def exp(n, u):
                    act.wait_ge(s_read, n + 1)
                    act.activation(prob[u][0:S], prob[u][0:S], ACT.Exp, scale=1.0 / float(HD) ** 0.5).then_inc(exp_done, 1)

                def copy_v(n, u):
                    act.wait_ge(v_mm, n + 1)
                    act.activation(va[u][0:S, :, 0:HD], pj[0:S, 0:D].rearrange("p (h w) -> p h w", w=HD), ACT.Copy).then_inc(v_read, 1)

                def copy_out(n):
                    act.wait_ge(ot_mm, n + 2)
                    act.activation(self.oT[:, :, bass.ds(n * S + OPAD, S)], ov_turned, ACT.Copy).then_inc(ot_read, 1)

                def step_of(n, i, u, ahead_s, ahead_v):
                    for g in range(4):
                        if g == 2:
                            copy_out(n - 1)
                        act.wait_ge(pt_mm[u], i * 4 + g + 1)
                        if g == 0:
                            act.wait_ge(pv_mm, n)
                        act.activation(pt[0:S, g], tp[g % 2][0:S, 0:H2 * S].rearrange("p (j s) -> p j s", s=S), ACT.Copy).then_inc(pt_read[g % 2], 1)
                    if ahead_s:
                        exp(n + 1, 1 - u)
                    if ahead_v:
                        act.wait_ge(pv_mm, n + 1)
                        copy_v(n + 2, u)

                act.wait_ge(preset, 3)
                copy_v(0, 0)
                copy_v(1, 1)
                exp(0, 0)
                with act.Fori(0, NB // 2 - 1) as i:
                    for u in range(2):
                        step_of(i * 2 + u, i, u, True, True)
                step_of(NB - 2, NB // 2 - 1, 0, True, False)
                step_of(NB - 1, NB // 2 - 1, 1, False, False)
                copy_out(NB - 1)

    def project(self, rep, w, bias, acc, load=None, cut=()):
        nc, m, sem = self.nc, self.mem, self.sem
        m.at(self.work_at)
        o = [m.take(C, GW) for _ in range(2)]
        staged, biased, mm, added = sem("o_staged", 2), sem("acc_biased", 2), sem("wo_mm", 2), sem("wo_added", 2)
        I = NG // 2
        B = rep * I
        with ExitStack() as ctx:
            ps = [ctx.enter_context(nc.psum_tensor(f"wo{rep}_{u}", [P, 1024], F32)) for u in range(2)]
            block = ctx.enter_context(nc.Block())

            if load is not None:
                @block.sync
                def _(sp):
                    load(sp)

            @block.gpsimd
            def _(pool):
                with pool.Fori(0, I) as i:
                    for u in range(2):
                        pool.tensor_tensor(three(acc, i, u), three(acc, i, u), spread(bias, G), ALU.add).then_inc(biased[u], 1)

            @block.scalar
            def _(act):
                with act.Fori(0, I) as i:
                    for u in range(2):
                        act.wait_ge(mm[u], B + i)
                        act.activation(o[u], self.oT[:, :, bass.ds(i * (2 * GW) + (OPAD + GW * u), GW)], ACT.Copy).then_inc(staged[u], 1)

            @block.tensor
            def _(pe):
                with pe.Fori(0, I) as i:
                    for u in range(2):
                        pe.wait_ge(staged[u], B + i + 1)
                        pe.wait_ge(added[u], B + i)
                        for j in range(G):
                            for c in range(C):
                                last = pe.matmul(ps[u][:, j * D:(j + 1) * D], o[u][:, c, j * P:(j + 1) * P], w[:, c, :],
                                                 start=(c == 0), stop=(c == C - 1))
                        last.then_inc(mm[u], 1)

            @block.vector
            def _(dve):
                for x, hi in cut:
                    leading(dve, hi, x)
                with dve.Fori(0, I) as i:
                    for u in range(2):
                        dve.wait_ge(mm[u], B + i + 1)
                        dve.wait_ge(biased[u], B + i + 1)
                        dve.tensor_tensor(three(acc, i, u), ps[u][:, 0:G * D].rearrange("p (j d) -> p j d", d=D),
                                          three(acc, i, u), ALU.add).then_inc(added[u], 1)
                        dve.wait_ge(added[u], B + i + 1)
                        self.tile_stats(dve, acc, i, u)
        self.stats_count += NT

    def choose(self, scores, first, second, best, tmp, dve, link):
        rank = self.rank.unsqueeze(1).to_broadcast([P, NT, E])
        for k, hot in enumerate((first, second)):
            link(dve.tensor_reduce(best[k], scores, AX_X, ALU.max))
            link(dve.tensor_tensor(tmp, scores, inner(best[k], E), ALU.is_equal))
            link(dve.tensor_tensor(tmp, tmp, rank, ALU.mult))
            link(dve.tensor_reduce(self.top_rank, tmp, AX_X, ALU.max))
            link(dve.tensor_tensor(hot, inner(self.top_rank, E), rank, ALU.is_equal))
            if k == 0:
                link(dve.tensor_scalar(tmp, hot, -BIG, None, ALU.mult))
                link(dve.tensor_tensor(scores, scores, tmp, ALU.add))

    def route_first(self):
        nc, m, sem = self.nc, self.mem, self.sem
        m.at(self.work_at)
        m.take(NT, E + 1)
        self.gates = m.take(NT, E + 1)
        kept = m.pos
        tmp, first, second = m.take(NT, E), m.take(NT, E), m.take(NT, E)
        best = [m.take(NT) for _ in range(2)]
        total = m.take(NT)
        self.route_end = kept
        exped, step, done = sem("route_exp"), sem("route_step"), sem("gates_ready")
        lg = self.lg
        with nc.Block() as block:
            @block.gpsimd
            def _(pool):
                pool.tensor_tensor(self.e1_lo, self.e1, self.e1_hi.bitcast(F32), ALU.subtract)
                pool.tensor_tensor(self.e2_lo, self.e2, self.e2_hi.bitcast(F32), ALU.subtract)

            @block.scalar
            def _(act):
                act.activation(lg, lg, ACT.Exp, scale=-1.0).then_inc(exped, 1)

            @block.vector
            def _(dve):
                link = Steps(dve, step, 0)
                link(dve.memset(self.gates, 1.0))
                dve.wait_ge(exped, 1)
                link(dve.tensor_scalar(lg, lg, 1.0, None, ALU.add))
                link(dve.reciprocal(lg, lg))
                link(dve.tensor_scalar(lg, lg, self.route_scale[:, 0:1], None, ALU.mult))
                self.choose(lg, first, second, best, tmp, dve, link)
                link(dve.tensor_tensor(total, best[0], best[1], ALU.add))
                link(dve.reciprocal(total, total))
                for b, hot in zip(best, (first, second)):
                    link(dve.tensor_tensor(b, b, total, ALU.mult))
                    link(dve.tensor_tensor(hot, hot, inner(b, E), ALU.mult))
                link(dve.tensor_tensor(self.gates[:, :, 0:E], first, second, ALU.add))

    def experts(self):
        nc, m, sem = self.nc, self.mem, self.sem
        X = E + 1
        R = 3
        e1_hi, e2_hi = self.e1_hi, self.e2_hi
        m.at(self.route_end)
        x_hi = [m.take_rounded(C, GW) for _ in range(2)]
        raw = [m.take(GW) for _ in range(R)]
        hi, lo = ([m.take_rounded(GW) for _ in range(R)] for _ in range(2))
        gs = [m.take(G, X) for _ in range(2)]
        gt = [m.take(GW) for _ in range(2)]
        e2_b = m.take(D)
        b_in, stats_done = sem("e2_b_in"), sem("stats_done")
        x_cut, x_split = sem("ex_x_cut"), sem("ex_x_split")
        gs_ready, gt_mm, gt_ready = sem("gate_staged"), sem("gate_turned"), sem("gate_copied")
        up_mm, gelu, cut, split = sem("up_mm", R), sem("gelu_done", R), sem("hidden_cut", R), sem("hidden_split", R)
        po_mm, po_read = sem("down_mm", G), sem("down_read", G)
        I = NG // 2
        assert X % R == 0

        def nth(it, e):
            return it * (X // R) + (e // R + 1)

        with ExitStack() as ctx:
            up = [ctx.enter_context(nc.psum_tensor(f"up{r}", [P, 512], F32)) for r in range(R)]
            po = [ctx.enter_context(nc.psum_tensor(f"down{j}", [P, 512], F32)) for j in range(G)]
            tg = ctx.enter_context(nc.psum_tensor("turned_gate", [P, 512], F32))
            block = ctx.enter_context(nc.Block())

            def x_group(x, i, u, following, c):
                return x[:, c, bass.ds(i * (2 * GW) + GW * (u + following), GW)]

            @block.sync
            def _(sp):
                sp.dma_start(e2_b[0:X], self.t["e2_b"]).then_inc(b_in, 16)

            @block.tensor
            def _(pe):
                def rise(i, u, e, following=False):
                    it = i * 2 + u + following
                    r = e % R
                    if e == 0:
                        pe.wait_ge(x_split, (it + 1) * C)
                    pe.wait_ge(gelu[r], nth(it, e) - 1)
                    for c in range(C):
                        last = product(pe, up[r][:, 0:GW], (e1_hi[:, e, c, :], self.e1_lo[:, e, c, :]),
                                       (x_hi[u ^ following][:, c, :], x_group(self.xT_lo, i, u, following, c)), c == 0, c == C - 1)
                    last.then_inc(up_mm[r], 1)

                def fall(i, u, e):
                    it = i * 2 + u
                    r = e % R
                    pe.wait_ge(split[r], nth(it, e))
                    for j in range(G):
                        pe.wait_ge(po_read[j], it * X + e)
                        if e == X - 1:
                            pe.matmul(po[j][:, 0:D], gt[u][0:X, j * P:(j + 1) * P], e2_b[0:X, :], start=True, stop=False)
                        last = product(pe, po[j][:, 0:D], (hi[r][:, j * P:(j + 1) * P], lo[r][:, j * P:(j + 1) * P]),
                                       (e2_hi[:, e, :], self.e2_lo[:, e, :]), e < X - 1, True)
                        last.then_inc(po_mm[j], 1)

                pe.wait_ge(b_in, 16)
                for e in range(R):
                    rise(0, 0, e)
                with pe.Fori(0, I) as i:
                    for u in range(2):
                        it = i * 2 + u
                        for e in range(X):
                            fall(i, u, e)
                            rise(i, u, (e + R) % X, e + R >= X)
                            if e == 2:
                                pe.wait_ge(gs_ready, it + 1)
                                pe.wait_ge(gt_ready, it)
                                for j in range(G):
                                    last = pe.transpose(tg[0:X, j * P:(j + 1) * P], gs[u][:, j, :], self.ident)
                                last.then_inc(gt_mm, 1)
                            if e == X - 2:
                                pe.wait_ge(gt_ready, it + 1)

            @block.scalar
            def _(act):
                def hidden(i, u, e, following=False):
                    it = i * 2 + u + following
                    r = e % R
                    act.wait_ge(up_mm[r], nth(it, e))
                    act.wait_ge(split[r], nth(it, e) - 1)
                    act.activation(raw[r], up[r][:, 0:GW], ACT.Gelu, bias=self.e1_b[:, e:e + 1]).then_inc(gelu[r], 1)

                for e in range(R):
                    hidden(0, 0, e)
                with act.Fori(0, I) as i:
                    for u in range(2):
                        for e in range(X):
                            hidden(i, u, (e + R) % X, e + R >= X)

            @block.gpsimd
            def _(pool):
                def split_x(i, u, following, c):
                    it = i * 2 + u + following
                    pool.wait_ge(x_cut, it * C + c + 1)
                    pool.tensor_tensor(x_group(self.xT_lo, i, u, following, c), x_group(self.xT, i, u, following, c),
                                       x_hi[u ^ following][:, c, :].bitcast(F32), ALU.subtract).then_inc(x_split, 1)

                def split_hidden(i, u, e, following=False):
                    r = e % R
                    pool.wait_ge(cut[r], nth(i * 2 + u + following, e))
                    pool.tensor_tensor(lo[r], raw[r], hi[r].bitcast(F32), ALU.subtract).then_inc(split[r], 1)

                for c in range(C):
                    split_x(0, 0, False, c)
                for e in range(R):
                    split_hidden(0, 0, e)
                with pool.Fori(0, I) as i:
                    for u in range(2):
                        for e in range(X):
                            if e in (1, 3):
                                split_x(i, u, True, e // 2)
                            split_hidden(i, u, (e + R) % X, e + R >= X)

            @block.vector
            def _(dve):
                def cut_x(i, u, following, c):
                    leading(dve, x_hi[u ^ following][:, c, :], x_group(self.xT, i, u, following, c)).then_inc(x_cut, 1)

                def cut_hidden(i, u, e, following=False):
                    it = i * 2 + u + following
                    r = e % R
                    dve.wait_ge(gelu[r], nth(it, e))
                    leading(dve, hi[r], raw[r]).then_inc(cut[r], 1)

                for c in range(C):
                    cut_x(0, 0, False, c)
                for e in range(R):
                    cut_hidden(0, 0, e)
                with dve.Fori(0, I) as i:
                    for u in range(2):
                        it = i * 2 + u
                        dve.wait_ge(gt_mm, it)
                        dve.tensor_copy(gs[u], self.gates[:, bass.ds(i * (2 * G) + G * u, G), :]).then_inc(gs_ready, 1)
                        dve.wait_ge(gs_ready, it + 1)
                        for e in range(X):
                            for j in range(G):
                                dve.wait_ge(po_mm[j], it * X + e + 1)
                                acc = one(self.h, i, u, j)
                                dve.wait_ge(po_read[j], it * X + e)
                                dve.scalar_tensor_tensor(out=acc, in0=po[j][:, 0:D], scalar=gs[u][:, j, e:e + 1],
                                                         in1=acc, op0=ALU.mult, op1=ALU.add).then_inc(po_read[j], 1)
                            cut_hidden(i, u, (e + R) % X, e + R >= X)
                            if e in (0, 2):
                                dve.wait_ge(up_mm[R - 1], nth(it - 1, X - 1))
                                cut_x(i, u, True, e // 2)
                            if e == 5:
                                dve.wait_ge(gt_mm, it + 1)
                                dve.tensor_copy(gt[u][0:X], tg[0:X, 0:GW]).then_inc(gt_ready, 1)
                        for j in range(G):
                            dve.wait_ge(po_read[j], (it + 1) * X)
                            dve.bn_stats(one(self.stats, i, u, j), one(self.h, i, u, j)).then_inc(stats_done, 1)
        self.stats_count += NT

    def linear_attention(self):
        nc, m, sem = self.nc, self.mem, self.sem
        NP = NB // 2
        QK = 2 * D
        m.at(self.la_at)
        qb = m.take(2, QK)
        kvm = m.take(2, C, P)
        qT = m.take(C, 2, S)
        x_hi, x_lo = ([m.take_rounded(C, PAIR) for _ in range(2)] for _ in range(2))
        m.at(self.work_at)
        el = [m.take(2, QK) for _ in range(2)]
        ex = [m.take(2, QK) for _ in range(2)]
        vb = [m.take(2, D) for _ in range(2)]
        nrm, var, tmp = m.take(2, 2 * HEADS), m.take(2, 2 * HEADS), m.take(2, 2 * HEADS)
        x_cut = sem("la_x_cut")
        staged, qk_mm, v_mm = sem("la_x_staged"), sem("la_qk_mm"), sem("la_v_mm")
        qk_read, v_read = sem("la_qk_read"), sem("la_v_read")
        e_done, r_done, el_done, sq_done = sem("la_exp"), sem("la_relu"), sem("la_elu"), sem("la_square")
        rn_done, n_done, tkv_mm, kv_read = sem("la_norms"), sem("la_unit"), sem("la_kv_mm"), sem("la_kv_read")
        qT_read, c_mm, c_read, step, zeroed = sem("la_q_copied"), sem("la_ctx_mm"), sem("la_ctx_copied"), sem("la_step"), sem("la_zeroed")
        per = 2 * RSQRT_PARTS

        with ExitStack() as ctx:
            pq = [ctx.enter_context(nc.psum_tensor(f"la_qk{u}", [P, 2, 512], F32)) for u in range(2)]
            pv = ctx.enter_context(nc.psum_tensor("la_v", [P, 2, D], F32))
            pkv = ctx.enter_context(nc.psum_tensor("la_kv", [P, 2, C, P], F32))
            pt = ctx.enter_context(nc.psum_tensor("la_qT", [P, 512], F32))
            pc = ctx.enter_context(nc.psum_tensor("la_ctx", [P, 512], F32))
            block = ctx.enter_context(nc.Block())

            @block.gpsimd
            def _(pool):
                def stage(p, u):
                    pool.wait_ge(x_cut, p + 1)
                    pool.tensor_tensor(x_lo[u], self.xT[:, :, bass.ds(p * PAIR, PAIR)], x_hi[u].bitcast(F32), ALU.subtract).then_inc(staged, 1)

                pool.memset(el[1][0:S], 0.0).then_inc(zeroed, 1)
                pool.memset(vb[1][0:S], 0.0).then_inc(zeroed, 1)
                stage(0, 0)
                stage(1, 1)
                with pool.Fori(0, NP // 2) as i:
                    for u in range(2):
                        p = i * 2 + u
                        stage(p + 2, u)
                        pool.wait_ge(rn_done, p + 1)
                        heads = el[u][0:S].rearrange("p b (h w) -> p (b h) w", w=HD)
                        pool.tensor_tensor(heads, heads, inner(nrm[0:S].rearrange("p b h -> p (b h)"), HD), ALU.mult).then_inc(n_done, 1)

            @block.tensor
            def _(pe):
                def proj(p, u):
                    pe.wait_ge(staged, p + 1)
                    for b in range(2):
                        for c in range(C):
                            last = product(pe, pq[u][0:S, b, :], (x_hi[u][:, c, b * S:(b + 1) * S], x_lo[u][:, c, b * S:(b + 1) * S]),
                                           (self.wqk1_hi[:, c, :], self.wqk1_lo[:, c, :]), c == 0, c == C - 1)
                    last.then_inc(qk_mm, 1)
                    pe.wait_ge(v_read, p * 2)
                    for b in range(2):
                        for c in range(C):
                            last = product(pe, pv[0:S, b, :], (x_hi[u][:, c, b * S:(b + 1) * S], x_lo[u][:, c, b * S:(b + 1) * S]),
                                           (self.wv1_hi[:, c, :], self.wv1_lo[:, c, :]), c == 0, c == C - 1)
                    last.then_inc(v_mm, 1)

                def turn_kv(p, u):
                    pe.wait_ge(n_done, p + 1)
                    pe.wait_ge(v_read, p * 2 + 2)
                    for c in range(C):
                        for b in range(2):
                            pe.transpose(pt[:, (c * 2 + b) * S:(c * 2 + b + 1) * S], el[u][0:S, b, c * P:(c + 1) * P], self.ident[0:S, 0:S])
                    for b in range(2):
                        for c in range(C):
                            last = pe.matmul(pkv[:, b, c, :], el[u][0:S, b, D + c * P:D + (c + 1) * P], vb[u][0:S, b, c * P:(c + 1) * P],
                                             start=True, stop=True)
                    last.then_inc(tkv_mm, 1)

                def context(p):
                    pe.wait_ge(kv_read, p * 2 + 4)
                    pe.wait_ge(qT_read, p + 2)
                    pe.wait_ge(c_read, p + 1)
                    for c in range(C):
                        for b in range(2):
                            last = pe.matmul(pc[:, (c * 2 + b) * S:(c * 2 + b + 1) * S], kvm[:, b, c, :], qT[:, c, b, :], start=True, stop=True)
                    last.then_inc(c_mm, 1)

                proj(0, 0)
                proj(1, 1)
                pe.wait_ge(zeroed, 2)
                with pe.Fori(0, NP // 2) as i:
                    for u in range(2):
                        p = i * 2 + u
                        turn_kv(p - 1, 1 - u)
                        pe.wait_ge(qk_read, p + 1)
                        proj(p + 2, u)
                        context(p - 1)
                turn_kv(NP - 1, 1)
                context(NP - 1)

            @block.vector
            def _(dve):
                def bias_qk(p, u):
                    dve.wait_ge(qk_mm, p + 1)
                    dve.wait_ge(e_done, p)
                    dve.wait_ge(el_done, p)
                    dve.tensor_tensor(qb[0:S], pq[u][0:S], spread(self.bqk1, 2)[0:S], ALU.add).then_inc(qk_read, 1)

                def bias_v(p, u, b):
                    dve.wait_ge(v_mm, p + 1)
                    dve.wait_ge(tkv_mm, p)
                    dve.tensor_tensor(vb[u][0:S, b], pv[0:S, b], self.bv1[0:S], ALU.add).then_inc(v_read, 1)

                def mask(b):
                    dve.tensor_tensor(kvm[:, b], pkv[:, b], self.head_mask.unsqueeze(1).to_broadcast([P, C, P]), ALU.mult).then_inc(kv_read, 1)

                def cut_x(p, u):
                    leading(dve, x_hi[u], self.xT[:, :, bass.ds(p * PAIR, PAIR)]).then_inc(x_cut, 1)

                for u in range(2):
                    cut_x(u, u)
                dve.wait_ge(zeroed, 2)
                for b in range(2):
                    bias_v(0, 0, b)
                bias_qk(0, 0)
                with dve.Fori(0, NP // 2) as i:
                    link = Steps(dve, step, i * per)
                    for u in range(2):
                        p = i * 2 + u
                        cut_x(p + 2, u)
                        dve.wait_ge(e_done, p + 1)
                        dve.wait_ge(qk_read, p + 1)
                        dve.wait_ge(tkv_mm, p)
                        dve.scalar_tensor_tensor(out=el[u][0:S].rearrange("p b d -> p (b d)"), in0=ex[u][0:S].rearrange("p b d -> p (b d)"),
                                                 scalar=-1.0, in1=qb[0:S].rearrange("p b d -> p (b d)"), op0=ALU.add, op1=ALU.max).then_inc(el_done, 1)
                        bias_qk(p + 1, 1 - u)
                        dve.wait_ge(sq_done, p + 1)
                        dve.wait_ge(n_done, p)
                        link.mark(dve.tensor_reduce(var[0:S], ex[u][0:S].rearrange("p b (h w) -> p b h w", w=HD), AX_X, ALU.add))
                        for k in range(RSQRT_PARTS):
                            if k in (0, 1):
                                bias_v(p + 1, 1 - u, k)
                            if k == 2:
                                dve.wait_ge(tkv_mm, p + 1)
                                dve.wait_ge(c_mm, p)
                            if k in (2, 3):
                                mask(k - 2)
                            link.wait()
                            ins = rsqrt_part(dve, k, var[0:S], nrm[0:S], tmp[0:S])
                            if k == RSQRT_PARTS - 1:
                                ins.then_inc(rn_done, 1)
                            else:
                                link.mark(ins)
                    assert link.n == per, (link.n, per)
                dve.wait_ge(tkv_mm, NP + 1)
                dve.wait_ge(c_mm, NP)
                for b in range(2):
                    mask(b)

            @block.scalar
            def _(act):
                def exp(p, u):
                    act.wait_ge(qk_read, p + 1)
                    act.activation(ex[u][0:S], qb[0:S], ACT.Relu, scale=-1.0).then_inc(r_done, 1)
                    act.wait_ge(r_done, p + 1)
                    act.activation(ex[u][0:S], ex[u][0:S], ACT.Exp, scale=-1.0).then_inc(e_done, 1)

                def copy_q(p):
                    act.wait_ge(tkv_mm, p + 2)
                    act.wait_ge(c_mm, p + 1)
                    act.activation(qT.rearrange("p c b s -> p (c b s)"), pt[:, 0:C * PAIR], ACT.Copy).then_inc(qT_read, 1)

                def copy_out(p):
                    act.wait_ge(c_mm, p + 2)
                    act.activation(self.oT[:, :, bass.ds(p * PAIR + OPAD, PAIR)], pc[:, 0:C * PAIR].rearrange("p (c s) -> p c s", c=C),
                                   ACT.Copy).then_inc(c_read, 1)

                def square(p, u):
                    act.wait_ge(el_done, p + 1)
                    act.activation(ex[u][0:S], el[u][0:S], ACT.Square).then_inc(sq_done, 1)

                def step_of(p, u, ahead):
                    act.wait_ge(rn_done, p)
                    exp(p + 1, 1 - u)
                    copy_q(p - 1)
                    if ahead:
                        square(p + 1, 1 - u)
                    copy_out(p - 1)

                exp(0, 0)
                square(0, 0)
                with act.Fori(0, NP // 2 - 1) as i:
                    for u in range(2):
                        step_of(i * 2 + u, u, True)
                step_of(NP - 2, 0, True)
                step_of(NP - 1, 1, False)
                copy_q(NP - 1)
                copy_out(NP - 1)

    def feed_forward(self):
        nc, m, sem = self.nc, self.mem, self.sem
        R = 4
        f1_hi, f2_hi = self.f1_hi, self.f2_hi
        m.at(self.work_at)
        x_hi = [m.take_rounded(C, GW) for _ in range(2)]
        raw = [m.take(GW) for _ in range(R)]
        hi, lo = ([m.take_rounded(GW) for _ in range(R)] for _ in range(2))
        x_cut, x_split, biased, stats_done = sem("ff_x_cut"), sem("ff_x_split"), sem("ff_biased"), sem("stats_done")
        up_mm, gelu, cut, split = sem("ff_up_mm", R), sem("ff_gelu", R), sem("ff_hidden_cut", R), sem("ff_hidden_split", R)
        down_mm, down_read = sem("ff_down_mm", G), sem("ff_down_read", G)
        I = NG // 2
        assert KF % R == 0

        def nth(it, k):
            return it * (KF // R) + (k // R + 1)

        with ExitStack() as ctx:
            up = [ctx.enter_context(nc.psum_tensor(f"ff_up{r}", [P, 512], F32)) for r in range(R)]
            po = [ctx.enter_context(nc.psum_tensor(f"ff_down{j}", [P, 512], F32)) for j in range(G)]
            block = ctx.enter_context(nc.Block())

            def x_group(x, i, u, following, c):
                return x[:, c, bass.ds(i * (2 * GW) + GW * (u + following), GW)]

            @block.tensor
            def _(pe):
                def rise(i, u, k, following=False):
                    it = i * 2 + u + following
                    r = k % R
                    if k == 0:
                        pe.wait_ge(x_split, (it + 1) * C)
                    pe.wait_ge(gelu[r], nth(it, k) - 1)
                    for c in range(C):
                        last = product(pe, up[r][:, 0:GW], (f1_hi[:, c, k * P:(k + 1) * P], self.f1_lo[:, c, k * P:(k + 1) * P]),
                                       (x_hi[u ^ following][:, c, :], x_group(self.xT_lo, i, u, following, c)), c == 0, c == C - 1)
                    last.then_inc(up_mm[r], 1)

                def fall(i, u, k):
                    it = i * 2 + u
                    r = k % R
                    pe.wait_ge(split[r], nth(it, k))
                    for j in range(G):
                        if k == 0:
                            pe.wait_ge(down_read[j], it)
                        last = product(pe, po[j][:, 0:D], (hi[r][:, j * P:(j + 1) * P], lo[r][:, j * P:(j + 1) * P]),
                                       (f2_hi[:, k, :], self.f2_lo[:, k, :]), k == 0, k == KF - 1)
                        last.then_inc(down_mm[j], 1)

                for k in range(R):
                    rise(0, 0, k)
                with pe.Fori(0, I) as i:
                    for u in range(2):
                        for k in range(KF):
                            fall(i, u, k)
                            rise(i, u, (k + R) % KF, k + R >= KF)

            @block.scalar
            def _(act):
                def hidden(i, u, k, following=False):
                    it = i * 2 + u + following
                    r = k % R
                    act.wait_ge(up_mm[r], nth(it, k))
                    act.wait_ge(split[r], nth(it, k) - 1)
                    act.activation(raw[r], up[r][:, 0:GW], ACT.Gelu, bias=self.f1_b[:, k:k + 1]).then_inc(gelu[r], 1)

                for k in range(R):
                    hidden(0, 0, k)
                with act.Fori(0, I) as i:
                    for u in range(2):
                        for k in range(KF):
                            hidden(i, u, (k + R) % KF, k + R >= KF)

            @block.gpsimd
            def _(pool):
                def split_x(i, u, following, c):
                    it = i * 2 + u + following
                    pool.wait_ge(x_cut, it * C + c + 1)
                    pool.tensor_tensor(x_group(self.xT_lo, i, u, following, c), x_group(self.xT, i, u, following, c),
                                       x_hi[u ^ following][:, c, :].bitcast(F32), ALU.subtract).then_inc(x_split, 1)

                def split_hidden(i, u, k, following=False):
                    r = k % R
                    pool.wait_ge(cut[r], nth(i * 2 + u + following, k))
                    pool.tensor_tensor(lo[r], raw[r], hi[r].bitcast(F32), ALU.subtract).then_inc(split[r], 1)

                for c in range(C):
                    split_x(0, 0, False, c)
                for k in range(R):
                    split_hidden(0, 0, k)
                with pool.Fori(0, I) as i:
                    for u in range(2):
                        for k in range(KF):
                            if k in (0, 1):
                                split_x(i, u, True, k)
                            if k == 4:
                                pool.tensor_tensor(three(self.xn, i, u), three(self.xn, i, u), spread(self.f2_b, G), ALU.add).then_inc(biased, 1)
                            split_hidden(i, u, (k + R) % KF, k + R >= KF)

            @block.vector
            def _(dve):
                def cut_x(i, u, following, c):
                    leading(dve, x_hi[u ^ following][:, c, :], x_group(self.xT, i, u, following, c)).then_inc(x_cut, 1)

                def cut_hidden(i, u, k, following=False):
                    it = i * 2 + u + following
                    r = k % R
                    dve.wait_ge(gelu[r], nth(it, k))
                    dve.wait_ge(down_mm[G - 1], (i * 2 + u) * KF + (k + KF * following - R + 1))
                    leading(dve, hi[r], raw[r]).then_inc(cut[r], 1)

                for c in range(C):
                    cut_x(0, 0, False, c)
                for k in range(R):
                    dve.wait_ge(gelu[k], 1)
                    leading(dve, hi[k], raw[k]).then_inc(cut[k], 1)
                with dve.Fori(0, I) as i:
                    for u in range(2):
                        it = i * 2 + u
                        for k in range(KF):
                            if k in (0, 1):
                                dve.wait_ge(up_mm[R - 1], nth(it - 1, KF - 1))
                                cut_x(i, u, True, k)
                            cut_hidden(i, u, (k + R) % KF, k + R >= KF)
                        dve.wait_ge(biased, it + 1)
                        for j in range(G):
                            dve.wait_ge(down_mm[j], (it + 1) * KF)
                            acc = one(self.xn, i, u, j)
                            dve.tensor_tensor(acc, po[j][:, 0:D], acc, ALU.add).then_inc(down_read[j], 1)
                        for j in range(G):
                            dve.wait_ge(down_read[j], it + 1)
                            dve.bn_stats(one(self.stats, i, u, j), one(self.xn, i, u, j)).then_inc(stats_done, 1)
        self.stats_count += NT

    def route_second(self):
        nc, m, sem, t = self.nc, self.mem, self.sem, self.t
        m.at(self.keep_at)
        self.source, self.target = m.take(XBLK).bitcast(U32), m.take(XBLK).bitcast(U32)
        self.weight = [m.take(NT) for _ in range(2)]
        self.owner = m.take(XBLK).bitcast(U32)
        m.at(self.route_at)
        tmp, first, second, place = m.take(NT, E), m.take(NT, E), m.take(NT, E), m.take(NT, E)
        total, cnt, blocks, base, fin = m.take(NT), m.take(E), m.take(E), m.take(E), m.take(E)
        over, before, past = m.take(E, NT), m.take(E, E), m.take(XBLK, E)
        own = m.take(XBLK)
        hits = m.take(NT * E // 2).bitcast(mybir.dt.bfloat16).rearrange("p (a e) -> p a e", e=E)
        tri = m.take(P // 2).bitcast(mybir.dt.bfloat16)
        ones = m.take(P // 2).bitcast(mybir.dt.bfloat16)
        consts = self.route_consts
        slot, blk, match = m.take(NT), m.take(NT), m.take(NT, XBLK)
        at = [m.take(NT) for _ in range(2)]
        at_hot = [m.take(NT * P // 2).bitcast(mybir.dt.bfloat16).rearrange("p (a n) -> p a n", n=P) for _ in range(2)]
        rows = [m.take(NT * XBLK).bitcast(mybir.dt.bfloat16).rearrange("p (a g b) -> p a g b", g=2, b=XBLK) for _ in range(2)]
        row = m.take(XBLK)
        assert m.pos <= self.route_consts_at
        exped, step = sem("route2_exp"), sem("route2_step")
        hit, ranked, hot_ready, table_mm = sem("hits_ready"), sem("ranks_mm"), sem("slot_rows_ready"), sem("slot_table_mm")
        xn_out = sem("xn_in_dram")
        self.xn_rows = self.dram("xn_rows", [NT * P, D])
        lg = self.lg
        with ExitStack() as ctx:
            rk = ctx.enter_context(nc.psum_tensor("ranks", [P, NT, E], F32))
            ct = ctx.enter_context(nc.psum_tensor("counts", [P, 512], F32))
            table = ctx.enter_context(nc.psum_tensor("slot_table", [P, 2, XBLK], F32))
            block = ctx.enter_context(nc.Block())

            @block.sync
            def _(sp):
                sp.dma_start(self.xn_rows.rearrange("(a p) d -> p a d", p=P), self.xn).then_inc(xn_out, 16)
                sp.wait_ge(xn_out, 16)

            @block.scalar
            def _(act):
                act.wait_ge(step, 2)
                act.activation(lg, lg, ACT.Exp).then_inc(exped, 1)

            @block.vector
            def _(dve):
                link = Steps(dve, step, 0)
                link(dve.tensor_reduce(total, lg, AX_X, ALU.max))
                link(dve.tensor_tensor(lg, lg, inner(total, E), ALU.subtract))
                link(dve.tensor_copy(tri, consts["tri"]))
                link(dve.memset(ones, 1.0))
                dve.wait_ge(exped, 1)
                link(dve.tensor_reduce(total, lg, AX_X, ALU.add))
                link(dve.reciprocal(total, total))
                link(dve.tensor_tensor(lg, lg, inner(total, E), ALU.mult))
                self.choose(lg, first, second, self.weight, tmp, dve, link)
                link(dve.tensor_tensor(tmp, first, second, ALU.add))
                dve.tensor_tensor(hits, tmp, inner(consts["valid"], E), ALU.mult).then_inc(hit, 1)
                link(dve.tensor_tensor(total, self.weight[0], self.weight[1], ALU.add))
                link(dve.tensor_scalar(total, total, 1e-8, None, ALU.add))
                link(dve.reciprocal(total, total))
                for w in self.weight:
                    link(dve.tensor_tensor(w, w, total, ALU.mult))
                dve.wait_ge(ranked, 1)
                link(dve.tensor_copy(cnt, ct[:, 0:E]))
                link(dve.tensor_tensor(over, inner(cnt, NT), spread(consts["steps"], E), ALU.is_gt))
                link(dve.tensor_reduce(blocks, over, AX_X, ALU.add))
                link(dve.tensor_tensor(before, consts["lower"], spread(blocks, E), ALU.mult))
                link(dve.tensor_reduce(base, before, AX_X, ALU.add))
                link(dve.tensor_tensor(fin, base, blocks, ALU.add))
                link(dve.tensor_tensor(past, inner(consts["blocks"], E), spread(fin, XBLK), ALU.is_ge))
                link(dve.tensor_reduce(own, past, AX_X, ALU.add))
                link(dve.tensor_scalar(self.owner, own, float(E - 1), None, ALU.min))
                link(dve.tensor_scalar(base, base, float(P), None, ALU.mult))
                link(dve.tensor_tensor(place, rk[:, :, :], spread(base, NT), ALU.add))
                for k, hot in enumerate((first, second)):
                    link(dve.tensor_tensor(tmp, place, hot, ALU.mult))
                    link(dve.tensor_reduce(slot, tmp, AX_X, ALU.add))
                    link(dve.tensor_copy(at[k].bitcast(I32), slot))
                    link(dve.tensor_scalar(at[k].bitcast(I32), at[k].bitcast(I32), P - 1, None, ALU.bitwise_and))
                    link(dve.tensor_copy(at[k], at[k].bitcast(I32)))
                    link(dve.tensor_tensor(blk, slot, at[k], ALU.subtract))
                    link(dve.tensor_scalar(blk, blk, 1.0 / P, 1.0, ALU.mult, ALU.add))
                    link(dve.tensor_tensor(blk, blk, consts["valid"], ALU.mult))
                    link(dve.tensor_scalar(blk, blk, -1.0, None, ALU.add))
                    link(dve.tensor_tensor(match, inner(blk, XBLK), spread(consts["blocks"], NT), ALU.is_equal))
                    dve.tensor_scalar(rows[k][:, :, 0, :], match, consts["row"][:, k:k + 1], None, ALU.mult).then_inc(hot_ready, 1)
                    dve.tensor_tensor(rows[k][:, :, 1, :], match, inner(consts["tile"], XBLK), ALU.mult).then_inc(hot_ready, 1)
                    dve.tensor_tensor(at_hot[k], inner(at[k], P), spread(consts["places"], NT), ALU.is_equal).then_inc(hot_ready, 1)
                    if k == 0:
                        dve.wait_ge(hot_ready, 3)
                dve.wait_ge(table_mm, 1)
                link(dve.tensor_copy(row, table[:, 0, :]))
                link(dve.scalar_tensor_tensor(out=row, in0=table[:, 1, :], scalar=2.0 * P, in1=row, op0=ALU.mult, op1=ALU.add))
                link(dve.tensor_copy(self.target, row))
                link(dve.tensor_scalar(row, row, -1.0, 0.0, ALU.add, ALU.max))
                link(dve.tensor_copy(self.source, row))
                link(dve.tensor_scalar(self.source, self.source, 1, None, ALU.logical_shift_right))

            @block.tensor
            def _(pe):
                pe.wait_ge(hit, 1)
                pe.matmul(rk[:, :, :], tri, hits, start=True, stop=False)
                for a in range(1, NT):
                    pe.matmul(rk[:, a:, :], ones, hits[:, 0:NT - a, :], start=False, stop=(a == NT - 1))
                for a in range(NT):
                    last = pe.matmul(ct[:, 0:E], ones, hits[:, a, :], start=(a == 0), stop=(a == NT - 1))
                last.then_inc(ranked, 1)
                for k in range(2):
                    pe.wait_ge(hot_ready, 3 * k + 3)
                    for a in range(NT):
                        last = pe.matmul(table[:, :, :], at_hot[k][:, a, :], rows[k][:, a], start=(k + a == 0), stop=(k == 1 and a == NT - 1))
                last.then_inc(table_mm, 1)

    def routed(self):
        nc, m, sem, t = self.nc, self.mem, self.sem, self.t
        HK = KF // 2
        m.at(self.xn_at)
        w2_hi, w2_lo = ([m.take_rounded(HK, D) for _ in range(2)] for _ in range(2))
        y = [m.take(D) for _ in range(2)]
        assert m.pos <= self.xn_at + NT * D
        m.at(self.route_at)
        w2_b = m.take(E, D)
        w1_b = m.take(E * KF)
        xg = [m.take(D) for _ in range(2)]
        xT = [m.take(C, P) for _ in range(2)]
        ws = [m.take(C, FF) for _ in range(2)]
        raw = [m.take(HK, P) for _ in range(2)]
        hi, lo = ([m.take_rounded(HK, P) for _ in range(2)] for _ in range(2))
        b_in, xg_in, tx_mm, xt_read = sem("moe_bias_in"), sem("slot_rows_in", 2), sem("slot_rows_turned"), sem("slot_rows_copied")
        ws_ready, up_mm, gl = sem("moe_w1_staged"), sem("moe_up_mm"), sem("moe_gelu", 2)
        h_cut, h_split, w2_cut, w2_split = sem("moe_hidden_cut"), sem("moe_hidden_split"), sem("moe_w2_cut"), sem("moe_w2_split")
        half_mm, down_mm, y_read, stored = sem("moe_half_mm"), sem("moe_down_mm", 2), sem("moe_down_read"), sem("choices_stored", 2)
        self.choices = self.dram("choices", [1 + 2 * NT * P, D])

        def split_count(n, f):
            return n * 2 + f + 3

        with ExitStack() as ctx:
            px = ctx.enter_context(nc.psum_tensor("moe_xT", [P, 512], F32))
            p1 = [[ctx.enter_context(nc.psum_tensor(f"moe_up{v}{f}", [P, 512], F32)) for f in range(2)] for v in range(2)]
            p2 = ctx.enter_context(nc.psum_tensor("moe_down", [P, 512], F32))
            block = ctx.enter_context(nc.Block())

            def owner_of(eng, n):
                return eng.value_load(self.owner[0:1, bass.ds(n, 1)], min_val=0, max_val=E - 1)

            @block.sync
            def _(sp):
                sp.dma_start(w2_b, t["w2_b"].rearrange("p (e d) -> p e d", e=E)).then_inc(b_in, 16)
                sp.dma_start(w1_b, t["w1_b"]).then_inc(b_in, 16)

            @block.gpsimd
            def _(pool):
                def load(n):
                    pool.indirect_dma_start(out=xg[n % 2], out_offset=None, in_=self.xn_rows,
                                            in_offset=bass.IndirectOffsetOnAxis(ap=self.source[:, n:n + 1], axis=0)).then_inc(xg_in[n % 2], 16)

                def store(n):
                    pool.wait_ge(y_read, n + 1)
                    if n >= 1:
                        pool.wait_ge(stored[(n - 1) % 2], 16 * ((n - 1) // 2 + 1))
                    pool.indirect_dma_start(out=self.choices, out_offset=bass.IndirectOffsetOnAxis(ap=self.target[:, n:n + 1], axis=0),
                                            in_=y[n % 2], in_offset=None).then_inc(stored[n % 2], 16)

                load(0)
                load(1)
                for f in range(2):
                    pool.memset(raw[f], 0.0).then_inc(h_split, 1)
                for n in range(2):
                    pool.wait_ge(tx_mm, n + 1)
                    load(n + 2)
                for n in range(NBLK):
                    for f in range(2):
                        pool.wait_ge(h_cut, n * 2 + f + 1)
                        pool.tensor_tensor(lo[f], raw[f], hi[f].bitcast(F32), ALU.subtract).then_inc(h_split, 1)
                        if f == 0 and n + 4 < XBLK:
                            pool.wait_ge(tx_mm, n + 3)
                            load(n + 4)
                    if n >= 1:
                        store(n - 1)
                store(NBLK - 1)
                for u in range(2):
                    pool.wait_ge(stored[u], 16 * (NBLK // 2))
                    pool.wait_ge(xg_in[u], 16 * (XBLK // 2))

            @block.tensor
            def _(pe):
                def turn_x(n, i, u):
                    pe.wait_ge(xg_in[u], i * 16 + 16)
                    pe.wait_ge(xt_read, n)
                    for c in range(C):
                        last = pe.transpose(px[:, c * P:(c + 1) * P], xg[u][:, c * P:(c + 1) * P], self.ident)
                    last.then_inc(tx_mm, 1)

                def rise(n, u):
                    pe.wait_ge(xt_read, n + 1)
                    pe.wait_ge(ws_ready, n + 1)
                    for k in range(KF):
                        for c in range(C):
                            last = pe.matmul(p1[u][k // HK][:, (k % HK) * P:(k % HK + 1) * P], ws[u][:, c, k * P:(k + 1) * P],
                                             xT[u][:, c, :], start=(c == 0), stop=(c == C - 1))
                        if k % HK == HK - 1:
                            last.then_inc(up_mm, 1)

                turn_x(0, 0, 0)
                turn_x(1, 0, 1)
                rise(0, 0)
                with pe.Fori(0, NBLK // 2) as i:
                    for u in range(2):
                        n = i * 2 + u
                        turn_x(n + 2, i + 1, u)
                        rise(n + 1, 1 - u)
                        pe.wait_ge(y_read, n)
                        for f in range(2):
                            pe.wait_ge(h_split, split_count(n, f))
                            pe.wait_ge(w2_split, n * 2 + f + 1)
                            for k in range(HK):
                                last = product(pe, p2[:, 0:D], (hi[f][:, k, :], lo[f][:, k, :]), (w2_hi[f][:, k, :], w2_lo[f][:, k, :]),
                                               f + k == 0, f == 1 and k == HK - 1)
                            if f == 0:
                                last.then_inc(half_mm, 1)
                        last.then_inc(down_mm[u], 1)

            @block.vector
            def _(dve):
                dve.wait_ge(b_in, 32)
                dve.wait_ge(self.w2_in, 16 * 2)

                def split(n, f, e):
                    dve.wait_ge(gl[f], n * HK + HK)
                    leading(dve, hi[f], raw[f]).then_inc(h_cut, 1)
                    w2 = self.w2[:, bass.ds(e * KF + f * HK, HK), :]
                    leading(dve, w2_hi[f], w2).then_inc(w2_cut, 1)
                    dve.wait_ge(w2_cut, n * 2 + f + 1)
                    dve.tensor_tensor(w2_lo[f], w2, w2_hi[f].bitcast(F32), ALU.subtract).then_inc(w2_split, 1)

                split(0, 0, owner_of(dve, 0))
                with dve.Fori(0, NBLK // 2) as i:
                    for u in range(2):
                        n = i * 2 + u
                        e, following = owner_of(dve, n), owner_of(dve, n + 1)
                        dve.wait_ge(down_mm[1 - u], i + u)
                        split(n, 1, e)
                        dve.wait_ge(half_mm, n + 1)
                        split(n + 1, 0, following)
                        dve.wait_ge(down_mm[u], i + 1)
                        dve.wait_ge(stored[u], i * 16)
                        dve.tensor_tensor(y[u], p2[:, 0:D], w2_b[:, bass.ds(e, 1), :].rearrange("p a d -> p (a d)"), ALU.add).then_inc(y_read, 1)

            @block.scalar
            def _(act):
                def copy_x(n, u):
                    act.wait_ge(tx_mm, n + 1)
                    act.activation(xT[u], px[:, 0:D].rearrange("p (c n) -> p c n", c=C), ACT.Copy).then_inc(xt_read, 1)

                def stage(n, u):
                    e = owner_of(act, n)
                    act.activation(ws[u], self.w1[:, :, bass.ds(e * FF, FF)], ACT.Copy).then_inc(ws_ready, 1)

                act.wait_ge(self.w1_in, 16 * C)
                stage(0, 0)
                stage(1, 1)
                act.wait_ge(b_in, 32)
                copy_x(0, 0)
                copy_x(1, 1)

                def hidden(n, u, e, f):
                    act.wait_ge(up_mm, n * 2 + f + 1)
                    act.wait_ge(h_split, n * 2 + f + 1)
                    for k in range(HK):
                        act.activation(raw[f][:, k, :], p1[u][f][:, k * P:(k + 1) * P],
                                       ACT.Gelu_apprx_tanh, bias=w1_b[:, bass.ds(e * KF + f * HK + k, 1)]).then_inc(gl[f], 1)

                e = owner_of(act, 0)
                for f in range(2):
                    hidden(0, 0, e, f)
                with act.Fori(0, NBLK // 2) as i:
                    for u in range(2):
                        n = i * 2 + u
                        e = owner_of(act, n + 1)
                        copy_x(n + 2, u)
                        stage(n + 2, u)
                        for f in range(2):
                            hidden(n + 1, 1 - u, e, f)

    def combine(self):
        nc, m, sem = self.nc, self.mem, self.sem
        m.at(self.w1_at)
        got = m.take(NT, 2, D)
        parts = [(a, min(a + G, NT - 1)) for a in range(0, NT - 1, G)] + [(NT - 1, NT)]
        got_in, mixed, stored = sem("choice_in", len(parts)), sem("choice_mixed"), sem("out_stored")

        def tiles(a, b):
            n = P if b < NT else LAST
            return n, a * P, a * P + (b - a) * n

        with nc.Block() as block:
            @block.scalar
            def _(act):
                for k, (a, b) in enumerate(parts):
                    n, t0, t1 = tiles(a, b)
                    act.dma_start(got[0:n, a:b], self.choices[1 + 2 * t0:1 + 2 * t1, :].rearrange(
                        "(a p k) d -> p a k d", k=2, p=n)).then_inc(got_in[k], 16)

            @block.vector
            def _(dve):
                for k, (a0, a1) in enumerate(parts):
                    n = tiles(a0, a1)[0]
                    dve.wait_ge(got_in[k], 16)
                    for a in range(a0, a1):
                        for c in range(2):
                            dve.scalar_tensor_tensor(out=self.h[0:n, a, :], in0=got[0:n, a, c, :], scalar=self.weight[c][0:n, a:a + 1],
                                                     in1=self.h[0:n, a, :], op0=ALU.mult, op1=ALU.add).then_inc(mixed, 1)
                            if c == 0:
                                dve.wait_ge(mixed, 2 * a + 1)

            @block.sync
            def _(sp):
                for a, b in parts:
                    n, t0, t1 = tiles(a, b)
                    sp.wait_ge(mixed, 2 * b)
                    sp.dma_start(self.out[t0:t1, :].rearrange("(a p) d -> p a d", p=n), self.h[0:n, a:b, :]).then_inc(stored, 16)
                sp.wait_ge(stored, 16 * len(parts))

    def load_w1(self, sp):
        self.w1_in = self.sem("moe_w1_in")
        for c in range(C - 1):
            sp.dma_start(self.w1[:, c, :], self.t["w1"][:, c, :]).then_inc(self.w1_in, 16)

    def load_route_consts(self, sp):
        m, c_in = self.mem, self.sem("route_consts_in")
        self.route_consts_at = m.cols // 8 * 8 - 512
        m.at(self.route_consts_at)
        self.route_consts = {"tri": m.take(P), "valid": m.take(NT), "steps": m.take(NT), "lower": m.take(E, E),
                             "blocks": m.take(XBLK), "places": m.take(P), "row": m.take(2), "tile": m.take(NT)}
        for name, view in self.route_consts.items():
            sp.dma_start(view, self.t["r_" + name]).then_inc(c_in, 16)
        sp.wait_ge(c_in, 16 * len(self.route_consts))

    def load_w2(self, sp):
        self.w2_in = self.sem("moe_w2_in")
        sp.dma_start(self.w1[:, C - 1, :], self.t["w1"][:, C - 1, :]).then_inc(self.w1_in, 16)
        half = E * KF // 2
        for j in range(2):
            sp.dma_start(self.w2[:, j * half:(j + 1) * half, :], self.t["w2"][:, j * half:(j + 1) * half, :]).then_inc(self.w2_in, 16)

    def run(self):
        self.embed()
        self.retire("patch_")
        self.norm(0, self.h, 1e-5, load=self.load_weights)
        self.rotate()
        self.retire("rot_")
        self.attention()
        self.retire("x_staged", "qk_staged", "v_", "scores_", "exp_done", "probs_", "pv_mm", "o_", "attn_")
        self.project(0, self.wo0, self.wo0_b, self.h, cut=((self.e1, self.e1_hi), (self.e2, self.e2_hi)))
        self.norm(1, self.h, 1e-5, gate=self.gate_w, logits=self.lg)
        self.route_first()
        self.experts()
        self.retire("ex_", "gate_", "up_mm", "gelu_done", "hidden_", "down_", "e2_b", "route_exp", "route_step")
        self.norm(2, self.h, 1e-5, keep=self.xn, split=((self.wqk1, self.wqk1_hi, self.wqk1_lo), (self.wv1, self.wv1_hi, self.wv1_lo)))
        self.linear_attention()
        self.project(1, self.wo1, self.bo1, self.xn, load=self.load_w1,
                     cut=((self.f1, self.f1_hi), (self.f2, self.f2_hi)))
        self.norm(3, self.xn, 1e-12, gain=(self.g1, self.be1), keep=self.xn,
                  rest=((self.f1, self.f1_hi, self.f1_lo), (self.f2, self.f2_hi, self.f2_lo)))
        self.feed_forward()
        self.norm(4, self.xn, 1e-12, gain=(self.g2, self.be2), turn=False, add_to=self.h, load=self.load_w2)
        self.norm(5, self.h, 1e-5, keep=self.xn, turn=False, gate=self.router, logits=self.lg, load=self.load_route_consts)
        self.route_second()
        self.routed()
        self.combine()


def build(nc, dram, out):
    with ExitStack() as ctx:
        Kernel(nc, dram, out, ctx).run()


def layout(inp):
    f = {k: np.asarray(v) for k, v in inp.items()}
    a = {}

    def rows(v):
        return np.ascontiguousarray(np.broadcast_to(v.reshape(1, -1), (P, v.size)))

    def chunks(v):
        return np.ascontiguousarray(v.reshape(-1, P, v.shape[-1]).transpose(1, 0, 2))

    x = f["x"].reshape(NB, 3, 6, 16, 6, 16).transpose(1, 3, 5, 0, 2, 4).reshape(KP, P, NPT, P)
    a["patches"] = np.ascontiguousarray(x.transpose(2, 1, 0, 3))
    a["txt"] = f["txt"]
    a["wpatch"] = chunks(f["L0_tok_W"].T)
    pos = f["L0_tok_pos_embedding"][0]
    a["pos"] = np.ascontiguousarray(np.tile(pos[1:], (NB, 1)).reshape(NPT, P, D).transpose(1, 0, 2))
    a["tok_b"] = rows(f["L0_tok_b"])
    cls = np.stack([f["L0_tok_cls_token"][0, 0], pos[0]])
    a["cls"] = np.ascontiguousarray(np.broadcast_to(cls[None], (NB, 2, D)))
    turn = np.concatenate([np.arange(0, D, 2), np.arange(1, D, 2)])
    a["wqk0"] = np.ascontiguousarray(np.stack([chunks(f["L0_attn_wq"][turn].T), chunks(f["L0_attn_wk"][turn].T)], 1))
    a["wv0"] = chunks(f["L0_attn_wv"].T)
    a["wo0"] = chunks(f["L0_attn_wo_w"].T)
    a["wo0_b"] = rows(f["L0_attn_wo_b"])
    freq = np.exp(np.arange(0, D, 2, dtype=np.float32) * np.float32(-np.log(10000.0) / D))
    angle = (freq[:, None] * np.arange(S, dtype=np.float32)[None]).astype(np.float32)
    cos, sin = np.cos(angle).astype(np.float32), np.sin(angle).astype(np.float32)
    a["cos_sin"], a["sin_cos"] = np.stack([cos, sin], 1), np.stack([sin, cos], 1)
    a["own_mask"] = (np.arange(P)[:, None] // HD == np.arange(2 * HALF)[None]).astype(np.float32).reshape(P, 2, HALF)
    e1 = np.concatenate([f["L0_ffn_W1"], f["L0_ffn_Ws1"][None]])
    a["e1"] = np.ascontiguousarray(e1.reshape(E + 1, C, P, P).transpose(2, 0, 1, 3))
    a["e1_b"] = np.ascontiguousarray(np.concatenate([f["L0_ffn_b1"], f["L0_ffn_bs1"][None]]).T)
    e2 = np.concatenate([f["L0_ffn_W2"], f["L0_ffn_Ws2"][None]])
    a["e2"] = np.ascontiguousarray(e2.transpose(1, 0, 2))
    a["e2_b"] = np.ascontiguousarray(np.concatenate([f["L0_ffn_b2"], f["L0_ffn_bs2"][None]]))
    a["gate_w"] = chunks(f["L0_ffn_gate_W"])
    a["route_scale"] = rows(f["L0_ffn_route_scale"].reshape(1))
    a["wqk1"] = chunks(np.concatenate([f["L1_attn_Wq"], f["L1_attn_Wk"]], 1))
    a["wv1"] = chunks(f["L1_attn_Wv"])
    a["bqk1"] = rows(np.concatenate([f["L1_attn_bq"], f["L1_attn_bk"]]))
    a["bv1"] = rows(f["L1_attn_bv"])
    a["wo1"] = chunks(f["L1_attn_Wo"])
    a["f1"] = chunks(f["L1_attn_W1"])
    a["f2"] = chunks(f["L1_attn_W2"])
    a["f1_b"] = np.ascontiguousarray(f["L1_attn_b1"].reshape(KF, P).T)
    for name, key in (("bo1", "bo"), ("f2_b", "b2"), ("g1", "g1"), ("be1", "be1"), ("g2", "g2"), ("be2", "be2")):
        a[name] = rows(f[f"L1_attn_{key}"])
    a["router"] = chunks(f["L1_ffn_router_w"].T)
    a["w1"] = np.ascontiguousarray(f["L1_ffn_w1"].reshape(E * FF, C, P).transpose(2, 1, 0))
    a["w2"] = np.ascontiguousarray(f["L1_ffn_w2"].transpose(0, 2, 1).reshape(E * KF, P, D).transpose(1, 0, 2))
    a["w1_b"] = np.ascontiguousarray(f["L1_ffn_b1"].reshape(E * KF, P).T)
    a["w2_b"] = rows(f["L1_ffn_b2"])
    same = (np.arange(P)[:, None] // HD == np.arange(P)[None] // HD)
    a["head_mask"] = (same / float(HD) ** 0.5).astype(np.float32)
    a["rank"] = rows(np.arange(E, 0, -1).astype(np.float32))
    a["r_tri"] = np.triu(np.ones((P, P), np.float32), 1)
    a["r_valid"] = (np.arange(NT)[None] * P + np.arange(P)[:, None] < N).astype(np.float32)
    a["r_steps"] = rows(np.arange(NT, dtype=np.float32) * P)
    a["r_lower"] = np.ascontiguousarray(np.broadcast_to(np.tril(np.ones((E, E), np.float32), -1), (P, E, E)))
    a["r_blocks"] = rows(np.arange(XBLK, dtype=np.float32))
    a["r_places"] = rows(np.arange(P, dtype=np.float32))
    a["r_row"] = (2 * np.arange(P)[:, None] + np.arange(1, 3)[None]).astype(np.float32)
    a["r_tile"] = rows(np.arange(NT, dtype=np.float32))
    a["ident"] = np.eye(P, dtype=np.float32)
    return {k: np.ascontiguousarray(v) for k, v in a.items()}


def kernel(**inputs):
    import concourse.bacc as bacc
    from concourse.bass_utils import run_bass_kernel_spmd

    arrays = layout(inputs)
    nc = bacc.Bacc("TRN2", target_bir_lowering=False, num_devices=1)
    dram = {}
    for key, a in arrays.items():
        dram[key] = nc.dram_tensor(f"in_{key}_dram", a.shape, mybir.dt.from_np(a.dtype), kind="ExternalInput").ap()
    out = nc.dram_tensor("out_0_dram", [N, D], F32, kind="ExternalOutput").ap()
    build(nc, dram, out)
    feed = {f"in_{key}_dram": a for key, a in arrays.items()}
    result = run_bass_kernel_spmd(nc, [feed], core_ids=[0]).results[0]
    return result["out_0_dram"].reshape(NB, S, D)
```
